# Optimizing a Trainium2 kernel written in Bass

```python
import numpy as np
import jax
import jax.numpy as jnp

def _softmax(x, axis=-1):
    return jax.nn.softmax(x, axis=axis)

def _gelu(x):
    return jax.nn.gelu(x, approximate=True)

def _silu(x):
    return jax.nn.silu(x)

def _sigmoid(x):
    return jax.nn.sigmoid(x)

def _layernorm(x, axis=-1, eps=1e-05):
    m = jnp.mean(x, axis=axis, keepdims=True)
    v = jnp.var(x, axis=axis, keepdims=True)
    return (x - m) / jnp.sqrt(v + eps)

def _scatter_add(tgt, idx, src, axis=0):
    return tgt.at[idx].add(src)

def _segment_sum(src, seg, n):
    return jax.ops.segment_sum(src, seg, n)
kernel_name = 'mk_prb_d2_jaxref_r4_d173a2'

def setup_inputs(seed: int=0):
    np.random.seed(seed)
    _w = jnp.asarray

    def _L0_attn_setup():
        import jax, jax.numpy as jnp
        import numpy as np
        import math
        DIM = 256
        N_HEADS = 16
        HEAD_DIM = DIM // N_HEADS
        B, S = (2, 512)
        key = jax.random.key(seed)
        k_x, k_wqkv, k_bqkv, k_wout, k_bout = jax.random.split(key, 5)
        scale_in = 1.0 / math.sqrt(DIM)
        x = jax.random.normal(k_x, (B, S, DIM), dtype=jnp.float32)
        Wqkv = jax.random.uniform(k_wqkv, (N_HEADS, DIM, 3 * HEAD_DIM), dtype=jnp.float32, minval=-scale_in, maxval=scale_in)
        bqkv = jax.random.uniform(k_bqkv, (N_HEADS, 3 * HEAD_DIM), dtype=jnp.float32, minval=-scale_in, maxval=scale_in)
        Wout = jax.random.uniform(k_wout, (DIM, DIM), dtype=jnp.float32, minval=-scale_in, maxval=scale_in)
        bout = jax.random.uniform(k_bout, (DIM,), dtype=jnp.float32, minval=-scale_in, maxval=scale_in)
        return {'x': x, 'Wqkv': Wqkv, 'bqkv': bqkv, 'Wout': Wout, 'bout': bout}
    _L0_attn_in = _L0_attn_setup()

    def _L0_ffn_setup():
        import jax, jax.numpy as jnp
        import numpy as np
        from jax import lax
        D = 256
        H = 352
        E = 8
        K = 2
        ROUTER_SCALE = 1.0

        def _expert(x, w1, b1, w3, b3, w2, b2):
            h = jax.nn.silu((x @ w1 + b1) * (x @ w3 + b3))
            return h @ w2 + b2
        key = jax.random.key(seed)
        ks = jax.random.split(key, 16)
        s = 0.02
        inp = {'x': jax.random.normal(ks[0], (2, 512, D), dtype=jnp.float32), 'gate_w': jax.random.normal(ks[1], (E, D), dtype=jnp.float32) * s, 'gate_b': jax.random.normal(ks[2], (E,), dtype=jnp.float32) * s, 'w1': jax.random.normal(ks[3], (E, D, H), dtype=jnp.float32) * s, 'b1': jax.random.normal(ks[4], (E, H), dtype=jnp.float32) * s, 'w3': jax.random.normal(ks[5], (E, D, H), dtype=jnp.float32) * s, 'b3': jax.random.normal(ks[6], (E, H), dtype=jnp.float32) * s, 'w2': jax.random.normal(ks[7], (E, H, D), dtype=jnp.float32) * s, 'b2': jax.random.normal(ks[8], (E, D), dtype=jnp.float32) * s, 'sw1': jax.random.normal(ks[9], (D, H), dtype=jnp.float32) * s, 'sb1': jax.random.normal(ks[10], (H,), dtype=jnp.float32) * s, 'sw3': jax.random.normal(ks[11], (D, H), dtype=jnp.float32) * s, 'sb3': jax.random.normal(ks[12], (H,), dtype=jnp.float32) * s, 'sw2': jax.random.normal(ks[13], (H, D), dtype=jnp.float32) * s, 'sb2': jax.random.normal(ks[14], (D,), dtype=jnp.float32) * s}
        return inp
    _L0_ffn_in = _L0_ffn_setup()

    def _L1_attn_setup():
        import jax, jax.numpy as jnp
        import numpy as np
        B, S, D = (4, 2048, 256)
        N = 4
        K = D // N
        Z_BIAS_MIN, Z_BIAS_MAX = (-2.0, 2.0)

        def _binop(q_i, q_j):
            a_i, b_i = q_i
            a_j, b_j = q_j
            return (a_i * a_j, a_j * b_i + b_j)
        key = jax.random.key(seed)
        k0, k1, k2, k3 = jax.random.split(key, 4)
        scale = 1.0 / np.sqrt(D)
        x = jax.random.normal(k0, (B, S, D), jnp.float32)
        Wz = jax.random.normal(k1, (N, D, K), jnp.float32) * scale
        z_biases = jnp.asarray(np.linspace(Z_BIAS_MIN, Z_BIAS_MAX, N).astype(np.float32))
        bz = jnp.broadcast_to(z_biases[:, None], (N, K))
        Wh = jax.random.normal(k2, (N, D, K), jnp.float32) * scale
        bh = jnp.zeros((N, K), jnp.float32)
        Wg = jax.random.normal(k3, (D, D), jnp.float32) * scale
        bg = jnp.zeros((D,), jnp.float32)
        return {'x': x, 'Wz': Wz, 'bz': bz, 'Wh': Wh, 'bh': bh, 'Wg': Wg, 'bg': bg}
    _L1_attn_in = _L1_attn_setup()

    def _L1_ffn_setup():
        import jax, jax.numpy as jnp
        import numpy as np
        DIM = 256
        LATENT = 128
        INTER = 128
        SHARED = 1024
        E = 8
        TOPK = 2
        NGROUP = 2
        TOPKG = 1
        NORM_TOPK = True
        SCALE = 1.0
        B, S = (2, 256)

        def relu2(x):
            r = jnp.maximum(x, 0.0)
            return r * r
        key = jax.random.key(seed)
        ks = jax.random.split(key, 8)

        def w(k, shape, std=0.02):
            return jax.random.normal(k, shape, dtype=jnp.float32) * std
        return {'x': jax.random.normal(ks[0], (B, S, DIM), dtype=jnp.float32), 'gate': w(ks[1], (E, DIM)), 'corr_bias': jnp.zeros((E,), jnp.float32), 'w1': w(ks[2], (E, INTER, LATENT)), 'w2': w(ks[3], (E, LATENT, INTER)), 'fc1_w': w(ks[4], (LATENT, DIM)), 'fc2_w': w(ks[5], (DIM, LATENT)), 'up_w': w(ks[6], (SHARED, DIM)), 'down_w': w(ks[7], (DIM, SHARED))}
    _L1_ffn_in = _L1_ffn_setup()
    _d = {'L0_attn_x': _L0_attn_in['x'], 'L0_attn_Wqkv': _L0_attn_in['Wqkv'], 'L0_attn_bqkv': _L0_attn_in['bqkv'], 'L0_attn_Wout': _L0_attn_in['Wout'], 'L0_attn_bout': _L0_attn_in['bout'], 'L0_ffn_gate_w': _L0_ffn_in['gate_w'], 'L0_ffn_gate_b': _L0_ffn_in['gate_b'], 'L0_ffn_w1': _L0_ffn_in['w1'], 'L0_ffn_b1': _L0_ffn_in['b1'], 'L0_ffn_w3': _L0_ffn_in['w3'], 'L0_ffn_b3': _L0_ffn_in['b3'], 'L0_ffn_w2': _L0_ffn_in['w2'], 'L0_ffn_b2': _L0_ffn_in['b2'], 'L0_ffn_sw1': _L0_ffn_in['sw1'], 'L0_ffn_sb1': _L0_ffn_in['sb1'], 'L0_ffn_sw3': _L0_ffn_in['sw3'], 'L0_ffn_sb3': _L0_ffn_in['sb3'], 'L0_ffn_sw2': _L0_ffn_in['sw2'], 'L0_ffn_sb2': _L0_ffn_in['sb2'], 'L1_attn_Wz': _L1_attn_in['Wz'], 'L1_attn_bz': _L1_attn_in['bz'], 'L1_attn_Wh': _L1_attn_in['Wh'], 'L1_attn_bh': _L1_attn_in['bh'], 'L1_attn_Wg': _L1_attn_in['Wg'], 'L1_attn_bg': _L1_attn_in['bg'], 'L1_ffn_gate': _L1_ffn_in['gate'], 'L1_ffn_corr_bias': _L1_ffn_in['corr_bias'], 'L1_ffn_w1': _L1_ffn_in['w1'], 'L1_ffn_w2': _L1_ffn_in['w2'], 'L1_ffn_fc1_w': _L1_ffn_in['fc1_w'], 'L1_ffn_fc2_w': _L1_ffn_in['fc2_w'], 'L1_ffn_up_w': _L1_ffn_in['up_w'], 'L1_ffn_down_w': _L1_ffn_in['down_w']}
    _x0 = _d['L0_attn_x']
    _d['L0_attn_x'] = jax.random.normal(jax.random.fold_in(jax.random.key(seed), 1), (8, 512, 256), dtype=_x0.dtype)
    del _x0
    return _d

def reference(L0_attn_x, L0_attn_Wqkv, L0_attn_bqkv, L0_attn_Wout, L0_attn_bout, L0_ffn_gate_w, L0_ffn_gate_b, L0_ffn_w1, L0_ffn_b1, L0_ffn_w3, L0_ffn_b3, L0_ffn_w2, L0_ffn_b2, L0_ffn_sw1, L0_ffn_sb1, L0_ffn_sw3, L0_ffn_sb3, L0_ffn_sw2, L0_ffn_sb2, L1_attn_Wz, L1_attn_bz, L1_attn_Wh, L1_attn_bh, L1_attn_Wg, L1_attn_bg, L1_ffn_gate, L1_ffn_corr_bias, L1_ffn_w1, L1_ffn_w2, L1_ffn_fc1_w, L1_ffn_fc2_w, L1_ffn_up_w, L1_ffn_down_w):

    def _L0_attn_ref(x, Wqkv, bqkv, Wout, bout):
        import jax, jax.numpy as jnp
        import numpy as np
        import math
        DIM = 256
        N_HEADS = 16
        HEAD_DIM = DIM // N_HEADS
        B, S = (2, 512)
        b, s, d = x.shape
        qkv = jnp.einsum('bsd,hde->bhse', x, Wqkv) + bqkv[None, :, None, :]
        q, k, v = jnp.split(qkv, 3, axis=-1)
        score = jnp.einsum('bhsd,bhtd->bhst', q, k)
        causal = jnp.tril(jnp.ones((s, s), dtype=bool))
        score = jnp.where(causal[None, None], score, -jnp.inf)
        attn = jax.nn.softmax(score / jnp.sqrt(jnp.asarray(HEAD_DIM, x.dtype)), axis=-1)
        y = jnp.einsum('bhst,bhtd->bhsd', attn, v)
        y = jnp.transpose(y, (0, 2, 1, 3)).reshape(b, s, d)
        out = y @ Wout + bout
        return out

    def _L0_ffn_ref(x, gate_w, gate_b, w1, b1, w3, b3, w2, b2, sw1, sb1, sw3, sb3, sw2, sb2):
        import jax, jax.numpy as jnp
        import numpy as np
        from jax import lax
        D = 256
        H = 352
        E = 8
        K = 2
        ROUTER_SCALE = 1.0

        def _expert(x, w1, b1, w3, b3, w2, b2):
            h = jax.nn.silu((x @ w1 + b1) * (x @ w3 + b3))
            return h @ w2 + b2
        shape = x.shape
        xf = x.reshape(-1, D)
        T = xf.shape[0]
        scores = jax.nn.softmax(xf @ gate_w.T, axis=-1)
        biased = scores + gate_b
        _, idx = lax.top_k(biased, K)
        w = jnp.take_along_axis(scores, idx, axis=-1) * ROUTER_SCALE
        rw = jnp.zeros((T, E), dtype=xf.dtype).at[jnp.arange(T)[:, None], idx].add(w)
        h = jax.nn.silu((jnp.einsum('td,edh->teh', xf, w1) + b1) * (jnp.einsum('td,edh->teh', xf, w3) + b3))
        oe = jnp.einsum('teh,ehd->ted', h, w2) + b2
        y = jnp.einsum('te,ted->td', rw, oe)
        z = _expert(xf, sw1, sb1, sw3, sb3, sw2, sb2)
        return (y + z).reshape(shape)

    def _L1_attn_ref(x, Wz, bz, Wh, bh, Wg, bg):
        import jax, jax.numpy as jnp
        import numpy as np
        B, S, D = (4, 2048, 256)
        N = 4
        K = D // N
        Z_BIAS_MIN, Z_BIAS_MAX = (-2.0, 2.0)

        def _binop(q_i, q_j):
            a_i, b_i = q_i
            a_j, b_j = q_j
            return (a_i * a_j, a_j * b_i + b_j)
        b_, s_, d_ = x.shape
        z = jax.nn.sigmoid(jnp.einsum('bsd,ndk->bsnk', x, Wz) + bz)
        h_tilde = jnp.einsum('bsd,ndk->bsnk', x, Wh) + bh
        a = (1.0 - z).reshape(b_, s_, d_)
        bb = (z * h_tilde).reshape(b_, s_, d_)
        _, h = jax.lax.associative_scan(_binop, (a, bb), axis=1)
        gate = jax.nn.sigmoid(jnp.einsum('bsd,de->bse', h, Wg) + bg)
        return gate * h

    def _L1_ffn_ref(x, gate, corr_bias, w1, w2, fc1_w, fc2_w, up_w, down_w):
        import jax, jax.numpy as jnp
        import numpy as np
        DIM = 256
        LATENT = 128
        INTER = 128
        SHARED = 1024
        E = 8
        TOPK = 2
        NGROUP = 2
        TOPKG = 1
        NORM_TOPK = True
        SCALE = 1.0
        B, S = (2, 256)

        def relu2(x):
            r = jnp.maximum(x, 0.0)
            return r * r
        Bv, Sv, D = x.shape
        xf = x.reshape(-1, D)
        N = xf.shape[0]
        scores = jax.nn.sigmoid(xf.astype(jnp.float32) @ gate.T)
        sfc = scores + corr_bias
        gs = E // NGROUP
        if NGROUP > 1:
            group_scores = jax.lax.top_k(sfc.reshape(N, NGROUP, gs), 2)[0].sum(-1)
            gidx = jax.lax.top_k(group_scores, TOPKG)[1]
            gmask = jnp.zeros((N, NGROUP), sfc.dtype).at[jnp.arange(N)[:, None], gidx].set(1.0)
            smask = jnp.repeat(gmask, gs, axis=1)
            sfc = jnp.where(smask > 0, sfc, 0.0)
        sel = jax.lax.top_k(sfc, TOPK)[1]
        top_scores = jnp.take_along_axis(scores, sel, axis=1)
        if NORM_TOPK:
            top_scores = top_scores / (top_scores.sum(-1, keepdims=True) + 1e-20)
        flat = sel.reshape(-1)
        perm = jnp.argsort(flat, stable=True)
        sorted_eid = flat[perm]
        scores_sorted = top_scores.reshape(-1)[perm]
        tok = perm // TOPK
        lat = xf @ fc1_w.T
        xs = lat[tok]
        out = jnp.zeros_like(xs)
        for e in range(E):
            he = relu2(xs @ w1[e].T) @ w2[e].T
            out = jnp.where((sorted_eid == e)[:, None], he, out)
        out = out * scores_sorted[:, None]
        comb = jnp.zeros((N, LATENT), out.dtype).at[tok].add(out)
        routed = comb @ fc2_w.T * SCALE
        shared = relu2(xf @ up_w.T) @ down_w.T
        return (routed + shared).reshape(Bv, Sv, D)
    x = L0_attn_x
    xn = _layernorm(x, axis=-1)
    x = x + _L0_attn_ref(xn, L0_attn_Wqkv, L0_attn_bqkv, L0_attn_Wout, L0_attn_bout) + _L0_ffn_ref(xn, L0_ffn_gate_w, L0_ffn_gate_b, L0_ffn_w1, L0_ffn_b1, L0_ffn_w3, L0_ffn_b3, L0_ffn_w2, L0_ffn_b2, L0_ffn_sw1, L0_ffn_sb1, L0_ffn_sw3, L0_ffn_sb3, L0_ffn_sw2, L0_ffn_sb2)
    xn = _layernorm(x, axis=-1)
    x = x + _L1_attn_ref(xn, L1_attn_Wz, L1_attn_bz, L1_attn_Wh, L1_attn_bh, L1_attn_Wg, L1_attn_bg) + _L1_ffn_ref(xn, L1_ffn_gate, L1_ffn_corr_bias, L1_ffn_w1, L1_ffn_w2, L1_ffn_fc1_w, L1_ffn_fc2_w, L1_ffn_up_w, L1_ffn_down_w)
    return x

_drawn_inputs = setup_inputs


def setup_inputs(seed=0):
    import zlib

    import numpy as np

    out = dict(_drawn_inputs(seed))
    spreads = {'L1_attn_bh': (0.0, 0.8), 'L1_attn_bg': (0.0, 2.0), 'L1_ffn_corr_bias': (0.0, 0.8)}
    factors = {'L0_ffn_gate_w': 8.0,
     'L0_ffn_gate_b': 8.0,
     'L0_ffn_w1': 8.0,
     'L0_ffn_b1': 8.0,
     'L0_ffn_w3': 8.0,
     'L0_ffn_b3': 8.0,
     'L0_ffn_w2': 8.0,
     'L0_ffn_b2': 8.0,
     'L0_ffn_sw1': 2.874,
     'L0_ffn_sb1': 8.0,
     'L0_ffn_sw3': 2.859,
     'L0_ffn_sb3': 8.0,
     'L0_ffn_sw2': 2.864,
     'L1_ffn_gate': 8.0,
     'L1_ffn_w1': 8.0,
     'L1_ffn_w2': 8.0,
     'L1_ffn_fc1_w': 8.0,
     'L1_ffn_fc2_w': 8.0,
     'L1_attn_Wz': 8.0,
     'L1_attn_bz': 8.0,
     'L1_attn_Wh': 8.0,
     'L1_attn_Wg': 8.0,
     'L1_ffn_up_w': 8.0,
     'L1_ffn_down_w': 8.0}
    for name, (base, spread) in spreads.items():
        noise = np.random.default_rng([zlib.crc32(name.encode()), seed]).standard_normal(out[name].shape)
        drawn = base * np.exp(spread * noise) if base else spread * noise
        out[name] = jnp.asarray(drawn.astype(out[name].dtype))
    for name, factor in factors.items():
        out[name] = (out[name] * factor).astype(out[name].dtype)
    return out
```

```python
from contextlib import ExitStack

import concourse.bass as bass
from concourse import mybir

F32 = mybir.dt.float32
F16 = mybir.dt.float16
BF16 = mybir.dt.bfloat16
I32 = mybir.dt.int32
U32 = mybir.dt.uint32
ALU = mybir.AluOpType
ACT = mybir.ActivationFunctionType
AX = mybir.AxisListType

P = 128
NB, S, D = 8, 512, 256
T = NB * S
DC = D // P
TT = S // P
NH, HD = 16, 16
E = 8
EPS = 1e-5
H0 = 352
HT = [(0, 128), (128, 128), (256, 96)]
ETOK = 256
NX = E + 1
SHARED_TILES = T // ETOK
MAX_TILES = SHARED_TILES + 2 * T // ETOK + E
SLOTS = (MAX_TILES + 1) * ETOK
ROUTED_SLOTS = SLOTS - SHARED_TILES * ETOK
LAT, INTER, UP = 128, 128, 1024

STK = 96
STKM = STK + 2
POFF = [0, 512, 896, 1152]
PCOLS = 1280
PBUF = 1408
MASKED = -1e30


class Signal:

    def __init__(self, nc, ctx, name, per_step):
        self.sem = ctx.enter_context(nc.semaphore(name))
        self.per = per_step

    def at(self, step, n=None):
        v = step * self.per + (self.per if n is None else max(n, 0))
        return max(v, 0) if isinstance(v, int) else v


def three_products(pe, out, hi_a, lo_a, hi_b, lo_b, chunks, first=True, last=True):
    n = len(chunks)
    for x, c in enumerate(chunks):
        pe.matmul(out, hi_a(c), hi_b(c), start=first and x == 0, stop=False)
        pe.matmul(out, hi_a(c), lo_b(c), start=False, stop=False)
        mm = pe.matmul(out, lo_a(c), hi_b(c), start=False, stop=last and x == n - 1)
    return mm


def mix_phase(nc, x, w, dram, consts, route):
    with ExitStack() as ctx:
        def sb(name, shape, dt=F32):
            return ctx.enter_context(nc.sbuf_tensor(name, shape, dt))

        def ps(name, shape, dt=F32):
            return ctx.enter_context(nc.psum_tensor(name, shape, dt))

        def sig(name, per):
            return Signal(nc, ctx, name, per)

        identf, identb, ones_b, tri, maskadd, iota8 = (consts[k] for k in ("identf", "identb", "ones_b", "tri", "maskadd", "iota8"))
        wqkv32 = sb("wqkv32", [P, DC, 3 * D])
        wout32 = sb("wout32", [P, DC, D])
        gate32 = sb("gate32", [P, DC, E])
        wqkv_hi, wqkv_lo = (sb(f"wqkv_{k}", [P, DC, 3 * D], F16) for k in ("hi", "lo"))
        wout_hi, wout_lo = (sb(f"wout_{k}", [P, DC, D], F16) for k in ("hi", "lo"))
        gate_hi, gate_lo = (sb(f"gate_{k}", [P, DC, E], F16) for k in ("hi", "lo"))
        bqk = sb("bqk", [P, 4])
        bv_row = sb("bv_row", [P, D])
        bout_row = sb("bout_row", [P, D])
        gateb_row = sb("gateb_row", [P, E])
        zeros16, ones16 = (sb(f"{k}16", [P, S], F16) for k in ("zeros", "ones"))
        zeros_f = sb("zeros_f", [P, D])
        xr = sb("xr", [P, TT, D])
        stats = sb("stats", [P, TT, 6])
        mv = sb("mv", [P, TT, 2])
        var_eps = sb("var_eps", [P, TT])
        rstd = sb("rstd", [P, TT])
        minus_half = sb("minus_half", [P, TT])
        xb = sb("xb", [P, 2, TT, D])
        xn = sb("xn", [P, TT, D])
        xT_hi, xT_lo = (sb(f"xT_{k}", [P, DC, S], F16) for k in ("hi", "lo"))
        qk_hi, qk_lo = (sb(f"qk_{k}", [P, 4, S], F16) for k in ("hi", "lo"))
        q_stack = sb("q_stack", [P, 2, NH, S], F16)
        k_stack = sb("k_stack", [P, 2, NH, S], F16)
        v32 = sb("v32", [P, TT, D])
        v_hi, v_lo = (sb(f"v_{k}", [P, 2, TT, NH, HD + 1], F16) for k in ("hi", "lo"))
        neg_max = sb("neg_max", [P, TT, NH])
        max_hi, max_lo = (sb(f"max_{k}", [NH, S], F16) for k in ("hi", "lo"))
        p32 = sb("p32", [P, 3, PBUF])
        p_hi, p_lo = (sb(f"p_{k}", [P, 2, PCOLS], F16) for k in ("hi", "lo"))
        row_sum = sb("row_sum", [P, TT, NH])
        o_rows = sb("o_rows", [P, TT, D])
        oT_hi, oT_lo = (sb(f"oT_{k}", [P, DC, S], F16) for k in ("hi", "lo"))
        x1 = sb("x1", [P, TT, D])
        lg = sb("lg", [P, TT, E])
        lmax = sb("lmax", [P, TT])
        ex = sb("ex", [P, TT, E])
        exs = sb("exs", [P, TT])
        scores = sb("scores", [P, TT, E])
        biased = sb("biased", [P, TT, E])
        top = sb("top", [P, TT, 8])
        topi = sb("topi", [P, TT, 8], U32)
        onehot = sb("onehot", [P, TT, 2, E])
        picked = sb("picked", [P, TT, 2, E])
        member = sb("member", [P, TT, E], BF16)
        ranks = sb("ranks", [P, TT, E])
        tot = sb("tot", [P, TT, E])
        run = route["run"]

        bank = [ps(f"bank{i}", [P, 512]) for i in range(8)]

        w_loaded = sig("w_loaded", 16 * 7)
        w_hi = sig("w_hi", 3)
        w_lo = sig("w_lo", 3)
        filled = sig("filled", 4)
        stacks_filled = sig("stacks_filled", 16 * 6)
        tail_filled = sig("tail_filled", 16)
        v_ones = sig("v_ones", 2)
        run_cleared = sig("run_cleared", 1)
        x_loaded = sig("x_loaded", 16)
        dve_ln = sig("dve_ln", 2)
        rstd_s = sig("rstd_s", 2)
        xn_ready = sig("xn_ready", 1)
        xb_ready = sig("xb_ready", 1)
        xn_stored = sig("xn_stored", 16)
        xT_psum = sig("xT_psum", DC)
        xT_hi_s = sig("xT_hi_s", DC)
        xT_lo_s = sig("xT_lo_s", DC)
        qk_psum = sig("qk_psum", 4)
        qk_hi_s = sig("qk_hi_s", 4)
        qk_lo_s = sig("qk_lo_s", 4)
        qk_stored = sig("qk_stored", 32)
        stacks_loaded = sig("stacks_loaded", 96)
        v_psum = sig("v_psum", 2)
        v32_s = sig("v32_s", 2)
        v_hi_s = sig("v_hi_s", 1)
        v_lo_s = sig("v_lo_s", 1)
        lg_psum = sig("lg_psum", 1)
        lg_shifted = sig("lg_shifted", 2)
        ex_s = sig("ex_s", 1)
        rt = sig("rt", 20)
        rank_psum = sig("rank_psum", 1)
        s_psum = sig("s_psum", TT * NH)
        s_max = sig("s_max", TT * NH)
        mT_psum = sig("mT_psum", 1)
        mT_hi_s = sig("mT_hi_s", 1)
        mT_lo_s = sig("mT_lo_s", 1)
        m_rows = sig("m_rows", 32)
        st_psum = sig("st_psum", 3 * NH)
        p_exp = sig("p_exp", 3 * NH)
        p_masked = sig("p_masked", 2 * NH)
        p_hi_s = sig("p_hi_s", NH)
        p_lo_s = sig("p_lo_s", NH)
        pv_done = sig("pv_done", NH)
        o_sum = sig("o_sum", TT)
        o_ready = sig("o_ready", TT)
        oT_psum = sig("oT_psum", DC)
        oT_hi_s = sig("oT_hi_s", DC)
        oT_lo_s = sig("oT_lo_s", DC)
        proj_psum = sig("proj_psum", 2)
        x1_ready = sig("x1_ready", 2)
        x1_stored = sig("x1_stored", 16)

        def rows(t, b):
            return t[bass.ds(b * S, S), :].rearrange("(t p) d -> p t d", p=P)

        def pipeline(eng, prologue, step):
            prologue(0, 0)
            step(0, 0, True)
            with eng.Fori(0, NB // 2 - 1) as i:
                for u in (1, 0):
                    step(2 * i + 2 - u, u, True)
            step(NB - 1, 1, False)

        block = ctx.enter_context(nc.Block())

        @block.sync
        def _(sp):
            sp.dma_start(wqkv32[:, :, :], w["wqkv"].rearrange("(c p) n -> p c n", p=P)).then_inc(w_loaded.sem, 16)
            sp.dma_start(gate32[:, :, :], w["gate0"].rearrange("(c p) n -> p c n", p=P)).then_inc(w_loaded.sem, 16)
            sp.dma_start(wout32[:, :, :], w["wout"].rearrange("(c p) n -> p c n", p=P)).then_inc(w_loaded.sem, 16)
            sp.dma_start(bqk[:, :], w["bqk"]).then_inc(w_loaded.sem, 16)
            sp.dma_start(bv_row[:, :], w["bv"].partition_broadcast(P)).then_inc(w_loaded.sem, 16)
            sp.dma_start(bout_row[:, :], w["bout"].partition_broadcast(P)).then_inc(w_loaded.sem, 16)
            sp.dma_start(gateb_row[:, :], w["gate_b"].partition_broadcast(P)).then_inc(w_loaded.sem, 16)

            def load_x(b):
                sp.wait_ge(xn_ready.sem, xn_ready.at(b - 1))
                sp.wait_ge(xb_ready.sem, xb_ready.at(b - 1))
                sp.dma_start(xr[:, :, :], rows(x, b)).then_inc(x_loaded.sem, 16)

                sp.wait_ge(xn_ready.sem, xn_ready.at(b))
                sp.dma_start(rows(dram["xn"], b), xn[:, :, :]).then_inc(xn_stored.sem, 16)

            def load_stacks(b, u):
                sp.wait_ge(stacks_loaded.sem, stacks_loaded.at(b - 1))
                sp.wait_ge(qk_hi_s.sem, qk_hi_s.at(b))
                sp.dma_start(dram["qk_hi"].rearrange("(m p) s -> p m s", p=P), qk_hi[:, :, :]).then_inc(qk_stored.sem, 16)
                sp.wait_ge(qk_lo_s.sem, qk_lo_s.at(b))
                sp.dma_start(dram["qk_lo"].rearrange("(m p) s -> p m s", p=P), qk_lo[:, :, :]).then_inc(qk_stored.sem, 16)
                sp.wait_ge(qk_stored.sem, qk_stored.at(b))
                sp.wait_ge(pv_done.sem, pv_done.at(b - 2))
                hi = dram["qk_hi"].rearrange("(m h d) s -> m d h s", m=2, d=HD)
                lo = dram["qk_lo"].rearrange("(m h d) s -> m d h s", m=2, d=HD)
                for r, (q, k) in enumerate(((hi, hi), (hi, lo), (lo, hi))):
                    sp.dma_start(q_stack[HD * r:HD * r + HD, u, :, :], q[0]).then_inc(stacks_loaded.sem, 16)
                    sp.dma_start(k_stack[HD * r:HD * r + HD, u, :, :], k[1]).then_inc(stacks_loaded.sem, 16)

            def max_rows(b, u):
                sp.wait_ge(mT_hi_s.sem, mT_hi_s.at(b))
                sp.wait_ge(mT_lo_s.sem, mT_lo_s.at(b))
                sp.dma_start(q_stack[STK:STK + 1, u, :, :], max_hi[:, :]).then_inc(m_rows.sem, 16)
                sp.dma_start(q_stack[STK + 1:STK + 2, u, :, :], max_lo[:, :]).then_inc(m_rows.sem, 16)

            def project(b, u):
                load_x(b)
                load_stacks(b, u)

            def step(b, u, more):
                if more:
                    load_x(b + 1)
                max_rows(b, u)
                if more:
                    load_stacks(b + 1, 1 - u)
                sp.wait_ge(x1_ready.sem, x1_ready.at(b))
                sp.dma_start(rows(dram["x1"], b), x1[:, :, :]).then_inc(x1_stored.sem, 16)

            sp.wait_ge(filled.sem, 4)
            for u in range(2):
                for stack in (q_stack, k_stack):
                    sp.dma_start(stack[3 * HD:STK, u, :, :], zeros16[3 * HD:STK, :].unsqueeze(1).to_broadcast([STK - 3 * HD, NH, S])).then_inc(stacks_filled.sem, 16)
                sp.dma_start(k_stack[STK:STKM, u, :, :], ones16[STK:STKM, :].unsqueeze(1).to_broadcast([2, NH, S])).then_inc(stacks_filled.sem, 16)
            tail = dram["y"][(MAX_TILES - E) * ETOK:MAX_TILES * ETOK, :].rearrange("(p c) d -> p c d", p=P)
            sp.dma_start(tail, zeros_f[:, :].unsqueeze(1).to_broadcast([P, E * ETOK // P, D])).then_inc(tail_filled.sem, 16)
            pipeline(sp, project, step)
            sp.wait_ge(tail_filled.sem, tail_filled.at(0))
            sp.wait_ge(x1_stored.sem, x1_stored.at(NB - 1))
            sp.wait_ge(xn_stored.sem, xn_stored.at(NB - 1))

        @block.gpsimd
        def _(pool):
            pool.memset(minus_half[:, :], -0.5).then_inc(filled.sem, 1)
            pool.memset(zeros16[:, :], 0.0).then_inc(filled.sem, 1)
            pool.memset(ones16[:, :], 1.0).then_inc(filled.sem, 1)
            pool.memset(zeros_f[:, :], 0.0).then_inc(filled.sem, 1)
            pool.wait_ge(filled.sem, 4)
            pool.wait_ge(w_loaded.sem, w_loaded.at(0))

            def project(b, u):
                pool.wait_ge(dve_ln.sem, dve_ln.at(b))
                pool.tensor_tensor(var_eps[:, :], mv[:, :, 1], consts["eps_col"][:, 0:TT], ALU.add).then_inc(rstd_s.sem, 1)
                pool.wait_ge(rstd_s.sem, rstd_s.at(b, 1))
                pool.tensor_tensor(rstd[:, :], var_eps[:, :], minus_half[:, :], ALU.pow).then_inc(rstd_s.sem, 1)
                pool.wait_ge(x1_ready.sem, x1_ready.at(b - 2))
                pool.tensor_tensor(xb[:, u, :, :], xr[:, :, :], bout_row[:, :].unsqueeze(1).to_broadcast([P, TT, D]),
                                   ALU.add).then_inc(xb_ready.sem, 1)

            def masks(b):
                for h in range(NH):
                    pool.wait_ge(p_exp.sem, p_exp.at(b, 3 * h + 3))
                    pool.nop(nofuse=True)
                    for lo_col, gap in ((0, 512), (896, 256)):
                        v = p32[:, h % 3, lo_col:lo_col + 2 * gap if lo_col == 0 else PBUF].rearrange(
                            "p (a c) -> p a c", c=gap)[:, :, 0:P]
                        pool.affine_select(out=v, in_=v, pattern=[[0, 2], [1, P]], compare_op=ALU.is_ge, fill=0.0,
                                           base=0, channel_multiplier=-1).then_inc(p_masked.sem, 1)

            def step(b, u, more):
                if more:
                    project(b + 1, 1 - u)
                masks(b)

            pipeline(pool, project, step)

        @block.scalar
        def _(act):
            act.wait_ge(w_loaded.sem, w_loaded.at(0))
            act.activation(wqkv_hi[:, :, :], wqkv32[:, :, :], ACT.Copy).then_inc(w_hi.sem, 1)
            act.activation(gate_hi[:, :, :], gate32[:, :, :], ACT.Copy).then_inc(w_hi.sem, 1)
            act.activation(wout_hi[:, :, :], wout32[:, :, :], ACT.Copy).then_inc(w_hi.sem, 1)

            def project(b, u):
                for c in range(DC):
                    act.wait_ge(xT_psum.sem, xT_psum.at(b, c + 1))
                    act.wait_ge(v_psum.sem, v_psum.at(b - 1))
                    act.activation(xT_hi[:, c, :], bank[3 + c][:, :], ACT.Copy).then_inc(xT_hi_s.sem, 1)
                for m in range(4):
                    act.wait_ge(qk_psum.sem, qk_psum.at(b, m + 1))
                    act.wait_ge(qk_stored.sem, qk_stored.at(b - 1))
                    act.activation(qk_hi[:, m, :], bank[(5, 6, 3, 4)[m]][:, :], ACT.Identity,
                                   bias=bqk[:, m:m + 1]).then_inc(qk_hi_s.sem, 1)
                act.wait_ge(v32_s.sem, v32_s.at(b))
                act.wait_ge(pv_done.sem, pv_done.at(b - 2))
                act.activation(v_hi[:, u, :, :, 0:HD], v32[:, :, :].rearrange("p t (h d) -> p t h d", h=NH),
                               ACT.Copy).then_inc(v_hi_s.sem, 1)
                act.wait_ge(lg_shifted.sem, lg_shifted.at(b))
                act.activation(ex[:, :, :], lg[:, :, :], ACT.Exp).then_inc(ex_s.sem, 1)

            def step(b, u, more):
                act.wait_ge(mT_psum.sem, mT_psum.at(b))
                act.wait_ge(m_rows.sem, m_rows.at(b - 1))
                act.activation(max_hi[:, :], bank[0][0:NH, :], ACT.Copy).then_inc(mT_hi_s.sem, 1)
                if more:
                    project(b + 1, 1 - u)
                for h in range(NH + 1):
                    if h < NH:
                        for n, (lo_col, cols) in enumerate(((0, 512), (512, 384), (896, 384))):
                            act.wait_ge(st_psum.sem, st_psum.at(b, 3 * h + n + 1))
                            if n == 0:
                                act.wait_ge(p_lo_s.sem, p_lo_s.at(b, h - 2))
                                act.wait_ge(p_hi_s.sem, p_hi_s.at(b, h - 2))
                            act.activation(p32[:, h % 3, lo_col:lo_col + cols], bank[(3 * h + n) % 3][:, 0:cols],
                                           ACT.Exp, scale=HD ** -0.5).then_inc(p_exp.sem, 1)
                    if h >= 1:
                        act.wait_ge(p_masked.sem, p_masked.at(b, 2 * h))
                        act.wait_ge(pv_done.sem, pv_done.at(b, h - 2))
                        act.activation(p_hi[:, (h - 1) % 2, :], p32[:, (h - 1) % 3, 0:PCOLS], ACT.Copy).then_inc(p_hi_s.sem, 1)
                for c in range(DC):
                    act.wait_ge(oT_psum.sem, oT_psum.at(b, c + 1))
                    act.wait_ge(proj_psum.sem, proj_psum.at(b - 1))
                    act.activation(oT_hi[:, c, :], bank[3 + c][:, :], ACT.Copy).then_inc(oT_hi_s.sem, 1)

            pipeline(act, project, step)

        @block.vector
        def _(dve):
            for k in range(2):
                dve.memset((v_hi, v_lo)[k][:, :, :, :, HD:HD + 1], 1.0 - k).then_inc(v_ones.sem, 1)
            dve.memset(run[:, 0, :], 0.0).then_inc(run_cleared.sem, 1)
            dve.wait_ge(run_cleared.sem, run_cleared.at(0))
            dve.wait_ge(w_hi.sem, 1)
            dve.tensor_tensor(wqkv_lo[:, :, :], wqkv32[:, :, :], wqkv_hi[:, :, :], ALU.subtract).then_inc(w_lo.sem, 1)
            dve.wait_ge(w_hi.sem, 2)
            dve.tensor_tensor(gate_lo[:, :, :], gate32[:, :, :], gate_hi[:, :, :], ALU.subtract).then_inc(w_lo.sem, 1)
            dve.wait_ge(w_hi.sem, 3)
            dve.tensor_tensor(wout_lo[:, :, :], wout32[:, :, :], wout_hi[:, :, :], ALU.subtract).then_inc(w_lo.sem, 1)

            def norm(b):
                dve.wait_ge(x_loaded.sem, x_loaded.at(b))
                for t in range(TT):
                    st = dve.bn_stats(stats[:, t, :], xr[:, t, :])
                st.then_inc(dve_ln.sem, 1)
                dve.wait_ge(rstd_s.sem, rstd_s.at(b - 1))
                dve.wait_ge(dve_ln.sem, dve_ln.at(b, 1))
                dve.nop(nofuse=True)
                for t in range(TT):
                    st = dve.bn_aggr(mv[:, t, :], stats[:, t, :])
                st.then_inc(dve_ln.sem, 1)
                dve.wait_ge(dve_ln.sem, dve_ln.at(b))
                dve.wait_ge(rstd_s.sem, rstd_s.at(b))
                dve.wait_ge(xT_psum.sem, xT_psum.at(b - 1))
                dve.wait_ge(xn_stored.sem, xn_stored.at(b - 1))
                for t in range(TT):
                    st = dve.tensor_scalar(xn[:, t, :], xr[:, t, :], mv[:, t, 0:1], rstd[:, t:t + 1],
                                           ALU.subtract, ALU.mult)
                st.then_inc(xn_ready.sem, 1)

            def router(b):
                at = [0]

                def done(ins):
                    ins.then_inc(rt.sem, 1)
                    at[0] += 1
                    dve.wait_ge(rt.sem, rt.at(b, at[0]))

                dve.wait_ge(lg_psum.sem, lg_psum.at(b))
                lgp = bank[7][:, 0:TT * E].rearrange("p (t e) -> p t e", e=E)
                dve.tensor_reduce(lmax[:, :], lgp, AX.X, ALU.max).then_inc(lg_shifted.sem, 1)
                dve.wait_ge(lg_shifted.sem, lg_shifted.at(b, 1))
                dve.tensor_tensor(lg[:, :, :], lgp, lmax[:, :].unsqueeze(2).to_broadcast([P, TT, E]),
                                  ALU.subtract).then_inc(lg_shifted.sem, 1)
                dve.wait_ge(ex_s.sem, ex_s.at(b))
                done(dve.tensor_reduce(exs[:, :], ex[:, :, :], AX.X, ALU.add))
                done(dve.reciprocal(exs[:, :], exs[:, :]))
                done(dve.tensor_tensor(scores[:, :, :], ex[:, :, :], exs[:, :].unsqueeze(2).to_broadcast([P, TT, E]), ALU.mult))
                done(dve.tensor_tensor(biased[:, :, :], scores[:, :, :],
                                       gateb_row[:, :].unsqueeze(1).to_broadcast([P, TT, E]), ALU.add))
                dve.nop(nofuse=True)
                for t in range(TT):
                    mx = dve.max(top[:, t, :], biased[:, t, :])
                done(mx)
                dve.nop(nofuse=True)
                for t in range(TT):
                    mx = dve.max_index(topi[:, t, :], top[:, t, :], biased[:, t, :])
                done(mx)
                for k in range(2):
                    oh = dve.tensor_tensor(onehot[:, :, k, :], iota8[:, :].unsqueeze(1).to_broadcast([P, TT, E]),
                                           topi[:, :, k:k + 1].to_broadcast([P, TT, E]), ALU.is_equal)
                done(oh)
                done(dve.tensor_tensor(member[:, :, :], onehot[:, :, 0, :], onehot[:, :, 1, :], ALU.add))
                for k in range(2):
                    oh = dve.tensor_tensor(picked[:, :, k, :], onehot[:, :, k, :], scores[:, :, :], ALU.mult)
                done(oh)
                done(dve.tensor_reduce(route["weights"][:, bass.ds(b * TT, TT), :], picked[:, :, :, :], AX.X, ALU.add))
                dve.wait_ge(rank_psum.sem, rank_psum.at(b))
                done(dve.tensor_copy(tot[:, :, :], bank[7][:, 64:64 + TT * E].rearrange("p (t e) -> p t e", e=E)))
                for t in range(TT):
                    done(dve.tensor_tensor(run[:, t + 1, :], run[:, t, :], tot[:, t, :], ALU.add))
                done(dve.tensor_tensor(ranks[:, :, :], bank[7][:, 32:32 + TT * E].rearrange("p (t e) -> p t e", e=E),
                                       run[:, 0:TT, :], ALU.add))
                for k in range(2):
                    oh = dve.tensor_tensor(picked[:, :, k, :], onehot[:, :, k, :], ranks[:, :, :], ALU.mult)
                done(oh)
                done(dve.tensor_reduce(route["rank"][:, bass.ds(b * TT, TT), :], picked[:, :, :, :], AX.X, ALU.add))
                done(dve.tensor_copy(route["onehot"][:, bass.ds(b * TT, TT), :, :], onehot[:, :, :, :]))
                done(dve.tensor_copy(run[:, 0, :], run[:, TT, :]))
                assert at[0] == rt.per

            def parts(b, u):
                for c in range(DC):
                    dve.wait_ge(xT_hi_s.sem, xT_hi_s.at(b, c + 1))
                    dve.tensor_tensor(xT_lo[:, c, :], bank[3 + c][:, :], xT_hi[:, c, :], ALU.subtract).then_inc(xT_lo_s.sem, 1)
                for m in range(4):
                    dve.wait_ge(qk_hi_s.sem, qk_hi_s.at(b, m + 1))
                    dve.scalar_tensor_tensor(qk_lo[:, m, :], bank[(5, 6, 3, 4)[m]][:, :], bqk[:, m:m + 1], qk_hi[:, m, :],
                                             ALU.add, ALU.subtract).then_inc(qk_lo_s.sem, 1)
                for g in range(2):
                    dve.wait_ge(v_psum.sem, v_psum.at(b, g + 1))
                    dve.tensor_tensor(v32[:, 2 * g:2 * g + 2, :], bank[5 + g][:, :].rearrange("p (t n) -> p t n", t=2),
                                      bv_row[:, :].unsqueeze(1).to_broadcast([P, 2, D]), ALU.add).then_inc(v32_s.sem, 1)
                dve.wait_ge(v_hi_s.sem, v_hi_s.at(b))
                dve.tensor_tensor(v_lo[:, u, :, :, 0:HD], v32[:, :, :].rearrange("p t (h d) -> p t h d", h=NH),
                                  v_hi[:, u, :, :, 0:HD], ALU.subtract).then_inc(v_lo_s.sem, 1)

            def project(b, u):
                norm(b)
                parts(b, u)
                router(b)

            def step(b, u, more):
                if more:
                    norm(b + 1)
                for h in range(NH):
                    for j in range(TT):
                        n = h * TT + j
                        dve.wait_ge(s_psum.sem, s_psum.at(b, n + 1))
                        dve.tensor_reduce(neg_max[:, j, h:h + 1], bank[n % 3][:, 0:(j + 1) * P], AX.X, ALU.max,
                                          negate=True).then_inc(s_max.sem, 1)
                dve.wait_ge(mT_hi_s.sem, mT_hi_s.at(b))
                dve.tensor_tensor(max_lo[:, :], bank[0][0:NH, :], max_hi[:, :], ALU.subtract).then_inc(mT_lo_s.sem, 1)
                if more:
                    parts(b + 1, 1 - u)
                    router(b + 1)
                for h in range(NH):
                    dve.wait_ge(p_hi_s.sem, p_hi_s.at(b, h + 1))
                    dve.tensor_tensor(p_lo[:, h % 2, :], p32[:, h % 3, 0:PCOLS], p_hi[:, h % 2, :],
                                      ALU.subtract).then_inc(p_lo_s.sem, 1)
                dve.wait_ge(pv_done.sem, pv_done.at(b))
                for j in range(TT):
                    o = bank[3 + j][:, 0:NH * (HD + 1)].rearrange("p (h d) -> p h d", h=NH)
                    dve.reciprocal(row_sum[:, j, :], o[:, :, HD]).then_inc(o_sum.sem, 1)
                for j in range(TT):
                    o = bank[3 + j][:, 0:NH * (HD + 1)].rearrange("p (h d) -> p h d", h=NH)
                    dve.wait_ge(o_sum.sem, o_sum.at(b, j + 1))
                    dve.tensor_tensor(o_rows[:, j, :].rearrange("p (h d) -> p h d", h=NH), o[:, :, 0:HD],
                                      row_sum[:, j, :].unsqueeze(2).to_broadcast([P, NH, HD]), ALU.mult).then_inc(o_ready.sem, 1)
                for c in range(DC):
                    dve.wait_ge(oT_hi_s.sem, oT_hi_s.at(b, c + 1))
                    dve.tensor_tensor(oT_lo[:, c, :], bank[3 + c][:, :], oT_hi[:, c, :], ALU.subtract).then_inc(oT_lo_s.sem, 1)
                dve.wait_ge(x1_stored.sem, x1_stored.at(b - 1))
                for g in range(2):
                    dve.wait_ge(proj_psum.sem, proj_psum.at(b, g + 1))
                    dve.tensor_tensor(x1[:, 2 * g:2 * g + 2, :], bank[5 + g][:, :].rearrange("p (t n) -> p t n", t=2),
                                      xb[:, u, 2 * g:2 * g + 2, :], ALU.add).then_inc(x1_ready.sem, 1)

            pipeline(dve, project, step)
            dve.wait_ge(rt.sem, rt.at(NB - 1))

        @block.tensor
        def _(pe):
            def transposes(b):
                pe.wait_ge(xn_ready.sem, xn_ready.at(b))
                pe.wait_ge(oT_lo_s.sem, oT_lo_s.at(b - 2))
                for c in range(DC):
                    for t in range(TT):
                        mm = pe.transpose(bank[3 + c][:, t * P:(t + 1) * P], xn[:, t, c * P:(c + 1) * P], identf[:, :])
                    mm.then_inc(xT_psum.sem, 1)

            def projections(b):
                pe.wait_ge(xT_lo_s.sem, xT_lo_s.at(b))
                pe.wait_ge(x1_ready.sem, x1_ready.at(b - 2))
                for m in range(4):
                    cols = slice(m * P, (m + 1) * P)
                    three_products(pe, bank[(5, 6, 3, 4)[m]][:, :], lambda c: wqkv_hi[:, c, cols], lambda c: wqkv_lo[:, c, cols],
                                   lambda c: xT_hi[:, c, :], lambda c: xT_lo[:, c, :], range(DC)).then_inc(qk_psum.sem, 1)
                pe.wait_ge(rt.sem, rt.at(b - 1))
                for t in range(TT):
                    tok = slice(t * P, (t + 1) * P)
                    mm = three_products(pe, bank[7][:, t * E:(t + 1) * E], lambda c: xT_hi[:, c, tok], lambda c: xT_lo[:, c, tok],
                                        lambda c: gate_hi[:, c, :], lambda c: gate_lo[:, c, :], range(DC))
                mm.then_inc(lg_psum.sem, 1)
                for t in range(TT):
                    tok = slice(t * P, (t + 1) * P)
                    if t % 2 == 0:
                        pe.wait_ge(qk_lo_s.sem, qk_lo_s.at(b, t // 2 + 1))
                    mm = three_products(pe, bank[5 + t // 2][:, (t % 2) * D:(t % 2 + 1) * D],
                                        lambda c: xT_hi[:, c, tok], lambda c: xT_lo[:, c, tok],
                                        lambda c: wqkv_hi[:, c, 2 * D:3 * D], lambda c: wqkv_lo[:, c, 2 * D:3 * D], range(DC))
                    if t % 2 == 1:
                        mm.then_inc(v_psum.sem, 1)

            def rank_sums(b):
                pe.wait_ge(rt.sem, rt.at(b, 8))
                m = member[:, :, :].rearrange("p t e -> p (t e)")
                pe.matmul(bank[7][:, 32:32 + TT * E], tri[:, :], m, start=True, stop=True)
                pe.matmul(bank[7][:, 64:64 + TT * E], ones_b[:, :], m, start=True, stop=True).then_inc(rank_psum.sem, 1)

            def score_tiles(b, u):
                pe.wait_ge(stacks_loaded.sem, stacks_loaded.at(b))
                pe.wait_ge(p_exp.sem, p_exp.at(b - 1))
                for h in range(NH):
                    for j in range(TT):
                        n = h * TT + j
                        if n >= 3:
                            pe.wait_ge(s_max.sem, s_max.at(b, n - 2))
                        pe.matmul(bank[n % 3][:, 0:(j + 1) * P], q_stack[0:STK, u, h, j * P:(j + 1) * P],
                                  k_stack[0:STK, u, h, 0:(j + 1) * P], start=True, stop=False)
                        pe.matmul(bank[n % 3][:, j * P:(j + 1) * P], identb[:, :], maskadd[:, :],
                                  start=False, stop=True).then_inc(s_psum.sem, 1)

            def max_transposes(b):
                pe.wait_ge(s_max.sem, s_max.at(b))
                for j in range(TT):
                    mm = pe.transpose(bank[0][0:NH, j * P:(j + 1) * P], neg_max[:, j, :], identf[:, :])
                mm.then_inc(mT_psum.sem, 1)

            def scores_t(b, u, h):
                if h == 0:
                    pe.wait_ge(m_rows.sem, m_rows.at(b))
                    pe.wait_ge(mT_lo_s.sem, mT_lo_s.at(b))
                for n, blocks in enumerate(((0,), (1,), (2, 3))):
                    if 3 * h + n >= 3:
                        pe.wait_ge(p_exp.sem, p_exp.at(b, 3 * h + n - 2))
                    for k in blocks:
                        at = 256 if k == 3 else 0
                        mm = pe.matmul(bank[(3 * h + n) % 3][:, at:at + S - k * P], k_stack[0:STKM, u, h, k * P:(k + 1) * P],
                                       q_stack[0:STKM, u, h, k * P:S], start=True, stop=True)
                    mm.then_inc(st_psum.sem, 1)

            def values(b, u, h, more):
                if h == 0:
                    if more:
                        pe.wait_ge(qk_lo_s.sem, qk_lo_s.at(b + 1))
                        pe.wait_ge(v32_s.sem, v32_s.at(b + 1))
                    else:
                        pe.wait_ge(x1_ready.sem, x1_ready.at(b - 1))
                    pe.wait_ge(v_lo_s.sem, v_lo_s.at(b))
                pe.wait_ge(p_lo_s.sem, p_lo_s.at(b, h + 1))
                for j in range(TT):
                    out = bank[3 + j][:, h * (HD + 1):(h + 1) * (HD + 1)]
                    for k in range(j + 1):
                        cols = slice(POFF[k] + (j - k) * P, POFF[k] + (j - k + 1) * P)
                        pe.matmul(out, p_hi[:, h % 2, cols], v_hi[:, u, k, h, :], start=k == 0, stop=False)
                        pe.matmul(out, p_hi[:, h % 2, cols], v_lo[:, u, k, h, :], start=False, stop=False)
                        mm = pe.matmul(out, p_lo[:, h % 2, cols], v_hi[:, u, k, h, :], start=False, stop=k == j)
                mm.then_inc(pv_done.sem, 1)

            def outputs(b):
                pe.wait_ge(o_ready.sem, o_ready.at(b))
                for c in range(DC):
                    for t in range(TT):
                        mm = pe.transpose(bank[3 + c][:, t * P:(t + 1) * P], o_rows[:, t, c * P:(c + 1) * P], identf[:, :])
                    mm.then_inc(oT_psum.sem, 1)
                pe.wait_ge(oT_lo_s.sem, oT_lo_s.at(b))
                for t in range(TT):
                    tok = slice(t * P, (t + 1) * P)
                    mm = three_products(pe, bank[5 + t // 2][:, (t % 2) * D:(t % 2 + 1) * D],
                                        lambda c: oT_hi[:, c, tok], lambda c: oT_lo[:, c, tok],
                                        lambda c: wout_hi[:, c, :], lambda c: wout_lo[:, c, :], range(DC))
                    if t % 2 == 1:
                        mm.then_inc(proj_psum.sem, 1)

            def project(b, u):
                transposes(b)
                projections(b)
                rank_sums(b)

            def step(b, u, more):
                score_tiles(b, u)
                if more:
                    transposes(b + 1)
                max_transposes(b)
                if more:
                    projections(b + 1)
                scores_t(b, u, 0)
                if more:
                    rank_sums(b + 1)
                for h in range(NH):
                    if h + 1 < NH:
                        scores_t(b, u, h + 1)
                    values(b, u, h, more)
                outputs(b)

            pe.wait_ge(w_lo.sem, 3)
            pe.wait_ge(stacks_filled.sem, stacks_filled.at(0))
            pe.wait_ge(v_ones.sem, v_ones.at(0))
            pipeline(pe, project, step)



def constants(nc, ctx):
    def sb(name, shape, dt=F32):
        return ctx.enter_context(nc.sbuf_tensor(name, shape, dt))

    c = {"identf": sb("identf", [P, P]), "identb": sb("identb", [P, P], BF16), "ones_b": sb("ones_b", [P, P], BF16),
         "tri": sb("tri", [P, P], BF16), "maskadd": sb("maskadd", [P, P], BF16), "iota8": sb("iota8", [P, E]),
         "eps_col": sb("eps_col", [P, TT]), "zero_i": sb("zero_i", [P, 2], I32)}
    with ExitStack() as own:
        start = own.enter_context(nc.semaphore("const_start"))
        made = own.enter_context(nc.semaphore("const_made"))
        zeros = own.enter_context(nc.sbuf_tensor("zeros", [P, P], F32))
        onesf = own.enter_context(nc.sbuf_tensor("onesf", [P, P], F32))
        block = own.enter_context(nc.Block())

        @block.gpsimd
        def _(pool):
            pool.memset(zeros[:, :], 0.0).then_inc(start, 1)
            pool.memset(onesf[:, :], 1.0).then_inc(start, 1)
            pool.memset(c["ones_b"][:, :], 1.0).then_inc(made, 1)
            pool.memset(c["eps_col"][:, :], EPS).then_inc(made, 1)
            pool.memset(c["zero_i"][:, :], 0).then_inc(made, 1)
            pool.iota(c["iota8"][:, :], [[1, E]], base=0, channel_multiplier=0,
                      allow_small_or_imprecise_dtypes=True).then_inc(made, 1)
            pool.wait_ge(start, 2)
            for name in ("identf", "identb"):
                pool.affine_select(out=c[name][:, :], in_=zeros[:, :], pattern=[[-1, P]], compare_op=ALU.not_equal,
                                   fill=1.0, base=0, channel_multiplier=1).then_inc(made, 1)
            pool.affine_select(out=c["tri"][:, :], in_=onesf[:, :], pattern=[[1, P]], compare_op=ALU.is_gt,
                               fill=0.0, base=0, channel_multiplier=-1).then_inc(made, 1)
            pool.affine_select(out=c["maskadd"][:, :], in_=zeros[:, :], pattern=[[-1, P]], compare_op=ALU.is_ge,
                               fill=MASKED, base=0, channel_multiplier=1).then_inc(made, 1)
            pool.wait_ge(made, 8)
    return c


def slots_phase(nc, route):
    run, bounds, pos, tokens = route["run"], route["bounds"], route["pos"], route["tokens"]
    with ExitStack() as ctx:
        def sb(name, shape, dt=F32):
            return ctx.enter_context(nc.sbuf_tensor(name, shape, dt))

        tiles_i = sb("tiles_i", [P, E], I32)
        tiles = sb("tiles", [P, E])
        ones8 = sb("ones8", [P, E])
        ends = sb("ends", [P, E])
        starts = sb("starts", [P, E])
        base = sb("base", [P, T // P, 2, E])
        posf = sb("posf", [P, T // P, 2])
        zeros_i = sb("zeros_i", [P, ROUTED_SLOTS // P], I32)
        chain = Signal(nc, ctx, "slot_chain", 10)
        made = Signal(nc, ctx, "slot_made", 4)
        zeroed = Signal(nc, ctx, "table_zeroed", 16)
        block = ctx.enter_context(nc.Block())

        @block.gpsimd
        def _(pool):
            pool.iota(tokens[:, 0:T // P], [[P, T // P]], base=0, channel_multiplier=1).then_inc(made.sem, 1)
            pool.iota(route["ids"][:, :], [[P, T // P]], base=0, channel_multiplier=1).then_inc(made.sem, 1)
            pool.memset(zeros_i[:, :], 0).then_inc(made.sem, 1)
            pool.memset(ones8[:, :], 1.0).then_inc(made.sem, 1)
            pool.wait_ge(made.sem, 4)

        @block.sync
        def _(sp):
            sp.wait_ge(made.sem, 4)
            sp.dma_start(route["table"].rearrange("(p c) o -> p (c o)", p=P), zeros_i[:, :]).then_inc(zeroed.sem, 16)
            sp.wait_ge(zeroed.sem, 16)

        @block.vector
        def _(dve):
            at = [0]

            def done(ins):
                ins.then_inc(chain.sem, 1)
                at[0] += 1
                dve.wait_ge(chain.sem, at[0])

            dve.wait_ge(made.sem, 4)
            done(dve.tensor_scalar(tiles_i[:, :], run[:, 0, :], 1.0 / ETOK, (ETOK - 1.0) / ETOK - 0.499, ALU.mult, ALU.add))
            done(dve.tensor_scalar(tiles[:, :], tiles_i[:, :], 1.0, None, ALU.max))
            done(dve.tensor_tensor_scan(ends[:, :], ones8[:, :], tiles[:, :], float(SHARED_TILES), ALU.mult, ALU.add))
            done(dve.tensor_tensor(starts[:, :], ends[:, :], tiles[:, :], ALU.subtract))
            done(dve.tensor_copy(bounds[:, 0:E], starts[:, :]))
            done(dve.tensor_copy(bounds[:, E:E + 1], ends[:, E - 1:E]))
            done(dve.tensor_scalar(starts[:, :], starts[:, :], float(SHARED_TILES), float(ETOK), ALU.subtract, ALU.mult))
            done(dve.tensor_tensor(base[:, :, :, :].rearrange("p t k e -> p (t k) e"),
                                   route["onehot"][:, :, :, :].rearrange("p t k e -> p (t k) e"),
                                   starts[:, :].unsqueeze(1).to_broadcast([P, 2 * T // P, E]), ALU.mult))
            done(dve.tensor_reduce(posf[:, :, :], base[:, :, :, :], AX.X, ALU.add))
            dve.tensor_tensor(pos[:, :, :], posf[:, :, :], route["rank"][:, :, :], ALU.add).then_inc(chain.sem, 1)
            dve.wait_ge(chain.sem, 10)


def experts_phase(nc, w, dram, consts, route):
    identf, bounds, pos, tokens = consts["identf"], route["bounds"], route["pos"], route["tokens"]
    HM = len(HT)
    HALF = ETOK // P
    with ExitStack() as ctx:
        def sb(name, shape, dt=F32):
            return ctx.enter_context(nc.sbuf_tensor(name, shape, dt))

        def sig(name, per):
            return Signal(nc, ctx, name, per)

        w13_32 = sb("w13_32", [P, DC, 2 * H0])
        w2_32 = sb("w2_32", [P, HM, D])
        w13_hi, w13_lo = (sb(f"w13_{k}", [P, 2, DC, 2 * H0], F16) for k in ("hi", "lo"))
        w2_hi, w2_lo = (sb(f"w2_{k}", [P, 2, HM, D], F16) for k in ("hi", "lo"))
        b13 = sb("b13", [P, 2, 2 * HM])
        b2 = sb("b2", [P, 2, D])
        token_now = sb("token_now", [P, HALF], I32)
        xg = sb("xg", [P, HALF, D])
        xT_hi, xT_lo = (sb(f"gT_{k}", [P, DC, ETOK], F16) for k in ("hi", "lo"))
        a1 = sb("a1", [P, HM, ETOK])
        prod = sb("prod", [P, HM, ETOK])
        h32 = sb("h32", [P, HM, ETOK])
        h_hi, h_lo = (sb(f"h_{k}", [P, HM, ETOK], F16) for k in ("hi", "lo"))
        y = sb("y", [P, HALF, D])
        table_rows = sb("table_rows", [ROUTED_SLOTS // P, P], I32)
        table_f = sb("table_f", [ROUTED_SLOTS // P, P])
        bank = [ctx.enter_context(nc.psum_tensor(f"xbank{i}", [P, 512], F32)) for i in range(6)]

        e_loaded = sig("e_loaded", 16 * 5)
        e_hi = sig("e_hi", 3)
        e_lo = sig("e_lo", 3)
        token_now_s = sig("token_now_s", 1)
        gathered = sig("gathered", 16 * HALF)
        gT_psum = sig("gT_psum", 1)
        gT_hi_s = sig("gT_hi_s", 1)
        gT_lo_s = sig("gT_lo_s", 1)
        gu_psum = sig("gu_psum", HM)
        a1_s = sig("a1_s", HM)
        prod_s = sig("prod_s", HM)
        h32_s = sig("h32_s", HM)
        h_hi_s = sig("h_hi_s", HM)
        h_lo_s = sig("h_lo_s", HM)
        y_psum = sig("y_psum", 1)
        y_ready = sig("y_ready", 1)
        y_stored = sig("y_stored", 16)
        scattered = sig("scattered", 16 * 2 * T // P)
        table_loaded = sig("table_loaded", 16)
        table_f_s = sig("table_f_s", 1)
        table_psum = sig("table_psum", 1)
        tokens_s = sig("tokens_s", 1)

        def over_experts(eng, prologue, new_expert, tile, table):
            prologue()
            new_expert(0, 0, 0)
            tile(0, 0)
            with eng.Fori(1, SHARED_TILES - 1) as i:
                tile(i, 0)
            table()
            tile(SHARED_TILES - 1, 0)
            with eng.Fori(0, E // 2) as half:
                for k in range(2):
                    first = eng.value_load(bounds[0:1, bass.ds(2 * half + k, 1)], min_val=SHARED_TILES, max_val=MAX_TILES)
                    end = eng.value_load(bounds[0:1, bass.ds(2 * half + k + 1, 1)], min_val=SHARED_TILES + 1, max_val=MAX_TILES)
                    new_expert(2 * half + k + 1, 1 - k, first)
                    with eng.Fori(first, end) as i:
                        tile(i, 1 - k)

        block = ctx.enter_context(nc.Block())

        @block.sync
        def _(sp):
            def load_expert(e, u, first):
                sp.wait_ge(e_hi.sem, e_hi.at(e, 0))
                sp.wait_ge(e_lo.sem, e_lo.at(e, 0))
                sp.wait_ge(y_ready.sem, y_ready.at(first, 0))
                d = e if isinstance(e, int) else bass.ds(e, 1)
                row = (lambda t: t[e]) if isinstance(e, int) else (lambda t: t[bass.ds(e, 1)].rearrange("a m n -> (a m) n"))
                sp.dma_start(w13_32[:, :, :], row(w["w13"]).rearrange("(c p) n -> p c n", p=P)).then_inc(e_loaded.sem, 16)
                sp.dma_start(w2_32[:, 0:2, :], row(w["w2"])[0:2 * P, :].rearrange("(m p) n -> p m n", p=P)).then_inc(e_loaded.sem, 16)
                sp.dma_start(w2_32[0:HT[2][1], 2, :], row(w["w2"])[2 * P:H0, :]).then_inc(e_loaded.sem, 16)
                sp.dma_start(b13[:, u, :], row(w["b13"])).then_inc(e_loaded.sem, 16)
                sp.dma_start(b2[:, u, :], row(w["b2"])[0].partition_broadcast(P)).then_inc(e_loaded.sem, 16)

            def new_expert(e, u, first):
                load_expert(e + 1, 1 - u, first)

            def tile(i, u):
                sp.wait_ge(y_ready.sem, y_ready.at(i))
                sp.dma_start(dram["y"][bass.ds(i * ETOK, ETOK), :].rearrange("(t p) d -> p t d", p=P),
                             y[:, :, :]).then_inc(y_stored.sem, 16)

            def table():
                sp.wait_ge(scattered.sem, scattered.at(0))
                sp.dma_start(table_rows[:, :], route["table"].rearrange("(c p) o -> c (p o)", p=P)).then_inc(table_loaded.sem, 16)

            over_experts(sp, lambda: load_expert(0, 0, 0), new_expert, tile, table)
            last = sp.value_load(bounds[0:1, E:E + 1], min_val=SHARED_TILES + 1, max_val=MAX_TILES)
            sp.wait_ge(y_stored.sem, y_stored.at(last, 0))
            sp.nop(nofuse=True)

        @block.gpsimd
        def _(pool):
            def gather(i):
                pool.wait_ge(gT_psum.sem, gT_psum.at(i, 0))
                pool.wait_ge(token_now_s.sem, token_now_s.at(i))
                pool.nop(nofuse=True)
                for half in range(HALF):
                    pool.indirect_dma_start(xg[:, half, :], None, dram["xn"],
                                            bass.IndirectOffsetOnAxis(token_now[:, half:half + 1], 0)).then_inc(gathered.sem, 16)

            gather(0)
            columns = [(t, k) for t in range(T // P) for k in range(2)]
            share = -(-len(columns) // (SHARED_TILES - 1))
            for i in range(SHARED_TILES - 1):
                gather(i + 1)
                for t, k in columns[i * share:(i + 1) * share]:
                    pool.indirect_dma_start(route["table"], bass.IndirectOffsetOnAxis(pos[:, t, k:k + 1], 0),
                                            route["ids"][:, t:t + 1], None).then_inc(scattered.sem, 16)
            gather(SHARED_TILES)
            end = pool.value_load(bounds[0:1, E:E + 1], min_val=SHARED_TILES + 1, max_val=MAX_TILES)
            with pool.Fori(SHARED_TILES, end) as i:
                gather(i + 1)

        @block.scalar
        def _(act):
            def split(e, u, first):
                act.wait_ge(e_loaded.sem, e_loaded.at(e))
                act.wait_ge(y_psum.sem, y_psum.at(first, 0))
                act.activation(w13_hi[:, u, :, :], w13_32[:, :, :], ACT.Copy).then_inc(e_hi.sem, 1)
                act.activation(w2_hi[:, u, 0:2, :], w2_32[:, 0:2, :], ACT.Copy).then_inc(e_hi.sem, 1)
                act.activation(w2_hi[0:HT[2][1], u, 2, :], w2_32[0:HT[2][1], 2, :], ACT.Copy).then_inc(e_hi.sem, 1)

            def x_part(i):
                act.wait_ge(gT_psum.sem, gT_psum.at(i))
                act.wait_ge(gu_psum.sem, gu_psum.at(i, 0))
                act.activation(xT_hi[:, :, :], bank[3][:, :].rearrange("p (c t) -> p c t", c=DC), ACT.Copy).then_inc(gT_hi_s.sem, 1)

            def bias1(i, u, m):
                M = HT[m][1]
                act.wait_ge(gu_psum.sem, gu_psum.at(i, m + 1))
                act.activation(a1[0:M, m, :], bank[m][0:M, 0:ETOK], ACT.Identity, bias=b13[0:M, u, m:m + 1]).then_inc(a1_s.sem, 1)

            def hidden(i, m):
                M = HT[m][1]
                act.wait_ge(prod_s.sem, prod_s.at(i, m + 1))
                act.wait_ge(y_psum.sem, y_psum.at(i, 0))
                act.activation(h32[0:M, m, :], prod[0:M, m, :], ACT.Silu).then_inc(h32_s.sem, 1)
                act.wait_ge(h32_s.sem, h32_s.at(i, m + 1))
                act.activation(h_hi[0:M, m, :], h32[0:M, m, :], ACT.Copy).then_inc(h_hi_s.sem, 1)

            def tile(i, u):
                bias1(i, u, 0)
                bias1(i, u, 1)
                hidden(i, 0)
                bias1(i, u, 2)
                hidden(i, 1)
                hidden(i, 2)
                x_part(i + 1)

            def prologue():
                split(0, 0, 0)
                x_part(0)

            over_experts(act, prologue, lambda e, u, first: split(e + 1, 1 - u, first), tile, lambda: None)

        @block.vector
        def _(dve):
            def split(e, u, first):
                dve.wait_ge(y_psum.sem, y_psum.at(first, 0))
                for n, (lo, a32, hi) in enumerate((
                        (w13_lo[:, u, :, :], w13_32[:, :, :], w13_hi[:, u, :, :]),
                        (w2_lo[:, u, 0:2, :], w2_32[:, 0:2, :], w2_hi[:, u, 0:2, :]),
                        (w2_lo[0:HT[2][1], u, 2, :], w2_32[0:HT[2][1], 2, :], w2_hi[0:HT[2][1], u, 2, :]))):
                    dve.wait_ge(e_hi.sem, e_hi.at(e, n + 1))
                    dve.tensor_tensor(lo, a32, hi, ALU.subtract).then_inc(e_lo.sem, 1)

            def name_tokens(i):
                dve.wait_ge(gathered.sem, gathered.at(i, 0))
                dve.nop(nofuse=True)
                dve.tensor_copy(token_now[:, :], tokens[:, bass.ds(i * HALF, HALF)]).then_inc(token_now_s.sem, 1)

            def x_part(i):
                dve.wait_ge(gT_hi_s.sem, gT_hi_s.at(i))
                dve.tensor_tensor(xT_lo[:, :, :], bank[3][:, :].rearrange("p (c t) -> p c t", c=DC), xT_hi[:, :, :],
                                  ALU.subtract).then_inc(gT_lo_s.sem, 1)

            def gated(i, u, m):
                M = HT[m][1]
                dve.wait_ge(a1_s.sem, a1_s.at(i, m + 1))
                dve.wait_ge(h32_s.sem, h32_s.at(i, 0))
                dve.scalar_tensor_tensor(prod[0:M, m, :], bank[m][0:M, ETOK:2 * ETOK], b13[0:M, u, HM + m:HM + m + 1],
                                         a1[0:M, m, :], ALU.add, ALU.mult).then_inc(prod_s.sem, 1)

            def hidden_lo(i, m):
                M = HT[m][1]
                dve.wait_ge(h_hi_s.sem, h_hi_s.at(i, m + 1))
                dve.tensor_tensor(h_lo[0:M, m, :], h32[0:M, m, :], h_hi[0:M, m, :], ALU.subtract).then_inc(h_lo_s.sem, 1)

            def tile(i, u):
                name_tokens(i + 1)
                gated(i, u, 0)
                gated(i, u, 1)
                hidden_lo(i, 0)
                gated(i, u, 2)
                hidden_lo(i, 1)
                hidden_lo(i, 2)
                x_part(i + 1)
                dve.wait_ge(y_psum.sem, y_psum.at(i))
                dve.wait_ge(y_stored.sem, y_stored.at(i, 0))
                for half in range(HALF):
                    ins = dve.tensor_tensor(y[:, half, :], bank[4 + half][:, 0:D], b2[:, u, :], ALU.add)
                ins.then_inc(y_ready.sem, 1)

            def prologue():
                name_tokens(0)
                split(0, 0, 0)
                x_part(0)

            def table():
                n = ROUTED_SLOTS // P
                dve.wait_ge(table_loaded.sem, 16)
                dve.tensor_copy(table_f[:, :], table_rows[:, :]).then_inc(table_f_s.sem, 1)
                dve.wait_ge(table_psum.sem, 1)
                dve.tensor_copy(tokens[:, T // P:T // P + n], bank[0][:, 0:n]).then_inc(tokens_s.sem, 1)
                dve.wait_ge(tokens_s.sem, 1)

            over_experts(dve, prologue, lambda e, u, first: split(e + 1, 1 - u, first), tile, table)

        @block.tensor
        def _(pe):
            def x_transposes(i):
                pe.wait_ge(gathered.sem, gathered.at(i))
                for c in range(DC):
                    for half in range(HALF):
                        mm = pe.transpose(bank[3][:, c * ETOK + half * P:c * ETOK + half * P + P],
                                          xg[:, half, c * P:(c + 1) * P], identf[:, :])
                mm.then_inc(gT_psum.sem, 1)

            def tile(i, u):
                pe.wait_ge(gT_lo_s.sem, gT_lo_s.at(i))
                for m, (h0, M) in enumerate(HT):
                    pe.wait_ge(prod_s.sem, prod_s.at(i, 0))
                    for side in range(2):
                        cols = slice(side * H0 + h0, side * H0 + h0 + M)
                        mm = three_products(pe, bank[m][0:M, side * ETOK:(side + 1) * ETOK],
                                            lambda c: w13_hi[:, u, c, cols], lambda c: w13_lo[:, u, c, cols],
                                            lambda c: xT_hi[:, c, :], lambda c: xT_lo[:, c, :], range(DC))
                    mm.then_inc(gu_psum.sem, 1)
                x_transposes(i + 1)
                pe.wait_ge(y_ready.sem, y_ready.at(i, 0))
                for m, (_, M) in enumerate(HT):
                    pe.wait_ge(h_lo_s.sem, h_lo_s.at(i, m + 1))
                    for half in range(HALF):
                        tok = slice(half * P, (half + 1) * P)
                        mm = three_products(pe, bank[4 + half][:, 0:D], lambda m: h_hi[0:M, m, tok], lambda m: h_lo[0:M, m, tok],
                                            lambda m: w2_hi[0:M, u, m, :], lambda m: w2_lo[0:M, u, m, :], (m,),
                                            first=m == 0, last=m == HM - 1)
                mm.then_inc(y_psum.sem, 1)

            def new_expert(e, u, first):
                pe.wait_ge(e_lo.sem, e_lo.at(e))
                pe.nop(nofuse=True)

            def table():
                n = ROUTED_SLOTS // P
                pe.wait_ge(table_f_s.sem, 1)
                pe.wait_ge(prod_s.sem, prod_s.at(SHARED_TILES - 2))
                pe.transpose(bank[0][:, 0:n], table_f[:, :], identf[0:n, 0:n]).then_inc(table_psum.sem, 1)
                pe.wait_ge(tokens_s.sem, 1)

            over_experts(pe, lambda: x_transposes(0), new_expert, tile, table)


PACK = {}
_at = 0
for _name, _shape in (("wz", (DC, D)), ("wh", (DC, D)), ("fc1", (DC, LAT)), ("gate", (DC, E)), ("up", (DC, UP)),
                      ("w1", (E, INTER)), ("w2", (E, LAT)), ("wg", (DC, D)), ("down", (UP // P, D)), ("fc2", (1, D))):
    PACK[_name] = (_at, _shape)
    _at += _shape[0] * _shape[1]
PACKED = _at
BZ, BH, BG = 0, DC, 2 * DC


def layer1_phase(nc, w, dram, consts, route, out):
    with ExitStack() as ctx:
        def sb(name, shape, dt=F32):
            return ctx.enter_context(nc.sbuf_tensor(name, shape, dt))

        def sig(name, per):
            return Signal(nc, ctx, name, per)

        identf, iota8 = consts["identf"], consts["iota8"]
        CHUNKS = 4
        w32 = sb("l1_w32", [P, PACKED])
        w_hi, w_lo = (sb(f"l1_w_{k}", [P, PACKED], F16) for k in ("hi", "lo"))

        def part(t, name, row, cols):
            at, (_, n) = PACK[name]
            return t[:, at + row * n + cols.start:at + row * n + cols.stop]

        bias = sb("l1_bias", [P, 3 * DC])
        neg_bz = sb("neg_bz", [P, DC])
        corr = sb("corr", [P, E])
        minus_half = sb("l1_minus_half", [P, TT])
        xin = sb("xin", [P, TT, D])
        ysh = sb("ysh", [P, TT, D])
        rows_k = sb("rows_k", [P, TT, 2, D])
        slot = sb("slot", [P, TT, 2], I32)
        wk = sb("wk", [P, TT, 2])
        x2 = sb("x2", [P, 2, TT, D])
        stats = sb("l1_stats", [P, TT, 6])
        mv = sb("l1_mv", [P, TT, 2])
        var_eps = sb("l1_var_eps", [P, TT])
        rstd = sb("l1_rstd", [P, TT])
        xn = sb("l1_xn", [P, TT, D])
        xT_hi, xT_lo = (sb(f"l1_xT_{k}", [P, DC, S], F16) for k in ("hi", "lo"))
        zs = sb("zs", [P, DC, S])
        keep = sb("keep", [P, DC, S])
        inject = sb("inject", [P, DC, S])
        hT = sb("hT", [P, DC, S])
        hT_hi, hT_lo = (sb(f"hT_{k}", [P, DC, S], F16) for k in ("hi", "lo"))
        gs = sb("gs", [P, DC, S])
        gh = sb("gh", [P, DC, S])
        lat_hi, lat_lo = (sb(f"lat_{k}", [P, S], F16) for k in ("hi", "lo"))
        sc = sb("l1_sc", [P, TT, E])
        sfc = sb("sfc", [P, TT, E])
        pairs = sb("pairs", [P, TT * 2, 6])
        gscore = sb("gscore", [P, TT, 2])
        gmask = sb("gmask", [P, TT, 2])
        top = sb("l1_top", [P, TT, 8])
        topi = sb("l1_topi", [P, TT, 8], U32)
        onehot = sb("l1_onehot", [P, 2, TT, E])
        chosen = sb("chosen", [P, TT, E])
        total = sb("total", [P, TT])
        weight = sb("weight", [P, TT, E])
        wT = sb("wT", [E, S])
        w_bc = sb("w_bc", [P, E, S])
        r = sb("r", [P, 3, S])
        rw = sb("rw", [P, 3, S])
        sq = sb("sq", [P, 3, S])
        up_hi, up_lo = (sb(f"up_{k}", [P, UP // P, S], F16) for k in ("hi", "lo"))
        he_hi, he_lo = (sb(f"he_{k}", [P, 3, S], F16) for k in ("hi", "lo"))
        comb_hi, comb_lo = (sb(f"comb_{k}", [P, S], F16) for k in ("hi", "lo"))
        y = sb("l1_y", [P, TT, D])
        bank = [ctx.enter_context(nc.psum_tensor(f"ybank{i}", [P, 512], F32)) for i in range(8)]
        OUT_BANK = (3, 4, 5, 7)
        NU = UP // P
        NR = NU + E

        loaded = sig("l1_loaded", 16 * 3)
        pack_loaded = [sig(f"pack_loaded{c}", 16) for c in range(CHUNKS)]
        pack_hi = sig("pack_hi", CHUNKS)
        pack_lo = sig("pack_lo", CHUNKS)
        half_filled = sig("half_filled", 1)
        neg_bz_s = sig("neg_bz_s", 1)
        xin_loaded = sig("xin_loaded", 32)
        slot_s = sig("slot_s", 2)
        gathered = sig("rows_gathered", 16 * TT * 2)
        x2_base = sig("x2_base", 1)
        x2_sum = sig("x2_sum", 2)
        dve_ln = sig("l1_dve_ln", 2)
        rstd_s = sig("l1_rstd_s", 2)
        xn_ready = sig("l1_xn_ready", 1)
        xT_psum = sig("l1_xT_psum", DC)
        xT_hi_s = sig("l1_xT_hi_s", DC)
        xT_lo_s = sig("l1_xT_lo_s", DC)
        zh_psum = sig("zh_psum", 2 * DC)
        lg_psum = sig("l1_lg_psum", 1)
        lat_psum = sig("lat_psum", 1)
        sc_s = sig("sc_s", 1)
        zs_s = sig("zs_s", DC)
        keep_s = sig("keep_s", DC)
        lat_hi_s = sig("lat_hi_s", 1)
        lat_lo_s = sig("lat_lo_s", 1)
        inject_s = sig("inject_s", DC)
        hT_s = sig("hT_s", DC)
        hT_hi_s = sig("hT_hi_s", DC)
        hT_lo_s = sig("hT_lo_s", DC)
        rt = sig("l1_rt", 15)
        wT_psum = sig("wT_psum", 1)
        wT_s = sig("wT_s", 1)
        wT_stored = sig("wT_stored", 16)
        w_bc_loaded = sig("w_bc_loaded", 16)
        u_psum = sig("u_psum", NR)
        r_s = sig("r_s", NR)
        rw_s = sig("rw_s", E)
        sq_s = sig("sq_s", NR)
        hid_hi = sig("hid_hi", NR)
        hid_lo = sig("hid_lo", NR)
        comb_psum = sig("comb_psum", E)
        comb_hi_s = sig("comb_hi_s", 1)
        comb_lo_s = sig("comb_lo_s", 1)
        g_psum = sig("g_psum", DC)
        gs_s = sig("gs_s", DC)
        gh_s = sig("gh_s", DC)
        out_psum = sig("out_psum", TT)
        y_ready = sig("l1_y_ready", 1)
        y_stored = sig("l1_y_stored", 16)

        def rows(t, b):
            return t[bass.ds(b * S, S), :].rearrange("(t p) d -> p t d", p=P)

        def pipeline(eng, front, step):
            front(0, 0)
            step(0, 0, True)
            with eng.Fori(0, NB // 2 - 1) as i:
                for u in (1, 0):
                    step(2 * i + 2 - u, u, True)
            step(NB - 1, 1, False)

        def hidden_bank(n):
            return bank[n % 3]

        block = ctx.enter_context(nc.Block())

        @block.sync
        def _(sp):
            for c in range(CHUNKS):
                cols = slice(PACKED * c // CHUNKS // 2 * 2, PACKED * (c + 1) // CHUNKS // 2 * 2)
                sp.dma_start(w32[:, cols], w["pack"][:, cols]).then_inc(pack_loaded[c].sem, 16)
            sp.dma_start(bias[:, :], w["bias"]).then_inc(loaded.sem, 16)
            sp.dma_start(corr[:, :], w["corr"].partition_broadcast(P)).then_inc(loaded.sem, 16)
            sp.dma_start(neg_bz[:, :], w["bias"][:, BZ:BZ + DC]).then_inc(loaded.sem, 16)

            def front(b, u):
                sp.wait_ge(x2_base.sem, x2_base.at(b, 0))
                sp.dma_start(xin[:, :, :], rows(dram["x1"], b)).then_inc(xin_loaded.sem, 16)
                sp.dma_start(ysh[:, :, :], rows(dram["y"], b)).then_inc(xin_loaded.sem, 16)

            def step(b, u, more):
                sp.wait_ge(wT_s.sem, wT_s.at(b))
                sp.dma_start(dram["wT"], wT[:, :]).then_inc(wT_stored.sem, 16)
                sp.wait_ge(wT_stored.sem, wT_stored.at(b))
                sp.nop(nofuse=True)
                sp.wait_ge(rw_s.sem, rw_s.at(b, 0))
                sp.dma_start(w_bc[:, :, :], dram["wT"].partition_broadcast(P)).then_inc(w_bc_loaded.sem, 16)
                if more:
                    front(b + 1, 1 - u)
                sp.wait_ge(y_ready.sem, y_ready.at(b))
                sp.dma_start(rows(out, b), y[:, :, :]).then_inc(y_stored.sem, 16)

            pipeline(sp, front, step)
            sp.wait_ge(y_stored.sem, y_stored.at(NB - 1))

        @block.gpsimd
        def _(pool):
            pool.memset(minus_half[:, :], -0.5).then_inc(half_filled.sem, 1)
            pool.wait_ge(half_filled.sem, 1)

            def front(b, u):
                pool.wait_ge(xin_loaded.sem, xin_loaded.at(b))
                pool.wait_ge(y_ready.sem, y_ready.at(b - 1, 0))
                pool.tensor_tensor(x2[:, u, :, :], xin[:, :, :], ysh[:, :, :], ALU.add).then_inc(x2_base.sem, 1)
                pool.wait_ge(x2_sum.sem, x2_sum.at(b, 0))
                pool.wait_ge(slot_s.sem, slot_s.at(b))
                pool.nop(nofuse=True)
                for t in range(TT):
                    for k in range(2):
                        pool.indirect_dma_start(rows_k[:, t, k, :], None, dram["y"],
                                                bass.IndirectOffsetOnAxis(slot[:, t, k:k + 1], 0)).then_inc(gathered.sem, 16)
                pool.wait_ge(dve_ln.sem, dve_ln.at(b))
                pool.tensor_tensor(var_eps[:, :], mv[:, :, 1], consts["eps_col"][:, 0:TT], ALU.add).then_inc(rstd_s.sem, 1)
                pool.wait_ge(rstd_s.sem, rstd_s.at(b, 1))
                pool.tensor_tensor(rstd[:, :], var_eps[:, :], minus_half[:, :], ALU.pow).then_inc(rstd_s.sem, 1)

            def step(b, u, more):
                pool.wait_ge(w_bc_loaded.sem, w_bc_loaded.at(b))
                for e in range(E):
                    n = NU + e
                    pool.wait_ge(r_s.sem, r_s.at(b, n + 1))
                    pool.wait_ge(sq_s.sem, sq_s.at(b, n - 2))
                    pool.tensor_tensor(rw[:, n % 3, :], r[:, n % 3, :], w_bc[:, e, :], ALU.mult).then_inc(rw_s.sem, 1)
                if more:
                    front(b + 1, 1 - u)

            pipeline(pool, front, step)

        @block.scalar
        def _(act):
            for c in range(CHUNKS):
                cols = slice(PACKED * c // CHUNKS // 2 * 2, PACKED * (c + 1) // CHUNKS // 2 * 2)
                act.wait_ge(pack_loaded[c].sem, 16)
                act.activation(w_hi[:, cols], w32[:, cols], ACT.Copy).then_inc(pack_hi.sem, 1)
            act.wait_ge(loaded.sem, loaded.at(0))
            act.wait_ge(neg_bz_s.sem, 1)

            def front(b, u):
                for c in range(DC):
                    act.wait_ge(xT_psum.sem, xT_psum.at(b, c + 1))
                    act.wait_ge(u_psum.sem, u_psum.at(b, 0))
                    act.activation(xT_hi[:, c, :], bank[c][:, :], ACT.Copy).then_inc(xT_hi_s.sem, 1)

            def relu(b, n):
                act.wait_ge(u_psum.sem, u_psum.at(b, n + 1))
                if n >= 3:
                    act.wait_ge(sq_s.sem, sq_s.at(b, n - 2))
                act.activation(r[:, n % 3, :], hidden_bank(n)[:, :], ACT.Relu).then_inc(r_s.sem, 1)

            def hidden_hi(b, n):
                act.wait_ge(sq_s.sem, sq_s.at(b, n + 1))
                if n < NU:
                    act.wait_ge(out_psum.sem, out_psum.at(b, 0))
                    dst = up_hi[:, n, :]
                else:
                    if n - NU >= 3:
                        act.wait_ge(comb_psum.sem, comb_psum.at(b, n - NU - 2))
                    dst = he_hi[:, (n - NU) % 3, :]
                act.activation(dst, sq[:, n % 3, :], ACT.Copy).then_inc(hid_hi.sem, 1)

            def step(b, u, more):
                for c in range(DC):
                    act.wait_ge(zh_psum.sem, zh_psum.at(b, c + 1))
                    act.activation(zs[:, c, :], bank[2 + c][:, :], ACT.Sigmoid, bias=bias[:, BZ + c:BZ + c + 1]).then_inc(zs_s.sem, 1)
                    act.activation(keep[:, c, :], bank[2 + c][:, :], ACT.Sigmoid, bias=neg_bz[:, c:c + 1],
                                   scale=-1.0).then_inc(keep_s.sem, 1)
                act.wait_ge(lg_psum.sem, lg_psum.at(b))
                act.activation(sc[:, :, :], bank[7][:, 0:TT * E].rearrange("p (t e) -> p t e", e=E),
                               ACT.Sigmoid).then_inc(sc_s.sem, 1)
                act.wait_ge(lat_psum.sem, lat_psum.at(b))
                act.activation(lat_hi[:, :], bank[6][:, :], ACT.Copy).then_inc(lat_hi_s.sem, 1)
                for n in range(NR + 2):
                    if n < NR:
                        relu(b, n)
                    if n >= 2:
                        hidden_hi(b, n - 2)
                    if n == 5:
                        for c in range(DC):
                            act.wait_ge(hT_s.sem, hT_s.at(b, c + 1))
                            act.activation(hT_hi[:, c, :], hT[:, c, :], ACT.Copy).then_inc(hT_hi_s.sem, 1)
                for c in range(DC):
                    act.wait_ge(g_psum.sem, g_psum.at(b, c + 1))
                    act.activation(gs[:, c, :], bank[c][:, :], ACT.Sigmoid, bias=bias[:, BG + c:BG + c + 1]).then_inc(gs_s.sem, 1)
                act.wait_ge(comb_psum.sem, comb_psum.at(b))
                act.activation(comb_hi[:, :], bank[6][:, :], ACT.Copy).then_inc(comb_hi_s.sem, 1)
                if more:
                    front(b + 1, 1 - u)

            pipeline(act, front, step)

        @block.vector
        def _(dve):
            for c in range(CHUNKS):
                cols = slice(PACKED * c // CHUNKS // 2 * 2, PACKED * (c + 1) // CHUNKS // 2 * 2)
                dve.wait_ge(pack_hi.sem, c + 1)
                dve.tensor_tensor(w_lo[:, cols], w32[:, cols], w_hi[:, cols], ALU.subtract).then_inc(pack_lo.sem, 1)
            dve.wait_ge(loaded.sem, loaded.at(0))
            dve.tensor_scalar(neg_bz[:, :], neg_bz[:, :], -1.0, None, ALU.mult).then_inc(neg_bz_s.sem, 1)

            def front(b, u):
                tiles = bass.ds(b * TT, TT)
                dve.wait_ge(gathered.sem, gathered.at(b, 0))
                dve.tensor_scalar(slot[:, :, :], route["pos"][:, tiles, :], float(SHARED_TILES * ETOK), None,
                                  ALU.add).then_inc(slot_s.sem, 1)
                dve.tensor_copy(wk[:, :, :], route["weights"][:, tiles, :]).then_inc(slot_s.sem, 1)
                dve.wait_ge(slot_s.sem, slot_s.at(b))
                dve.wait_ge(x2_base.sem, x2_base.at(b))
                dve.wait_ge(gathered.sem, gathered.at(b))
                for k in range(2):
                    for t in range(TT):
                        ins = dve.scalar_tensor_tensor(x2[:, u, t, :], rows_k[:, t, k, :], wk[:, t, k:k + 1], x2[:, u, t, :],
                                                       ALU.mult, ALU.add)
                    ins.then_inc(x2_sum.sem, 1)
                    dve.wait_ge(x2_sum.sem, x2_sum.at(b, k + 1))
                for t in range(TT):
                    ins = dve.bn_stats(stats[:, t, :], x2[:, u, t, :])
                ins.then_inc(dve_ln.sem, 1)
                dve.wait_ge(dve_ln.sem, dve_ln.at(b, 1))
                dve.nop(nofuse=True)
                for t in range(TT):
                    ins = dve.bn_aggr(mv[:, t, :], stats[:, t, :])
                ins.then_inc(dve_ln.sem, 1)
                dve.wait_ge(dve_ln.sem, dve_ln.at(b))
                dve.wait_ge(rstd_s.sem, rstd_s.at(b))
                for t in range(TT):
                    ins = dve.tensor_scalar(xn[:, t, :], x2[:, u, t, :], mv[:, t, 0:1], rstd[:, t:t + 1],
                                            ALU.subtract, ALU.mult)
                ins.then_inc(xn_ready.sem, 1)

            def x_low(b):
                for c in range(DC):
                    dve.wait_ge(xT_hi_s.sem, xT_hi_s.at(b, c + 1))
                    dve.tensor_tensor(xT_lo[:, c, :], bank[c][:, :], xT_hi[:, c, :], ALU.subtract).then_inc(xT_lo_s.sem, 1)

            def router(b):
                at = [0]

                def done(ins):
                    ins.then_inc(rt.sem, 1)
                    at[0] += 1
                    dve.wait_ge(rt.sem, rt.at(b, at[0]))

                dve.wait_ge(sc_s.sem, sc_s.at(b))
                done(dve.tensor_tensor(sfc[:, :, :], sc[:, :, :], corr[:, :].unsqueeze(1).to_broadcast([P, TT, E]), ALU.add))
                g4 = sfc[:, :, :].rearrange("p t (g s) -> p (t g) s", s=E // 2)
                dve.tensor_tensor(pairs[:, :, 0:3], g4[:, :, 0:3], g4[:, :, 1:4], ALU.add)
                dve.tensor_tensor(pairs[:, :, 3:5], g4[:, :, 0:2], g4[:, :, 2:4], ALU.add)
                done(dve.tensor_tensor(pairs[:, :, 5:6], g4[:, :, 0:1], g4[:, :, 3:4], ALU.add))
                done(dve.tensor_reduce(gscore[:, :, :].rearrange("p t g -> p (t g)"), pairs[:, :, :], AX.X, ALU.max))
                done(dve.tensor_tensor(gmask[:, :, 0:1], gscore[:, :, 0:1], gscore[:, :, 1:2], ALU.is_ge))
                done(dve.tensor_scalar(gmask[:, :, 1:2], gmask[:, :, 0:1], -1.0, 1.0, ALU.mult, ALU.add))
                done(dve.tensor_tensor(g4, g4, gmask[:, :, :].rearrange("p t g -> p (t g)").unsqueeze(2).to_broadcast([P, TT * 2, E // 2]),
                                       ALU.mult))
                dve.nop(nofuse=True)
                for t in range(TT):
                    ins = dve.max(top[:, t, :], sfc[:, t, :])
                done(ins)
                dve.nop(nofuse=True)
                for t in range(TT):
                    ins = dve.max_index(topi[:, t, :], top[:, t, :], sfc[:, t, :])
                done(ins)
                for k in range(2):
                    ins = dve.tensor_tensor(onehot[:, k, :, :], iota8[:, :].unsqueeze(1).to_broadcast([P, TT, E]),
                                            topi[:, :, k:k + 1].to_broadcast([P, TT, E]), ALU.is_equal)
                done(ins)
                done(dve.tensor_tensor(chosen[:, :, :], onehot[:, 0, :, :], onehot[:, 1, :, :], ALU.add))
                done(dve.tensor_tensor(chosen[:, :, :], chosen[:, :, :], sc[:, :, :], ALU.mult))
                done(dve.tensor_reduce(total[:, :], chosen[:, :, :], AX.X, ALU.add))
                done(dve.tensor_scalar(total[:, :], total[:, :], 1e-20, None, ALU.add))
                done(dve.reciprocal(total[:, :], total[:, :]))
                done(dve.tensor_tensor(weight[:, :, :], chosen[:, :, :], total[:, :].unsqueeze(2).to_broadcast([P, TT, E]), ALU.mult))
                assert at[0] == rt.per

            def square(b, n):
                if n < NU:
                    dve.wait_ge(r_s.sem, r_s.at(b, n + 1))
                    other = r
                else:
                    dve.wait_ge(rw_s.sem, rw_s.at(b, n - NU + 1))
                    other = rw
                if n >= 3:
                    dve.wait_ge(hid_lo.sem, hid_lo.at(b, n - 2))
                dve.tensor_tensor(sq[:, n % 3, :], r[:, n % 3, :], other[:, n % 3, :], ALU.mult).then_inc(sq_s.sem, 1)

            def hidden_low(b, n):
                dve.wait_ge(hid_hi.sem, hid_hi.at(b, n + 1))
                hi, lo = (up_hi[:, n, :], up_lo[:, n, :]) if n < NU else (he_hi[:, (n - NU) % 3, :], he_lo[:, (n - NU) % 3, :])
                dve.tensor_tensor(lo, sq[:, n % 3, :], hi, ALU.subtract).then_inc(hid_lo.sem, 1)

            def step(b, u, more):
                for c in range(DC):
                    dve.wait_ge(zh_psum.sem, zh_psum.at(b, DC + c + 1))
                    dve.wait_ge(zs_s.sem, zs_s.at(b, c + 1))
                    dve.scalar_tensor_tensor(inject[:, c, :], bank[4 + c][:, :], bias[:, BH + c:BH + c + 1], zs[:, c, :],
                                             ALU.add, ALU.mult).then_inc(inject_s.sem, 1)
                dve.wait_ge(lat_hi_s.sem, lat_hi_s.at(b))
                dve.tensor_tensor(lat_lo[:, :], bank[6][:, :], lat_hi[:, :], ALU.subtract).then_inc(lat_lo_s.sem, 1)
                router(b)
                for c in range(DC):
                    dve.wait_ge(inject_s.sem, inject_s.at(b, c + 1))
                    dve.wait_ge(keep_s.sem, keep_s.at(b, c + 1))
                    dve.tensor_tensor_scan(hT[:, c, :], keep[:, c, :], inject[:, c, :], 0.0, ALU.mult, ALU.add).then_inc(hT_s.sem, 1)
                for n in range(NR + 2):
                    if n == 3:
                        dve.wait_ge(wT_psum.sem, wT_psum.at(b))
                        dve.tensor_copy(wT[:, :], bank[7][0:E, :]).then_inc(wT_s.sem, 1)
                    if n < NR:
                        square(b, n)
                    if n >= 2:
                        hidden_low(b, n - 2)
                    if n == 7:
                        for c in range(DC):
                            dve.wait_ge(hT_hi_s.sem, hT_hi_s.at(b, c + 1))
                            dve.tensor_tensor(hT_lo[:, c, :], hT[:, c, :], hT_hi[:, c, :], ALU.subtract).then_inc(hT_lo_s.sem, 1)
                for c in range(DC):
                    dve.wait_ge(gs_s.sem, gs_s.at(b, c + 1))
                    dve.tensor_tensor(gh[:, c, :], gs[:, c, :], hT[:, c, :], ALU.mult).then_inc(gh_s.sem, 1)
                dve.wait_ge(comb_hi_s.sem, comb_hi_s.at(b))
                dve.tensor_tensor(comb_lo[:, :], bank[6][:, :], comb_hi[:, :], ALU.subtract).then_inc(comb_lo_s.sem, 1)
                if more:
                    front(b + 1, 1 - u)
                dve.wait_ge(y_stored.sem, y_stored.at(b, 0))
                for t in range(TT):
                    dve.wait_ge(out_psum.sem, out_psum.at(b, t + 1))
                    ins = dve.tensor_tensor(y[:, t, :], bank[OUT_BANK[t]][:, 0:D], x2[:, u, t, :], ALU.add)
                ins.then_inc(y_ready.sem, 1)
                if more:
                    x_low(b + 1)

            def first(b, u):
                front(b, u)
                x_low(b)

            pipeline(dve, first, step)

        @block.tensor
        def _(pe):
            whole = slice(0, S)

            def transposes(b):
                pe.wait_ge(xn_ready.sem, xn_ready.at(b))
                for c in range(DC):
                    for t in range(TT):
                        mm = pe.transpose(bank[c][:, t * P:(t + 1) * P], xn[:, t, c * P:(c + 1) * P], identf[:, :])
                    mm.then_inc(xT_psum.sem, 1)

            def from_x(out, name, cols):
                return three_products(pe, out, lambda c: part(w_hi, name, c, cols), lambda c: part(w_lo, name, c, cols),
                                      lambda c: xT_hi[:, c, :], lambda c: xT_lo[:, c, :], range(DC))

            def hidden(b, n):
                if n >= 3:
                    pe.wait_ge(r_s.sem, r_s.at(b, n - 2))
                if n < NU:
                    mm = from_x(hidden_bank(n)[:, :], "up", slice(n * P, (n + 1) * P))
                else:
                    mm = three_products(pe, hidden_bank(n)[:, :], lambda e: part(w_hi, "w1", e, slice(0, INTER)),
                                        lambda e: part(w_lo, "w1", e, slice(0, INTER)),
                                        lambda e: lat_hi[:, :], lambda e: lat_lo[:, :], (n - NU,))
                mm.then_inc(u_psum.sem, 1)

            def combine(b, e):
                pe.wait_ge(hid_lo.sem, hid_lo.at(b, NU + e + 1))
                three_products(pe, bank[6][:, :], lambda e: part(w_hi, "w2", e, slice(0, LAT)),
                               lambda e: part(w_lo, "w2", e, slice(0, LAT)),
                               lambda e: he_hi[:, e % 3, :], lambda e: he_lo[:, e % 3, :], (e,),
                               first=e == 0, last=e == E - 1).then_inc(comb_psum.sem, 1)

            def step(b, u, more):
                pe.wait_ge(xT_lo_s.sem, xT_lo_s.at(b))
                pe.wait_ge(y_ready.sem, y_ready.at(b, 0))
                for c in range(DC):
                    from_x(bank[2 + c][:, :], "wz", slice(c * P, (c + 1) * P)).then_inc(zh_psum.sem, 1)
                for c in range(DC):
                    from_x(bank[4 + c][:, :], "wh", slice(c * P, (c + 1) * P)).then_inc(zh_psum.sem, 1)
                for t in range(TT):
                    tok = slice(t * P, (t + 1) * P)
                    mm = three_products(pe, bank[7][:, t * E:(t + 1) * E], lambda c: xT_hi[:, c, tok], lambda c: xT_lo[:, c, tok],
                                        lambda c: part(w_hi, "gate", c, slice(0, E)), lambda c: part(w_lo, "gate", c, slice(0, E)),
                                        range(DC))
                mm.then_inc(lg_psum.sem, 1)
                from_x(bank[6][:, :], "fc1", slice(0, LAT)).then_inc(lat_psum.sem, 1)
                pe.wait_ge(keep_s.sem, keep_s.at(b))
                for n in range(NU):
                    hidden(b, n)
                    if n == 4:
                        pe.wait_ge(rt.sem, rt.at(b))
                        for t in range(TT):
                            mm = pe.transpose(bank[7][0:E, t * P:(t + 1) * P], weight[:, t, :], identf[:, :])
                        mm.then_inc(wT_psum.sem, 1)
                pe.wait_ge(lat_lo_s.sem, lat_lo_s.at(b))
                for e in range(E + 3):
                    if e < E:
                        hidden(b, NU + e)
                    if e >= 3:
                        combine(b, e - 3)
                pe.wait_ge(hT_lo_s.sem, hT_lo_s.at(b))
                pe.wait_ge(r_s.sem, r_s.at(b))
                for c in range(DC):
                    three_products(pe, bank[c][:, :], lambda k: part(w_hi, "wg", k, slice(c * P, (c + 1) * P)),
                                   lambda k: part(w_lo, "wg", k, slice(c * P, (c + 1) * P)),
                                   lambda k: hT_hi[:, k, :], lambda k: hT_lo[:, k, :], range(DC)).then_inc(g_psum.sem, 1)
                pe.wait_ge(wT_s.sem, wT_s.at(b))
                pe.wait_ge(inject_s.sem, inject_s.at(b))
                for t in range(TT):
                    tok = slice(t * P, (t + 1) * P)
                    o = bank[OUT_BANK[t]][:, 0:D]
                    three_products(pe, o, lambda n: up_hi[:, n, tok], lambda n: up_lo[:, n, tok],
                                   lambda n: part(w_hi, "down", n, slice(0, D)), lambda n: part(w_lo, "down", n, slice(0, D)),
                                   range(NU), last=False)
                    if t == 0:
                        pe.wait_ge(comb_lo_s.sem, comb_lo_s.at(b))
                        pe.wait_ge(gh_s.sem, gh_s.at(b))
                    three_products(pe, o, lambda n: comb_hi[:, tok], lambda n: comb_lo[:, tok],
                                   lambda n: part(w_hi, "fc2", 0, slice(0, D)), lambda n: part(w_lo, "fc2", 0, slice(0, D)),
                                   (0,), first=False, last=False)
                    for c in range(DC):
                        mm = pe.matmul(bank[OUT_BANK[t]][:, c * P:(c + 1) * P], gh[:, c, tok], identf[:, :],
                                       start=False, stop=c == DC - 1)
                    mm.then_inc(out_psum.sem, 1)
                    if t == 1 and more:
                        pe.wait_ge(gs_s.sem, gs_s.at(b))
                        transposes(b + 1)

            pe.wait_ge(pack_lo.sem, CHUNKS)
            pipeline(pe, lambda b, u: transposes(b), step)


_INS = ["x", "wqkv", "gate0", "wout", "bqk", "bv", "bout", "gate_b", "w13", "w2", "b13", "b2", "pack", "bias", "corr"]


def build(nc, ins, out):
    with ExitStack() as ctx:
        def sb(name, shape, dt=F32):
            return ctx.enter_context(nc.sbuf_tensor(name, shape, dt))

        consts = constants(nc, ctx)
        dram = {"x1": nc.dram_tensor("x1_dram", (T, D), F32).ap(),
                "xn": nc.dram_tensor("xn_dram", (T, D), F32).ap(),
                "qk_hi": nc.dram_tensor("qk_hi_dram", (2 * D, S), F16).ap(),
                "qk_lo": nc.dram_tensor("qk_lo_dram", (2 * D, S), F16).ap(),
                "y": nc.dram_tensor("y_dram", (MAX_TILES * ETOK, D), F32).ap(),
                "wT": nc.dram_tensor("wT_dram", (E, S), F32).ap()}
        route = {"weights": sb("route_weights", [P, T // P, 2]), "rank": sb("route_rank", [P, T // P, 2]),
                 "onehot": sb("route_onehot", [P, T // P, 2, E]), "run": sb("route_run", [P, TT + 1, E]),
                 "bounds": sb("bounds", [P, E + 1], I32), "pos": sb("pos", [P, T // P, 2], I32),
                 "tokens": sb("tokens", [P, SLOTS // P], I32), "ids": sb("ids", [P, T // P], I32),
                 "table": nc.dram_tensor("table_dram", (ROUTED_SLOTS, 1), I32).ap()}
        mix_phase(nc, ins["x"], ins, dram, consts, route)
        slots_phase(nc, route)
        experts_phase(nc, ins, dram, consts, route)
        layer1_phase(nc, ins, dram, consts, route, out)


def _layout(i):
    import numpy as np

    def rows(a):
        a = np.asarray(a)
        return a.reshape(-1, P, a.shape[-1]).transpose(1, 0, 2).reshape(P, -1)

    wqkv = np.asarray(i["L0_attn_Wqkv"]).reshape(NH, D, 3, HD).transpose(1, 2, 0, 3).reshape(D, 3 * D)
    bqkv = np.asarray(i["L0_attn_bqkv"]).reshape(NH, 3, HD).transpose(1, 0, 2).reshape(3 * D)
    f = {k: np.asarray(i["L0_ffn_" + k]) for k in ("w1", "w3", "w2", "b1", "b3", "b2", "sw1", "sw3", "sw2", "sb1", "sb3", "sb2")}

    def experts(shared, routed):
        return np.concatenate([shared[None], routed, routed[-1:]])

    b13 = np.zeros((NX + 1, P, 2 * len(HT)), f["b1"].dtype)
    for side, b in enumerate((experts(f["sb1"], f["b1"]), experts(f["sb3"], f["b3"]))):
        for m, (h0, n) in enumerate(HT):
            b13[:, :n, side * len(HT) + m] = b[:, h0:h0 + n]
    a = {k: np.asarray(i["L1_attn_" + k]) for k in ("Wz", "bz", "Wh", "bh", "Wg", "bg")}
    g = {k: np.asarray(i["L1_ffn_" + k]) for k in ("gate", "corr_bias", "w1", "w2", "fc1_w", "fc2_w", "up_w", "down_w")}
    pack = {"wz": rows(a["Wz"].transpose(1, 0, 2).reshape(D, D)), "wh": rows(a["Wh"].transpose(1, 0, 2).reshape(D, D)),
            "fc1": rows(g["fc1_w"].T), "gate": rows(g["gate"].T), "up": rows(g["up_w"].T),
            "w1": g["w1"].transpose(2, 0, 1).reshape(LAT, -1), "w2": g["w2"].transpose(2, 0, 1).reshape(INTER, -1),
            "wg": rows(a["Wg"]), "down": rows(g["down_w"].T), "fc2": rows(g["fc2_w"].T)}
    return {
        "x": np.asarray(i["L0_attn_x"]).reshape(T, D), "wqkv": wqkv, "gate0": np.asarray(i["L0_ffn_gate_w"]).T,
        "wout": np.asarray(i["L0_attn_Wout"]), "bqk": bqkv[:2 * D].reshape(4, P).T, "bv": bqkv[2 * D:],
        "bout": np.asarray(i["L0_attn_bout"]), "gate_b": np.asarray(i["L0_ffn_gate_b"]),
        "w13": np.concatenate([experts(f["sw1"], f["w1"]), experts(f["sw3"], f["w3"])], 2),
        "w2": experts(f["sw2"], f["w2"]), "b13": b13, "b2": experts(f["sb2"], f["b2"])[:, None, :],
        "pack": np.concatenate([pack[n] for n in PACK], 1),
        "bias": np.concatenate([a["bz"].reshape(DC, P).T, a["bh"].reshape(DC, P).T, a["bg"].reshape(DC, P).T], 1),
        "corr": g["corr_bias"],
    }


def kernel(**inputs):
    import numpy as np
    import concourse.bacc as bacc
    from concourse.bass_utils import run_bass_kernel_spmd

    laid = _layout(inputs)
    nc = bacc.Bacc("TRN2", target_bir_lowering=False, num_devices=1)
    arrays, ins = {}, {}
    for name in _INS:
        a = np.ascontiguousarray(laid[name])
        arrays[f"in_{name}"] = a
        ins[name] = nc.dram_tensor(f"in_{name}", a.shape, mybir.dt.from_np(a.dtype), kind="ExternalInput").ap()
    out = nc.dram_tensor("out_0", (T, D), F32, kind="ExternalOutput").ap()
    build(nc, ins, out)
    r = run_bass_kernel_spmd(nc, [arrays], core_ids=[0])
    return r.results[0]["out_0"].reshape(NB, S, D)
```

```python
from contextlib import ExitStack

import concourse.bass as bass
from concourse import mybir

F32 = mybir.dt.float32
F16 = mybir.dt.float16
BF16 = mybir.dt.bfloat16
I32 = mybir.dt.int32
U32 = mybir.dt.uint32
ALU = mybir.AluOpType
ACT = mybir.ActivationFunctionType
AX = mybir.AxisListType

P = 128
NB, S, D = 8, 512, 256
T = NB * S
DC = D // P
TT = S // P
NH, HD = 16, 16
E = 8
EPS = 1e-5
H0 = 352
HT = [(0, 128), (128, 128), (256, 96)]
ETOK = 256
NX = E + 1
SHARED_TILES = T // ETOK
MAX_TILES = SHARED_TILES + 2 * T // ETOK + E
SLOTS = (MAX_TILES + 1) * ETOK
ROUTED_SLOTS = SLOTS - SHARED_TILES * ETOK
LAT, INTER, UP = 128, 128, 1024
COMBINE_LAG = 5
HE = 5

STK = 96
PCOLS = P * (TT * (TT + 1) // 2)
QOFF = [P * j * (j + 1) // 2 for j in range(TT)]
KOFF = [P * sum(TT - i for i in range(k)) for k in range(TT)]
Q_UNITS = ((0, 1), (2,), (3,))
K_UNITS = ((0,), (1,), (2, 3))
U = len(Q_UNITS)
MASKED = -1e30
AT_CHOICE, AT_RANKS, AT_DIVIDE, AT_OUT_T, AT_PROJ = 0, 1, 0, (2, 3), (4, 5)
AT_NORM, AT_X_T, AT_Q, AT_K, AT_V, AT_ROUTE = 3, (6, 7), (8, 9), (10, 11), (12, 13), 14
LAG = 1


class Signal:

    def __init__(self, nc, ctx, name, per_step):
        self.sem = ctx.enter_context(nc.semaphore(name))
        self.per = per_step

    def at(self, step, n=None):
        v = step * self.per + (self.per if n is None else n)
        return max(v, 0) if isinstance(v, int) else v


def three_products(pe, out, hi_a, lo_a, hi_b, lo_b, chunks, first=True, last=True):
    n = len(chunks)
    for x, c in enumerate(chunks):
        pe.matmul(out, hi_a(c), hi_b(c), start=first and x == 0, stop=False)
        pe.matmul(out, hi_a(c), lo_b(c), start=False, stop=False)
        mm = pe.matmul(out, lo_a(c), hi_b(c), start=False, stop=last and x == n - 1)
    return mm


def mix_phase(nc, x, w, dram, consts, route):
    with ExitStack() as ctx:
        def sb(name, shape, dt=F32):
            return ctx.enter_context(nc.sbuf_tensor(name, shape, dt))

        def ps(name, shape, dt=F32):
            return ctx.enter_context(nc.psum_tensor(name, shape, dt))

        def sig(name, per):
            return Signal(nc, ctx, name, per)

        identf, identb, ones_b, tri, maskadd, iota8 = (consts[k] for k in ("identf", "identb", "ones_b", "tri", "maskadd", "iota8"))
        wqkv32 = sb("wqkv32", [P, DC, 3 * D])
        wout32 = sb("wout32", [P, DC, D])
        gate32 = sb("gate32", [P, DC, E])
        wqkv_hi, wqkv_lo = (sb(f"wqkv_{k}", [P, DC, 3 * D], F16) for k in ("hi", "lo"))
        wout_hi, wout_lo = (sb(f"wout_{k}", [P, DC, D], F16) for k in ("hi", "lo"))
        gate_hi, gate_lo = (sb(f"gate_{k}", [P, DC, E], F16) for k in ("hi", "lo"))
        bqk = sb("bqk", [P, 4])
        bq = sb("bq", [P, 2])
        bv_row = sb("bv_row", [P, D])
        bout_row = sb("bout_row", [P, D])
        gateb_row = sb("gateb_row", [P, E])
        zeros16 = sb("zeros16", [P, S], F16)
        zeros_f = sb("zeros_f", [P, D])
        xr = sb("xr", [P, TT, D])
        stats = sb("stats", [P, TT, 6])
        mv = sb("mv", [P, TT, 2])
        var_eps = sb("var_eps", [P, TT])
        rstd = sb("rstd", [P, TT])
        minus_half = sb("minus_half", [P, TT])
        xb = sb("xb", [P, 2, TT, D])
        xn = sb("xn", [P, TT, D])
        xT_hi, xT_lo = (sb(f"xT_{k}", [P, DC, S], F16) for k in ("hi", "lo"))
        qk_hi, qk_lo = (sb(f"qk_{k}", [P, 4, S], F16) for k in ("hi", "lo"))
        q32 = sb("q32", [P, 2, S])
        q_stack = sb("q_stack", [STK, 2, NH, S], F16)
        k_stack = sb("k_stack", [STK, 2, NH, S], F16)
        v32 = sb("v32", [P, TT, D])
        v_hi, v_lo = (sb(f"v_{k}", [P, 2, TT, NH, HD], F16) for k in ("hi", "lo"))
        neg_max = sb("neg_max", [P, 2, TT])
        p32 = sb("p32", [P, 2, PCOLS])
        p_hi, p_lo = (sb(f"p_{k}", [P, 2, PCOLS], F16) for k in ("hi", "lo"))
        row_sum = sb("row_sum", [P, 2, TT, NH])
        o_rows = sb("o_rows", [P, TT, D])
        oT_hi, oT_lo = (sb(f"oT_{k}", [P, DC, S], F16) for k in ("hi", "lo"))
        x1 = sb("x1", [P, TT, D])
        lg = sb("lg", [P, TT, E])
        lmax = sb("lmax", [P, TT])
        ex = sb("ex", [P, TT, E])
        exs = sb("exs", [P, TT])
        scores = sb("scores", [P, TT, E])
        biased = sb("biased", [P, TT, E])
        top = sb("top", [P, TT, 8])
        topi = sb("topi", [P, TT, 8], U32)
        onehot = sb("onehot", [P, TT, 2, E])
        picked = sb("picked", [P, TT, 2, E])
        member = sb("member", [P, TT, E], BF16)
        ranks = sb("ranks", [P, TT, E])
        tot = sb("tot", [P, TT, E])
        run = route["run"]

        bank = [ps(f"bank{i}", [P, 512]) for i in range(8)]

        w_loaded = sig("w_loaded", 16 * 7)
        w_hi = sig("w_hi", 3)
        w_lo = sig("w_lo", 3)
        bq_scaled = sig("bq_scaled", 1)
        filled = sig("filled", 3)
        stacks_filled = sig("stacks_filled", 16 * 4)
        tail_filled = sig("tail_filled", 16)
        run_cleared = sig("run_cleared", 1)
        x_loaded = sig("x_loaded", 16)
        dve_ln = sig("dve_ln", 2)
        rstd_s = sig("rstd_s", 2)
        xn_ready = sig("xn_ready", 1)
        xb_ready = sig("xb_ready", 1)
        xn_stored = sig("xn_stored", 16)
        xT_psum = sig("xT_psum", DC)
        xT_hi_s = sig("xT_hi_s", DC)
        xT_lo_s = sig("xT_lo_s", DC)
        qk_psum = sig("qk_psum", 4)
        q32_s = sig("q32_s", 2)
        qk_hi_s = sig("qk_hi_s", 4)
        q_lo_s = sig("q_lo_s", 2)
        k_lo_s = sig("k_lo_s", 2)
        qk_stored = sig("qk_stored", 32)
        stacks_loaded = sig("stacks_loaded", 96)
        v_psum = sig("v_psum", 2)
        v32_s = sig("v32_s", 2)
        v_hi_s = sig("v_hi_s", 1)
        v_lo_s = sig("v_lo_s", 1)
        lg_psum = sig("lg_psum", 1)
        lg_shifted = sig("lg_shifted", 2)
        ex_s = sig("ex_s", 1)
        rt = sig("rt", 20)
        rank_psum = sig("rank_psum", 1)
        s_psum = sig("s_psum", U * NH)
        s_max = sig("s_max", U * NH)
        p_exp = sig("p_exp", U * NH)
        pt_psum = sig("pt_psum", U * NH)
        p_hi_s = sig("p_hi_s", U * NH)
        p_lo_s = sig("p_lo_s", U * NH)
        pv_done = sig("pv_done", NH)
        o_sum = sig("o_sum", 1)
        o_ready = sig("o_ready", 2)
        oT_psum = sig("oT_psum", DC)
        oT_hi_s = sig("oT_hi_s", DC)
        oT_lo_s = sig("oT_lo_s", DC)
        proj_psum = sig("proj_psum", 2)
        x1_ready = sig("x1_ready", 2)
        x1_stored = sig("x1_stored", 16)

        def rows(t, b):
            return t[bass.ds(b * S, S), :].rearrange("(t p) d -> p t d", p=P)

        def pipeline(eng, prologue, step, epilogue):
            prologue()
            step(0, 0, False, True)
            with eng.Fori(0, NB // 2 - 1) as i:
                for u in (1, 0):
                    step(2 * i + 2 - u, u, True, True)
            step(NB - 1, 1, True, False)
            epilogue()

        def score_bank(h, n):
            return bank[(U * h + n) % 2]

        def prob_bank(h, n):
            return bank[2 + n]

        out_bank = (bank[5], bank[6])
        turn = bank[7]

        block = ctx.enter_context(nc.Block())

        @block.sync
        def _(sp):
            sp.dma_start(xr[:, :, :], rows(x, 0)).then_inc(x_loaded.sem, 16)
            sp.dma_start(wqkv32[:, :, :], w["wqkv"].rearrange("(c p) n -> p c n", p=P)).then_inc(w_loaded.sem, 16)
            sp.dma_start(gate32[:, :, :], w["gate0"].rearrange("(c p) n -> p c n", p=P)).then_inc(w_loaded.sem, 16)
            sp.dma_start(wout32[:, :, :], w["wout"].rearrange("(c p) n -> p c n", p=P)).then_inc(w_loaded.sem, 16)
            sp.dma_start(bqk[:, :], w["bqk"]).then_inc(w_loaded.sem, 16)
            sp.dma_start(bv_row[:, :], w["bv"].partition_broadcast(P)).then_inc(w_loaded.sem, 16)
            sp.dma_start(bout_row[:, :], w["bout"].partition_broadcast(P)).then_inc(w_loaded.sem, 16)
            sp.dma_start(gateb_row[:, :], w["gate_b"].partition_broadcast(P)).then_inc(w_loaded.sem, 16)

            def store_xn(b):
                sp.wait_ge(xn_ready.sem, xn_ready.at(b))
                sp.dma_start(rows(dram["xn"], b), xn[:, :, :]).then_inc(xn_stored.sem, 16)

            def store_x1(b):
                sp.wait_ge(x1_ready.sem, x1_ready.at(b))
                sp.dma_start(rows(dram["x1"], b), x1[:, :, :]).then_inc(x1_stored.sem, 16)

            def load_stacks(b, u):
                sp.wait_ge(qk_hi_s.sem, qk_hi_s.at(b))
                sp.dma_start(dram["qk_hi"].rearrange("(m p) s -> p m s", p=P), qk_hi[:, :, :]).then_inc(qk_stored.sem, 16)
                sp.wait_ge(q_lo_s.sem, q_lo_s.at(b))
                sp.wait_ge(k_lo_s.sem, k_lo_s.at(b))
                sp.dma_start(dram["qk_lo"].rearrange("(m p) s -> p m s", p=P), qk_lo[:, :, :]).then_inc(qk_stored.sem, 16)
                sp.wait_ge(qk_stored.sem, qk_stored.at(b))
                sp.wait_ge(s_psum.sem, s_psum.at(b - 2))
                hi = dram["qk_hi"].rearrange("(m h d) s -> m d h s", m=2, d=HD)
                lo = dram["qk_lo"].rearrange("(m h d) s -> m d h s", m=2, d=HD)
                for r, (q, k) in enumerate(((hi, hi), (hi, lo), (lo, hi))):
                    sp.dma_start(q_stack[HD * r:HD * r + HD, u, :, :], q[0]).then_inc(stacks_loaded.sem, 16)
                    sp.dma_start(k_stack[HD * r:HD * r + HD, u, :, :], k[1]).then_inc(stacks_loaded.sem, 16)

            def prologue():
                sp.wait_ge(filled.sem, 3)
                for u in range(2):
                    for stack in (q_stack, k_stack):
                        sp.dma_start(stack[3 * HD:STK, u, :, :],
                                     zeros16[3 * HD:STK, :].unsqueeze(1).to_broadcast([STK - 3 * HD, NH, S])).then_inc(stacks_filled.sem, 16)
                tail = dram["y"][(MAX_TILES - E) * ETOK:MAX_TILES * ETOK, :].rearrange("(p c) d -> p c d", p=P)
                sp.dma_start(tail, zeros_f[:, :].unsqueeze(1).to_broadcast([P, E * ETOK // P, D])).then_inc(tail_filled.sem, 16)
                store_xn(0)
                load_stacks(0, 0)

            def step(b, u, before, more):
                if more:
                    sp.wait_ge(xb_ready.sem, xb_ready.at(b))
                    sp.dma_start(xr[:, :, :], rows(x, b + 1)).then_inc(x_loaded.sem, 16)
                if before:
                    store_x1(b - 1)
                if more:
                    store_xn(b + 1)
                    load_stacks(b + 1, 1 - u)

            def epilogue():
                store_x1(NB - 1)
                sp.wait_ge(tail_filled.sem, tail_filled.at(0))
                sp.wait_ge(x1_stored.sem, x1_stored.at(NB - 1))
                sp.wait_ge(xn_stored.sem, xn_stored.at(NB - 1))

            pipeline(sp, prologue, step, epilogue)

        @block.gpsimd
        def _(pool):
            pool.memset(minus_half[:, :], -0.5).then_inc(filled.sem, 1)
            pool.memset(zeros16[:, :], 0.0).then_inc(filled.sem, 1)
            pool.memset(zeros_f[:, :], 0.0).then_inc(filled.sem, 1)
            pool.wait_ge(filled.sem, 3)

            def project(b, u):
                pool.wait_ge(dve_ln.sem, dve_ln.at(b))
                pool.tensor_tensor(var_eps[:, :], mv[:, :, 1], consts["eps_col"][:, 0:TT], ALU.add).then_inc(rstd_s.sem, 1)
                pool.wait_ge(rstd_s.sem, rstd_s.at(b, 1))
                pool.tensor_tensor(rstd[:, :], var_eps[:, :], minus_half[:, :], ALU.pow).then_inc(rstd_s.sem, 1)
                pool.wait_ge(x1_ready.sem, x1_ready.at(b - 2))
                pool.wait_ge(xn_ready.sem, xn_ready.at(b))
                if isinstance(b, int):
                    pool.wait_ge(w_loaded.sem, w_loaded.at(0))
                pool.tensor_tensor(xb[:, u, :, :], xr[:, :, :], bout_row[:, :].unsqueeze(1).to_broadcast([P, TT, D]),
                                   ALU.add).then_inc(xb_ready.sem, 1)
                for m in range(2):
                    pool.wait_ge(qk_hi_s.sem, qk_hi_s.at(b, m + 1))
                    pool.tensor_tensor(qk_lo[:, m, :], q32[:, m, :], qk_hi[:, m, :], ALU.subtract).then_inc(q_lo_s.sem, 1)
                pool.wait_ge(v_hi_s.sem, v_hi_s.at(b))
                pool.tensor_tensor(v_lo[:, u, :, :, :], v32[:, :, :].rearrange("p t (h d) -> p t h d", h=NH),
                                   v_hi[:, u, :, :, :], ALU.subtract).then_inc(v_lo_s.sem, 1)

            def step(b, u, before, more):
                if more:
                    project(b + 1, 1 - u)

            pipeline(pool, lambda: project(0, 0), step, lambda: None)

        @block.scalar
        def _(act):
            act.wait_ge(w_loaded.sem, w_loaded.at(0))
            act.activation(wqkv_hi[:, :, :], wqkv32[:, :, :], ACT.Copy).then_inc(w_hi.sem, 1)
            act.activation(gate_hi[:, :, :], gate32[:, :, :], ACT.Copy).then_inc(w_hi.sem, 1)
            act.activation(wout_hi[:, :, :], wout32[:, :, :], ACT.Copy).then_inc(w_hi.sem, 1)
            act.wait_ge(bq_scaled.sem, 1)

            def x_high(b, c):
                act.wait_ge(xT_psum.sem, xT_psum.at(b, c + 1))
                act.wait_ge(lg_psum.sem, lg_psum.at(b - 1))
                act.activation(xT_hi[:, c, :], turn[:, :], ACT.Copy).then_inc(xT_hi_s.sem, 1)

            def q_scaled(b, m):
                act.wait_ge(qk_psum.sem, qk_psum.at(b, m + 1))
                act.wait_ge(q_lo_s.sem, q_lo_s.at(b - 1))
                act.activation(q32[:, m, :], turn[:, :], ACT.Identity, bias=bq[:, m:m + 1],
                               scale=HD ** -0.5).then_inc(q32_s.sem, 1)

            def q_high(b, m):
                act.wait_ge(q32_s.sem, q32_s.at(b, m + 1))
                act.wait_ge(qk_stored.sem, qk_stored.at(b - 1))
                act.activation(qk_hi[:, m, :], q32[:, m, :], ACT.Copy).then_inc(qk_hi_s.sem, 1)

            def k_high(b, m):
                act.wait_ge(qk_psum.sem, qk_psum.at(b, m + 3))
                act.activation(qk_hi[:, 2 + m, :], turn[:, :], ACT.Identity, bias=bqk[:, 2 + m:3 + m]).then_inc(qk_hi_s.sem, 1)

            def v_high(b, u):
                act.wait_ge(v32_s.sem, v32_s.at(b))
                act.wait_ge(pv_done.sem, pv_done.at(b - 2))
                act.activation(v_hi[:, u, :, :, :], v32[:, :, :].rearrange("p t (h d) -> p t h d", h=NH),
                               ACT.Copy).then_inc(v_hi_s.sem, 1)

            def router_exp(b):
                act.wait_ge(lg_shifted.sem, lg_shifted.at(b))
                act.activation(ex[:, :, :], lg[:, :, :], ACT.Exp).then_inc(ex_s.sem, 1)

            def out_high(b, c):
                act.wait_ge(oT_psum.sem, oT_psum.at(b, c + 1))
                act.wait_ge(proj_psum.sem, proj_psum.at(b - 1))
                act.activation(oT_hi[:, c, :], turn[:, :], ACT.Copy).then_inc(oT_hi_s.sem, 1)

            def exps(b, u, h, n):
                act.wait_ge(s_max.sem, s_max.at(b, U * h + n + 1))
                if h == 0 and n == 0:
                    act.wait_ge(o_ready.sem, o_ready.at(b - 2))
                for j in Q_UNITS[n]:
                    at = QOFF[j] - QOFF[Q_UNITS[n][0]]
                    ins = act.activation(p32[:, h % 2, QOFF[j]:QOFF[j] + (j + 1) * P], score_bank(h, n)[:, at:at + (j + 1) * P],
                                         ACT.Exp, bias=neg_max[:, h % 2, j:j + 1], accum_out=row_sum[:, u, j, h:h + 1])
                ins.then_inc(p_exp.sem, 1)

            def prob_high(b, h, n):
                act.wait_ge(pt_psum.sem, pt_psum.at(b, U * h + n + 1))
                if n == 0:
                    act.wait_ge(pv_done.sem, pv_done.at(b, h - 1))
                first, last = K_UNITS[n][0], K_UNITS[n][-1]
                cols = slice(KOFF[first], KOFF[last] + (TT - last) * P)
                act.activation(p_hi[:, h % 2, cols], prob_bank(h, n)[:, 0:cols.stop - cols.start], ACT.Copy).then_inc(p_hi_s.sem, 1)

            def prologue():
                for c in range(DC):
                    x_high(0, c)
                for m in range(2):
                    q_scaled(0, m)
                for m in range(2):
                    q_high(0, m)
                for m in range(2):
                    k_high(0, m)
                v_high(0, 0)
                router_exp(0)
                for n in range(U):
                    exps(0, 0, 0, n)

            def pieces(b, u, h, before, more):
                if before and h in AT_OUT_T:
                    out_high(b - 1, AT_OUT_T.index(h))
                if more:
                    if h in AT_X_T:
                        x_high(b + 1, AT_X_T.index(h))
                    if h in AT_Q:
                        q_scaled(b + 1, AT_Q.index(h))
                    if h - 1 in AT_Q:
                        q_high(b + 1, AT_Q.index(h - 1))
                    if h in AT_K:
                        k_high(b + 1, AT_K.index(h))
                    if h - 1 == AT_V[1]:
                        v_high(b + 1, 1 - u)
                    if h == AT_ROUTE + 1:
                        router_exp(b + 1)

            def step(b, u, before, more):
                for h in range(NH):
                    for n in range(U):
                        if h + 1 < NH:
                            exps(b, u, h + 1, n)
                        elif more:
                            exps(b + 1, 1 - u, 0, n)
                        prob_high(b, h, n)
                        if n == 1:
                            pieces(b, u, h, before, more)

            def epilogue():
                for c in range(DC):
                    out_high(NB - 1, c)

            pipeline(act, prologue, step, epilogue)

        @block.vector
        def _(dve):
            dve.memset(run[:, 0, :], 0.0).then_inc(run_cleared.sem, 1)
            dve.wait_ge(run_cleared.sem, run_cleared.at(0))

            def norm_stats(b):
                dve.wait_ge(x_loaded.sem, x_loaded.at(b))
                for t in range(TT):
                    st = dve.bn_stats(stats[:, t, :], xr[:, t, :])
                st.then_inc(dve_ln.sem, 1)
                dve.wait_ge(rstd_s.sem, rstd_s.at(b - 1))
                dve.wait_ge(dve_ln.sem, dve_ln.at(b, 1))
                dve.nop(nofuse=True)
                for t in range(TT):
                    st = dve.bn_aggr(mv[:, t, :], stats[:, t, :])
                st.then_inc(dve_ln.sem, 1)

            def normalise(b):
                dve.wait_ge(dve_ln.sem, dve_ln.at(b))
                dve.wait_ge(rstd_s.sem, rstd_s.at(b))
                dve.wait_ge(xT_psum.sem, xT_psum.at(b - 1))
                dve.wait_ge(xn_stored.sem, xn_stored.at(b - 1))
                for t in range(TT):
                    st = dve.tensor_scalar(xn[:, t, :], xr[:, t, :], mv[:, t, 0:1], rstd[:, t:t + 1],
                                           ALU.subtract, ALU.mult)
                st.then_inc(xn_ready.sem, 1)

            def x_low(b, c):
                dve.wait_ge(xT_hi_s.sem, xT_hi_s.at(b, c + 1))
                dve.tensor_tensor(xT_lo[:, c, :], turn[:, :], xT_hi[:, c, :], ALU.subtract).then_inc(xT_lo_s.sem, 1)

            def k_low(b, m):
                dve.wait_ge(qk_hi_s.sem, qk_hi_s.at(b, m + 3))
                dve.scalar_tensor_tensor(qk_lo[:, 2 + m, :], turn[:, :], bqk[:, 2 + m:3 + m], qk_hi[:, 2 + m, :],
                                         ALU.add, ALU.subtract).then_inc(k_lo_s.sem, 1)

            def v_bias(b, g):
                dve.wait_ge(v_lo_s.sem, v_lo_s.at(b - 1))
                dve.wait_ge(v_psum.sem, v_psum.at(b, g + 1))
                dve.tensor_tensor(v32[:, 2 * g:2 * g + 2, :], turn[:, :].rearrange("p (t n) -> p t n", t=2),
                                  bv_row[:, :].unsqueeze(1).to_broadcast([P, 2, D]), ALU.add).then_inc(v32_s.sem, 1)

            def done(b, n, ins):
                ins.then_inc(rt.sem, 1)
                dve.wait_ge(rt.sem, rt.at(b, n))

            def router_shift(b):
                dve.wait_ge(lg_psum.sem, lg_psum.at(b))
                lgp = turn[:, 0:TT * E].rearrange("p (t e) -> p t e", e=E)
                dve.tensor_reduce(lmax[:, :], lgp, AX.X, ALU.max).then_inc(lg_shifted.sem, 1)
                dve.wait_ge(lg_shifted.sem, lg_shifted.at(b, 1))
                dve.tensor_tensor(lg[:, :, :], lgp, lmax[:, :].unsqueeze(2).to_broadcast([P, TT, E]),
                                  ALU.subtract).then_inc(lg_shifted.sem, 1)

            def router_choice(b):
                dve.wait_ge(ex_s.sem, ex_s.at(b))
                done(b, 1, dve.tensor_reduce(exs[:, :], ex[:, :, :], AX.X, ALU.add))
                done(b, 2, dve.reciprocal(exs[:, :], exs[:, :]))
                done(b, 3, dve.tensor_tensor(scores[:, :, :], ex[:, :, :], exs[:, :].unsqueeze(2).to_broadcast([P, TT, E]), ALU.mult))
                done(b, 4, dve.tensor_tensor(biased[:, :, :], scores[:, :, :],
                                             gateb_row[:, :].unsqueeze(1).to_broadcast([P, TT, E]), ALU.add))
                dve.nop(nofuse=True)
                for t in range(TT):
                    mx = dve.max(top[:, t, :], biased[:, t, :])
                done(b, 5, mx)
                dve.nop(nofuse=True)
                for t in range(TT):
                    mx = dve.max_index(topi[:, t, :], top[:, t, :], biased[:, t, :])
                done(b, 6, mx)
                for k in range(2):
                    oh = dve.tensor_tensor(onehot[:, :, k, :], iota8[:, :].unsqueeze(1).to_broadcast([P, TT, E]),
                                           topi[:, :, k:k + 1].to_broadcast([P, TT, E]), ALU.is_equal)
                done(b, 7, oh)
                done(b, 8, dve.tensor_tensor(member[:, :, :], onehot[:, :, 0, :], onehot[:, :, 1, :], ALU.add))

            def router_ranks(b):
                for k in range(2):
                    oh = dve.tensor_tensor(picked[:, :, k, :], onehot[:, :, k, :], scores[:, :, :], ALU.mult)
                done(b, 9, oh)
                done(b, 10, dve.tensor_reduce(route["weights"][:, bass.ds(b * TT, TT), :], picked[:, :, :, :], AX.X, ALU.add))
                dve.wait_ge(rank_psum.sem, rank_psum.at(b))
                done(b, 11, dve.tensor_copy(tot[:, :, :], turn[:, 64:64 + TT * E].rearrange("p (t e) -> p t e", e=E)))
                for t in range(TT):
                    done(b, 12 + t, dve.tensor_tensor(run[:, t + 1, :], run[:, t, :], tot[:, t, :], ALU.add))
                done(b, 16, dve.tensor_tensor(ranks[:, :, :], turn[:, 32:32 + TT * E].rearrange("p (t e) -> p t e", e=E),
                                              run[:, 0:TT, :], ALU.add))
                for k in range(2):
                    oh = dve.tensor_tensor(picked[:, :, k, :], onehot[:, :, k, :], ranks[:, :, :], ALU.mult)
                done(b, 17, oh)
                done(b, 18, dve.tensor_reduce(route["rank"][:, bass.ds(b * TT, TT), :], picked[:, :, :, :], AX.X, ALU.add))
                done(b, 19, dve.tensor_copy(route["onehot"][:, bass.ds(b * TT, TT), :, :], onehot[:, :, :, :]))
                done(b, 20, dve.tensor_copy(run[:, 0, :], run[:, TT, :]))

            def divide(b, u):
                dve.wait_ge(pv_done.sem, pv_done.at(b))
                dve.wait_ge(oT_psum.sem, oT_psum.at(b - 1))
                dve.reciprocal(row_sum[:, u, :, :], row_sum[:, u, :, :]).then_inc(o_sum.sem, 1)
                dve.wait_ge(o_sum.sem, o_sum.at(b))
                for g in range(2):
                    dve.tensor_tensor(o_rows[:, 2 * g:2 * g + 2, :].rearrange("p t (h d) -> p (t h) d", h=NH),
                                      out_bank[g][:, :].rearrange("p (t d) -> p t d", d=HD),
                                      row_sum[:, u, 2 * g:2 * g + 2, :].rearrange("p t h -> p (t h)").unsqueeze(2).to_broadcast([P, 2 * NH, HD]),
                                      ALU.mult).then_inc(o_ready.sem, 1)

            def out_low(b, c):
                dve.wait_ge(oT_hi_s.sem, oT_hi_s.at(b, c + 1))
                dve.tensor_tensor(oT_lo[:, c, :], turn[:, :], oT_hi[:, c, :], ALU.subtract).then_inc(oT_lo_s.sem, 1)

            def residual(b, u, g):
                dve.wait_ge(x1_stored.sem, x1_stored.at(b - 1))
                dve.wait_ge(proj_psum.sem, proj_psum.at(b, g + 1))
                dve.tensor_tensor(x1[:, 2 * g:2 * g + 2, :], turn[:, :].rearrange("p (t n) -> p t n", t=2),
                                  xb[:, u, 2 * g:2 * g + 2, :], ALU.add).then_inc(x1_ready.sem, 1)

            def maxima(b, h, n):
                dve.wait_ge(s_psum.sem, s_psum.at(b, U * h + n + 1))
                for j in Q_UNITS[n]:
                    at = QOFF[j] - QOFF[Q_UNITS[n][0]]
                    ins = dve.tensor_reduce(neg_max[:, h % 2, j:j + 1], score_bank(h, n)[:, at:at + (j + 1) * P], AX.X,
                                            ALU.max, negate=True)
                ins.then_inc(s_max.sem, 1)

            def prob_low(b, h, n):
                dve.wait_ge(p_hi_s.sem, p_hi_s.at(b, U * h + n + 1))
                first, last = K_UNITS[n][0], K_UNITS[n][-1]
                cols = slice(KOFF[first], KOFF[last] + (TT - last) * P)
                dve.tensor_tensor(p_lo[:, h % 2, cols], prob_bank(h, n)[:, 0:cols.stop - cols.start], p_hi[:, h % 2, cols],
                                  ALU.subtract).then_inc(p_lo_s.sem, 1)

            def prologue():
                norm_stats(0)
                normalise(0)
                dve.wait_ge(w_loaded.sem, w_loaded.at(0))
                dve.tensor_scalar(bq[:, :], bqk[:, 0:2], HD ** -0.5, None, ALU.mult).then_inc(bq_scaled.sem, 1)
                dve.wait_ge(w_hi.sem, 1)
                dve.tensor_tensor(wqkv_lo[:, :, :], wqkv32[:, :, :], wqkv_hi[:, :, :], ALU.subtract).then_inc(w_lo.sem, 1)
                dve.wait_ge(w_hi.sem, 2)
                dve.tensor_tensor(gate_lo[:, :, :], gate32[:, :, :], gate_hi[:, :, :], ALU.subtract).then_inc(w_lo.sem, 1)
                dve.wait_ge(w_hi.sem, 3)
                dve.tensor_tensor(wout_lo[:, :, :], wout32[:, :, :], wout_hi[:, :, :], ALU.subtract).then_inc(w_lo.sem, 1)
                for c in range(DC):
                    x_low(0, c)
                for m in range(2):
                    k_low(0, m)
                for g in range(2):
                    v_bias(0, g)
                router_shift(0)
                for n in range(U):
                    maxima(0, 0, n)

            def step(b, u, before, more):
                for h in range(NH):
                    for n in range(U):
                        if h + 1 < NH or more:
                            maxima(b, h + 1, n)
                        if n >= LAG:
                            prob_low(b, h, n - LAG)
                        elif h >= 1 or before:
                            prob_low(b, h - 1, n - LAG + U)
                    if h == AT_DIVIDE and before:
                        divide(b - 1, 1 - u)
                    if h == AT_CHOICE:
                        router_choice(b)
                    if h == AT_RANKS:
                        router_ranks(b)
                    if before:
                        if h in AT_OUT_T:
                            out_low(b - 1, AT_OUT_T.index(h))
                        if h in AT_PROJ:
                            residual(b - 1, 1 - u, AT_PROJ.index(h))
                    if more:
                        if h == AT_NORM:
                            norm_stats(b + 1)
                        if h == AT_NORM + 1:
                            normalise(b + 1)
                        if h in AT_X_T:
                            x_low(b + 1, AT_X_T.index(h))
                        if h in AT_K:
                            k_low(b + 1, AT_K.index(h))
                        if h in AT_V:
                            v_bias(b + 1, AT_V.index(h))
                        if h == AT_ROUTE:
                            router_shift(b + 1)

            def epilogue():
                for n in range(U - LAG, U):
                    prob_low(NB - 1, NH - 1, n)
                divide(NB - 1, 1)
                for c in range(DC):
                    out_low(NB - 1, c)
                for g in range(2):
                    residual(NB - 1, 1, g)

            pipeline(dve, prologue, step, epilogue)

        @block.tensor
        def _(pe):
            def x_transposes(b, c):
                if c == 0:
                    pe.wait_ge(xn_ready.sem, xn_ready.at(b))
                    pe.wait_ge(rt.sem, rt.at(b - 1))
                    pe.wait_ge(x1_ready.sem, x1_ready.at(b - 2))
                else:
                    pe.wait_ge(xT_lo_s.sem, xT_lo_s.at(b, 1))
                for t in range(TT):
                    mm = pe.transpose(turn[:, t * P:(t + 1) * P], xn[:, t, c * P:(c + 1) * P], identf[:, :])
                mm.then_inc(xT_psum.sem, 1)

            def qk_products(b, m):
                if m == 0:
                    pe.wait_ge(xT_lo_s.sem, xT_lo_s.at(b))
                elif m <= 2:
                    pe.wait_ge(q32_s.sem, q32_s.at(b, m))
                else:
                    pe.wait_ge(k_lo_s.sem, k_lo_s.at(b, 1))
                cols = slice(m * P, (m + 1) * P)
                three_products(pe, turn[:, :], lambda c: wqkv_hi[:, c, cols], lambda c: wqkv_lo[:, c, cols],
                               lambda c: xT_hi[:, c, :], lambda c: xT_lo[:, c, :], range(DC)).then_inc(qk_psum.sem, 1)

            def v_products(b, g):
                if g == 0:
                    pe.wait_ge(k_lo_s.sem, k_lo_s.at(b))
                else:
                    pe.wait_ge(v32_s.sem, v32_s.at(b, 1))
                for t in (2 * g, 2 * g + 1):
                    tok = slice(t * P, (t + 1) * P)
                    mm = three_products(pe, turn[:, (t % 2) * D:(t % 2 + 1) * D],
                                        lambda c: xT_hi[:, c, tok], lambda c: xT_lo[:, c, tok],
                                        lambda c: wqkv_hi[:, c, 2 * D:3 * D], lambda c: wqkv_lo[:, c, 2 * D:3 * D], range(DC))
                mm.then_inc(v_psum.sem, 1)

            def logits(b):
                pe.wait_ge(v32_s.sem, v32_s.at(b))
                for t in range(TT):
                    tok = slice(t * P, (t + 1) * P)
                    mm = three_products(pe, turn[:, t * E:(t + 1) * E], lambda c: xT_hi[:, c, tok], lambda c: xT_lo[:, c, tok],
                                        lambda c: gate_hi[:, c, :], lambda c: gate_lo[:, c, :], range(DC))
                mm.then_inc(lg_psum.sem, 1)

            def rank_sums(b):
                pe.wait_ge(rt.sem, rt.at(b, 8))
                m = member[:, :, :].rearrange("p t e -> p (t e)")
                pe.matmul(turn[:, 32:32 + TT * E], tri[:, :], m, start=True, stop=True)
                pe.matmul(turn[:, 64:64 + TT * E], ones_b[:, :], m, start=True, stop=True).then_inc(rank_psum.sem, 1)

            def scores_of(b, u, h, n):
                if h == 0 and n == 0:
                    pe.wait_ge(stacks_loaded.sem, stacks_loaded.at(b))
                if not (h == 0 and n < 2 and isinstance(b, int) and b == 0):
                    pe.wait_ge(p_exp.sem, p_exp.at(b, U * h + n - 1))
                for j in Q_UNITS[n]:
                    at = QOFF[j] - QOFF[Q_UNITS[n][0]]
                    pe.matmul(score_bank(h, n)[:, at:at + (j + 1) * P], q_stack[0:STK, u, h, j * P:(j + 1) * P],
                              k_stack[0:STK, u, h, 0:(j + 1) * P], start=True, stop=False)
                    mm = pe.matmul(score_bank(h, n)[:, at + j * P:at + (j + 1) * P], identb[:, :], maskadd[:, :],
                                   start=False, stop=True)
                mm.then_inc(s_psum.sem, 1)

            def prob_transposes(b, h, n):
                if n == 0:
                    pe.wait_ge(p_exp.sem, p_exp.at(b, U * h + U))
                if not (h == 0 and isinstance(b, int) and b == 0):
                    pe.wait_ge(p_lo_s.sem, p_lo_s.at(b, U * h + n - 2))
                for k in K_UNITS[n]:
                    for j in range(k, TT):
                        at = KOFF[k] - KOFF[K_UNITS[n][0]] + (j - k) * P
                        mm = pe.transpose(prob_bank(h, n)[:, at:at + P], p32[:, h % 2, QOFF[j] + k * P:QOFF[j] + (k + 1) * P],
                                          identf[:, :])
                mm.then_inc(pt_psum.sem, 1)

            def values(b, u, h, before):
                if h == 0:
                    pe.wait_ge(v_lo_s.sem, v_lo_s.at(b))
                    if before:
                        pe.wait_ge(o_ready.sem, o_ready.at(b - 1))
                pe.wait_ge(p_lo_s.sem, p_lo_s.at(b, U * h + U))
                for j in range(TT):
                    out = out_bank[j // 2][:, (j % 2) * D + h * HD:(j % 2) * D + (h + 1) * HD]
                    for k in range(j + 1):
                        cols = slice(KOFF[k] + (j - k) * P, KOFF[k] + (j - k + 1) * P)
                        pe.matmul(out, p_hi[:, h % 2, cols], v_hi[:, u, k, h, :], start=k == 0, stop=False)
                        pe.matmul(out, p_hi[:, h % 2, cols], v_lo[:, u, k, h, :], start=False, stop=False)
                        mm = pe.matmul(out, p_lo[:, h % 2, cols], v_hi[:, u, k, h, :], start=False, stop=k == j)
                mm.then_inc(pv_done.sem, 1)

            def out_transposes(b, c):
                if c == 0:
                    pe.wait_ge(o_ready.sem, o_ready.at(b))
                else:
                    pe.wait_ge(oT_lo_s.sem, oT_lo_s.at(b, 1))
                for t in range(TT):
                    mm = pe.transpose(turn[:, t * P:(t + 1) * P], o_rows[:, t, c * P:(c + 1) * P], identf[:, :])
                mm.then_inc(oT_psum.sem, 1)

            def out_products(b, g):
                if g == 0:
                    pe.wait_ge(oT_lo_s.sem, oT_lo_s.at(b))
                else:
                    pe.wait_ge(x1_ready.sem, x1_ready.at(b, 1))
                for t in (2 * g, 2 * g + 1):
                    tok = slice(t * P, (t + 1) * P)
                    mm = three_products(pe, turn[:, (t % 2) * D:(t % 2 + 1) * D],
                                        lambda c: oT_hi[:, c, tok], lambda c: oT_lo[:, c, tok],
                                        lambda c: wout_hi[:, c, :], lambda c: wout_lo[:, c, :], range(DC))
                mm.then_inc(proj_psum.sem, 1)

            def prologue():
                for c in range(DC):
                    x_transposes(0, c)
                pe.wait_ge(w_lo.sem, 3)
                for m in range(4):
                    qk_products(0, m)
                for g in range(2):
                    v_products(0, g)
                logits(0)
                pe.wait_ge(stacks_filled.sem, stacks_filled.at(0))
                for n in range(U):
                    scores_of(0, 0, 0, n)

            def pieces(b, u, h, before, more):
                if h == AT_RANKS:
                    rank_sums(b)
                if before:
                    if h == AT_OUT_T[0]:
                        pe.wait_ge(rt.sem, rt.at(b))
                    if h in AT_OUT_T:
                        out_transposes(b - 1, AT_OUT_T.index(h))
                    if h in AT_PROJ:
                        out_products(b - 1, AT_PROJ.index(h))
                if more:
                    if h in AT_X_T:
                        x_transposes(b + 1, AT_X_T.index(h))
                    if h in AT_Q + AT_K:
                        qk_products(b + 1, (AT_Q + AT_K).index(h))
                    if h in AT_V:
                        v_products(b + 1, AT_V.index(h))
                    if h == AT_ROUTE:
                        logits(b + 1)

            def step(b, u, before, more):
                for h in range(NH):
                    for n in range(U):
                        if h + 1 < NH:
                            scores_of(b, u, h + 1, n)
                        elif more:
                            scores_of(b + 1, 1 - u, 0, n)
                        prob_transposes(b, h, n)
                        if n == 0:
                            pieces(b, u, h, before, more)
                        elif n == 1 and h >= 1:
                            values(b, u, h - 1, before)
                        elif n == 1 and before:
                            values(b - 1, 1 - u, NH - 1, True)

            def epilogue():
                values(NB - 1, 1, NH - 1, True)
                for c in range(DC):
                    out_transposes(NB - 1, c)
                for g in range(2):
                    out_products(NB - 1, g)

            pipeline(pe, prologue, step, epilogue)


def constants(nc, ctx):
    def sb(name, shape, dt=F32):
        return ctx.enter_context(nc.sbuf_tensor(name, shape, dt))

    c = {"identf": sb("identf", [P, P]), "identb": sb("identb", [P, P], BF16), "ones_b": sb("ones_b", [P, P], BF16),
         "tri": sb("tri", [P, P], BF16), "maskadd": sb("maskadd", [P, P], BF16), "iota8": sb("iota8", [P, E]),
         "eps_col": sb("eps_col", [P, TT]), "zero_i": sb("zero_i", [P, 2], I32)}
    with ExitStack() as own:
        start = own.enter_context(nc.semaphore("const_start"))
        made = own.enter_context(nc.semaphore("const_made"))
        zeros = own.enter_context(nc.sbuf_tensor("zeros", [P, P], F32))
        onesf = own.enter_context(nc.sbuf_tensor("onesf", [P, P], F32))
        block = own.enter_context(nc.Block())

        @block.gpsimd
        def _(pool):
            pool.memset(zeros[:, :], 0.0).then_inc(start, 1)
            pool.memset(onesf[:, :], 1.0).then_inc(start, 1)
            pool.memset(c["ones_b"][:, :], 1.0).then_inc(made, 1)
            pool.memset(c["eps_col"][:, :], EPS).then_inc(made, 1)
            pool.memset(c["zero_i"][:, :], 0).then_inc(made, 1)
            pool.iota(c["iota8"][:, :], [[1, E]], base=0, channel_multiplier=0,
                      allow_small_or_imprecise_dtypes=True).then_inc(made, 1)
            pool.wait_ge(start, 2)
            for name in ("identf", "identb"):
                pool.affine_select(out=c[name][:, :], in_=zeros[:, :], pattern=[[-1, P]], compare_op=ALU.not_equal,
                                   fill=1.0, base=0, channel_multiplier=1).then_inc(made, 1)
            pool.affine_select(out=c["tri"][:, :], in_=onesf[:, :], pattern=[[1, P]], compare_op=ALU.is_gt,
                               fill=0.0, base=0, channel_multiplier=-1).then_inc(made, 1)
            pool.affine_select(out=c["maskadd"][:, :], in_=zeros[:, :], pattern=[[-1, P]], compare_op=ALU.is_ge,
                               fill=MASKED, base=0, channel_multiplier=1).then_inc(made, 1)
            pool.wait_ge(made, 8)
    return c


def slots_phase(nc, route):
    run, bounds, pos, tokens = route["run"], route["bounds"], route["pos"], route["tokens"]
    with ExitStack() as ctx:
        def sb(name, shape, dt=F32):
            return ctx.enter_context(nc.sbuf_tensor(name, shape, dt))

        tiles_i = sb("tiles_i", [P, E], I32)
        tiles = sb("tiles", [P, E])
        ones8 = sb("ones8", [P, E])
        ends = sb("ends", [P, E])
        starts = sb("starts", [P, E])
        base = sb("base", [P, T // P, 2, E])
        posf = sb("posf", [P, T // P, 2])
        zeros_i = sb("zeros_i", [P, ROUTED_SLOTS // P], I32)
        chain = Signal(nc, ctx, "slot_chain", 10)
        made = Signal(nc, ctx, "slot_made", 4)
        zeroed = Signal(nc, ctx, "table_zeroed", 16)
        block = ctx.enter_context(nc.Block())

        @block.gpsimd
        def _(pool):
            pool.iota(tokens[:, 0:T // P], [[P, T // P]], base=0, channel_multiplier=1).then_inc(made.sem, 1)
            pool.iota(route["ids"][:, :], [[P, T // P]], base=0, channel_multiplier=1).then_inc(made.sem, 1)
            pool.memset(zeros_i[:, :], 0).then_inc(made.sem, 1)
            pool.memset(ones8[:, :], 1.0).then_inc(made.sem, 1)
            pool.wait_ge(made.sem, 4)

        @block.sync
        def _(sp):
            sp.wait_ge(made.sem, 4)
            sp.dma_start(route["table"].rearrange("(p c) o -> p (c o)", p=P), zeros_i[:, :]).then_inc(zeroed.sem, 16)
            sp.wait_ge(zeroed.sem, 16)

        @block.vector
        def _(dve):
            at = [0]

            def done(ins):
                ins.then_inc(chain.sem, 1)
                at[0] += 1
                dve.wait_ge(chain.sem, at[0])

            dve.wait_ge(made.sem, 4)
            done(dve.tensor_scalar(tiles_i[:, :], run[:, 0, :], 1.0 / ETOK, (ETOK - 1.0) / ETOK - 0.499, ALU.mult, ALU.add))
            done(dve.tensor_scalar(tiles[:, :], tiles_i[:, :], 1.0, None, ALU.max))
            done(dve.tensor_tensor_scan(ends[:, :], ones8[:, :], tiles[:, :], float(SHARED_TILES), ALU.mult, ALU.add))
            done(dve.tensor_tensor(starts[:, :], ends[:, :], tiles[:, :], ALU.subtract))
            done(dve.tensor_copy(bounds[:, 0:E], starts[:, :]))
            done(dve.tensor_copy(bounds[:, E:E + 1], ends[:, E - 1:E]))
            done(dve.tensor_scalar(starts[:, :], starts[:, :], float(SHARED_TILES), float(ETOK), ALU.subtract, ALU.mult))
            done(dve.tensor_tensor(base[:, :, :, :].rearrange("p t k e -> p (t k) e"),
                                   route["onehot"][:, :, :, :].rearrange("p t k e -> p (t k) e"),
                                   starts[:, :].unsqueeze(1).to_broadcast([P, 2 * T // P, E]), ALU.mult))
            done(dve.tensor_reduce(posf[:, :, :], base[:, :, :, :], AX.X, ALU.add))
            dve.tensor_tensor(pos[:, :, :], posf[:, :, :], route["rank"][:, :, :], ALU.add).then_inc(chain.sem, 1)
            dve.wait_ge(chain.sem, 10)


def experts_phase(nc, w, dram, consts, route):
    identf, bounds, pos, tokens = consts["identf"], route["bounds"], route["pos"], route["tokens"]
    HM = len(HT)
    HALF = ETOK // P
    with ExitStack() as ctx:
        def sb(name, shape, dt=F32):
            return ctx.enter_context(nc.sbuf_tensor(name, shape, dt))

        def sig(name, per):
            return Signal(nc, ctx, name, per)

        w13_32 = sb("w13_32", [P, DC, 2 * H0])
        w2_32 = sb("w2_32", [P, HM, D])
        w13_hi, w13_lo = (sb(f"w13_{k}", [P, 2, DC, 2 * H0], F16) for k in ("hi", "lo"))
        w2_hi, w2_lo = (sb(f"w2_{k}", [P, 2, HM, D], F16) for k in ("hi", "lo"))
        b13 = sb("b13", [P, 2, 2 * HM])
        b2 = sb("b2", [P, 2, D])
        token_now = sb("token_now", [P, HALF], I32)
        xg = sb("xg", [P, HALF, D])
        xT_hi, xT_lo = (sb(f"gT_{k}", [P, DC, ETOK], F16) for k in ("hi", "lo"))
        a1 = sb("a1", [P, HM, ETOK])
        prod = sb("prod", [P, HM, ETOK])
        h32 = sb("h32", [P, HM, ETOK])
        h_hi, h_lo = (sb(f"h_{k}", [P, HM, ETOK], F16) for k in ("hi", "lo"))
        y = sb("y", [P, HALF, D])
        table_rows = sb("table_rows", [ROUTED_SLOTS // P, P], I32)
        table_f = sb("table_f", [ROUTED_SLOTS // P, P])
        bank = [ctx.enter_context(nc.psum_tensor(f"xbank{i}", [P, 512], F32)) for i in range(6)]

        e_loaded = sig("e_loaded", 16 * 5)
        e_hi = sig("e_hi", 3)
        e_lo = sig("e_lo", 3)
        token_now_s = sig("token_now_s", 1)
        gathered = sig("gathered", 16 * HALF)
        gT_psum = sig("gT_psum", 1)
        gT_hi_s = sig("gT_hi_s", 1)
        gT_lo_s = sig("gT_lo_s", 1)
        gu_psum = sig("gu_psum", HM)
        a1_s = sig("a1_s", HM)
        prod_s = sig("prod_s", HM)
        h32_s = sig("h32_s", HM)
        h_hi_s = sig("h_hi_s", HM)
        h_lo_s = sig("h_lo_s", HM)
        y_psum = sig("y_psum", 1)
        y_ready = sig("y_ready", 1)
        y_stored = sig("y_stored", 16)
        scattered = sig("scattered", 16 * 2 * T // P)
        table_loaded = sig("table_loaded", 16)
        table_f_s = sig("table_f_s", 1)
        table_psum = sig("table_psum", 1)
        tokens_s = sig("tokens_s", 1)

        def over_experts(eng, prologue, new_expert, tile, table):
            prologue()
            new_expert(0, 0, 0)
            tile(0, 0)
            with eng.Fori(1, SHARED_TILES - 1) as i:
                tile(i, 0)
            table()
            tile(SHARED_TILES - 1, 0)
            with eng.Fori(0, E // 2) as half:
                for k in range(2):
                    first = eng.value_load(bounds[0:1, bass.ds(2 * half + k, 1)], min_val=SHARED_TILES, max_val=MAX_TILES)
                    end = eng.value_load(bounds[0:1, bass.ds(2 * half + k + 1, 1)], min_val=SHARED_TILES + 1, max_val=MAX_TILES)
                    new_expert(2 * half + k + 1, 1 - k, first)
                    with eng.Fori(first, end) as i:
                        tile(i, 1 - k)

        block = ctx.enter_context(nc.Block())

        @block.sync
        def _(sp):
            def load_expert(e, u, first):
                sp.wait_ge(e_hi.sem, e_hi.at(e, 0))
                sp.wait_ge(e_lo.sem, e_lo.at(e, 0))
                sp.wait_ge(y_ready.sem, y_ready.at(first, 0))
                d = e if isinstance(e, int) else bass.ds(e, 1)
                row = (lambda t: t[e]) if isinstance(e, int) else (lambda t: t[bass.ds(e, 1)].rearrange("a m n -> (a m) n"))
                sp.dma_start(w13_32[:, :, :], row(w["w13"]).rearrange("(c p) n -> p c n", p=P)).then_inc(e_loaded.sem, 16)
                sp.dma_start(w2_32[:, 0:2, :], row(w["w2"])[0:2 * P, :].rearrange("(m p) n -> p m n", p=P)).then_inc(e_loaded.sem, 16)
                sp.dma_start(w2_32[0:HT[2][1], 2, :], row(w["w2"])[2 * P:H0, :]).then_inc(e_loaded.sem, 16)
                sp.dma_start(b13[:, u, :], row(w["b13"])).then_inc(e_loaded.sem, 16)
                sp.dma_start(b2[:, u, :], row(w["b2"])[0].partition_broadcast(P)).then_inc(e_loaded.sem, 16)

            def new_expert(e, u, first):
                load_expert(e + 1, 1 - u, first)

            def tile(i, u):
                sp.wait_ge(y_ready.sem, y_ready.at(i))
                sp.dma_start(dram["y"][bass.ds(i * ETOK, ETOK), :].rearrange("(t p) d -> p t d", p=P),
                             y[:, :, :]).then_inc(y_stored.sem, 16)

            def table():
                sp.wait_ge(scattered.sem, scattered.at(0))
                sp.dma_start(table_rows[:, :], route["table"].rearrange("(c p) o -> c (p o)", p=P)).then_inc(table_loaded.sem, 16)

            over_experts(sp, lambda: load_expert(0, 0, 0), new_expert, tile, table)
            last = sp.value_load(bounds[0:1, E:E + 1], min_val=SHARED_TILES + 1, max_val=MAX_TILES)
            sp.wait_ge(y_stored.sem, y_stored.at(last, 0))
            sp.nop(nofuse=True)

        @block.gpsimd
        def _(pool):
            def gather(i):
                pool.wait_ge(gT_psum.sem, gT_psum.at(i, 0))
                pool.wait_ge(token_now_s.sem, token_now_s.at(i))
                pool.nop(nofuse=True)
                for half in range(HALF):
                    pool.indirect_dma_start(xg[:, half, :], None, dram["xn"],
                                            bass.IndirectOffsetOnAxis(token_now[:, half:half + 1], 0)).then_inc(gathered.sem, 16)

            gather(0)
            columns = [(t, k) for t in range(T // P) for k in range(2)]
            share = -(-len(columns) // (SHARED_TILES - 1))
            for i in range(SHARED_TILES - 1):
                gather(i + 1)
                for t, k in columns[i * share:(i + 1) * share]:
                    pool.indirect_dma_start(route["table"], bass.IndirectOffsetOnAxis(pos[:, t, k:k + 1], 0),
                                            route["ids"][:, t:t + 1], None).then_inc(scattered.sem, 16)
            gather(SHARED_TILES)
            end = pool.value_load(bounds[0:1, E:E + 1], min_val=SHARED_TILES + 1, max_val=MAX_TILES)
            with pool.Fori(SHARED_TILES, end) as i:
                gather(i + 1)

        @block.scalar
        def _(act):
            def split(e, u, first):
                act.wait_ge(e_loaded.sem, e_loaded.at(e))
                act.wait_ge(y_psum.sem, y_psum.at(first, 0))
                act.activation(w13_hi[:, u, :, :], w13_32[:, :, :], ACT.Copy).then_inc(e_hi.sem, 1)
                act.activation(w2_hi[:, u, 0:2, :], w2_32[:, 0:2, :], ACT.Copy).then_inc(e_hi.sem, 1)
                act.activation(w2_hi[0:HT[2][1], u, 2, :], w2_32[0:HT[2][1], 2, :], ACT.Copy).then_inc(e_hi.sem, 1)

            def x_part(i):
                act.wait_ge(gT_psum.sem, gT_psum.at(i))
                act.wait_ge(gu_psum.sem, gu_psum.at(i, 0))
                act.activation(xT_hi[:, :, :], bank[3][:, :].rearrange("p (c t) -> p c t", c=DC), ACT.Copy).then_inc(gT_hi_s.sem, 1)

            def bias1(i, u, m):
                M = HT[m][1]
                act.wait_ge(gu_psum.sem, gu_psum.at(i, m + 1))
                act.activation(a1[0:M, m, :], bank[m][0:M, 0:ETOK], ACT.Identity, bias=b13[0:M, u, m:m + 1]).then_inc(a1_s.sem, 1)

            def hidden(i, m):
                M = HT[m][1]
                act.wait_ge(prod_s.sem, prod_s.at(i, m + 1))
                act.wait_ge(y_psum.sem, y_psum.at(i, 0))
                act.activation(h32[0:M, m, :], prod[0:M, m, :], ACT.Silu).then_inc(h32_s.sem, 1)
                act.wait_ge(h32_s.sem, h32_s.at(i, m + 1))
                act.activation(h_hi[0:M, m, :], h32[0:M, m, :], ACT.Copy).then_inc(h_hi_s.sem, 1)

            def tile(i, u):
                bias1(i, u, 0)
                bias1(i, u, 1)
                hidden(i, 0)
                bias1(i, u, 2)
                hidden(i, 1)
                hidden(i, 2)
                x_part(i + 1)

            def prologue():
                split(0, 0, 0)
                x_part(0)

            over_experts(act, prologue, lambda e, u, first: split(e + 1, 1 - u, first), tile, lambda: None)

        @block.vector
        def _(dve):
            def split(e, u, first):
                dve.wait_ge(y_psum.sem, y_psum.at(first, 0))
                for n, (lo, a32, hi) in enumerate((
                        (w13_lo[:, u, :, :], w13_32[:, :, :], w13_hi[:, u, :, :]),
                        (w2_lo[:, u, 0:2, :], w2_32[:, 0:2, :], w2_hi[:, u, 0:2, :]),
                        (w2_lo[0:HT[2][1], u, 2, :], w2_32[0:HT[2][1], 2, :], w2_hi[0:HT[2][1], u, 2, :]))):
                    dve.wait_ge(e_hi.sem, e_hi.at(e, n + 1))
                    dve.tensor_tensor(lo, a32, hi, ALU.subtract).then_inc(e_lo.sem, 1)

            def name_tokens(i):
                dve.wait_ge(gathered.sem, gathered.at(i, 0))
                dve.nop(nofuse=True)
                dve.tensor_copy(token_now[:, :], tokens[:, bass.ds(i * HALF, HALF)]).then_inc(token_now_s.sem, 1)

            def x_part(i):
                dve.wait_ge(gT_hi_s.sem, gT_hi_s.at(i))
                dve.tensor_tensor(xT_lo[:, :, :], bank[3][:, :].rearrange("p (c t) -> p c t", c=DC), xT_hi[:, :, :],
                                  ALU.subtract).then_inc(gT_lo_s.sem, 1)

            def gated(i, u, m):
                M = HT[m][1]
                dve.wait_ge(a1_s.sem, a1_s.at(i, m + 1))
                dve.wait_ge(h32_s.sem, h32_s.at(i, 0))
                dve.scalar_tensor_tensor(prod[0:M, m, :], bank[m][0:M, ETOK:2 * ETOK], b13[0:M, u, HM + m:HM + m + 1],
                                         a1[0:M, m, :], ALU.add, ALU.mult).then_inc(prod_s.sem, 1)

            def hidden_lo(i, m):
                M = HT[m][1]
                dve.wait_ge(h_hi_s.sem, h_hi_s.at(i, m + 1))
                dve.tensor_tensor(h_lo[0:M, m, :], h32[0:M, m, :], h_hi[0:M, m, :], ALU.subtract).then_inc(h_lo_s.sem, 1)

            def tile(i, u):
                name_tokens(i + 1)
                gated(i, u, 0)
                gated(i, u, 1)
                hidden_lo(i, 0)
                gated(i, u, 2)
                hidden_lo(i, 1)
                hidden_lo(i, 2)
                x_part(i + 1)
                dve.wait_ge(y_psum.sem, y_psum.at(i))
                dve.wait_ge(y_stored.sem, y_stored.at(i, 0))
                for half in range(HALF):
                    ins = dve.tensor_tensor(y[:, half, :], bank[4 + half][:, 0:D], b2[:, u, :], ALU.add)
                ins.then_inc(y_ready.sem, 1)

            def prologue():
                name_tokens(0)
                split(0, 0, 0)
                x_part(0)

            def table():
                n = ROUTED_SLOTS // P
                dve.wait_ge(table_loaded.sem, 16)
                dve.tensor_copy(table_f[:, :], table_rows[:, :]).then_inc(table_f_s.sem, 1)
                dve.wait_ge(table_psum.sem, 1)
                dve.tensor_copy(tokens[:, T // P:T // P + n], bank[0][:, 0:n]).then_inc(tokens_s.sem, 1)
                dve.wait_ge(tokens_s.sem, 1)

            over_experts(dve, prologue, lambda e, u, first: split(e + 1, 1 - u, first), tile, table)

        @block.tensor
        def _(pe):
            def x_transposes(i):
                pe.wait_ge(gathered.sem, gathered.at(i))
                for c in range(DC):
                    for half in range(HALF):
                        mm = pe.transpose(bank[3][:, c * ETOK + half * P:c * ETOK + half * P + P],
                                          xg[:, half, c * P:(c + 1) * P], identf[:, :])
                mm.then_inc(gT_psum.sem, 1)

            def tile(i, u):
                pe.wait_ge(gT_lo_s.sem, gT_lo_s.at(i))
                for m, (h0, M) in enumerate(HT):
                    pe.wait_ge(prod_s.sem, prod_s.at(i, 0))
                    for side in range(2):
                        cols = slice(side * H0 + h0, side * H0 + h0 + M)
                        mm = three_products(pe, bank[m][0:M, side * ETOK:(side + 1) * ETOK],
                                            lambda c: w13_hi[:, u, c, cols], lambda c: w13_lo[:, u, c, cols],
                                            lambda c: xT_hi[:, c, :], lambda c: xT_lo[:, c, :], range(DC))
                    mm.then_inc(gu_psum.sem, 1)
                x_transposes(i + 1)
                pe.wait_ge(y_ready.sem, y_ready.at(i, 0))
                for m, (_, M) in enumerate(HT):
                    pe.wait_ge(h_lo_s.sem, h_lo_s.at(i, m + 1))
                    for half in range(HALF):
                        tok = slice(half * P, (half + 1) * P)
                        mm = three_products(pe, bank[4 + half][:, 0:D], lambda m: h_hi[0:M, m, tok], lambda m: h_lo[0:M, m, tok],
                                            lambda m: w2_hi[0:M, u, m, :], lambda m: w2_lo[0:M, u, m, :], (m,),
                                            first=m == 0, last=m == HM - 1)
                mm.then_inc(y_psum.sem, 1)

            def new_expert(e, u, first):
                pe.wait_ge(e_lo.sem, e_lo.at(e))
                pe.nop(nofuse=True)

            def table():
                n = ROUTED_SLOTS // P
                pe.wait_ge(table_f_s.sem, 1)
                pe.wait_ge(prod_s.sem, prod_s.at(SHARED_TILES - 2))
                pe.transpose(bank[0][:, 0:n], table_f[:, :], identf[0:n, 0:n]).then_inc(table_psum.sem, 1)
                pe.wait_ge(tokens_s.sem, 1)

            over_experts(pe, lambda: x_transposes(0), new_expert, tile, table)


PACK = {}
_at = 0
for _name, _shape in (("wz", (DC, D)), ("wh", (DC, D)), ("fc1", (DC, LAT)), ("gate", (DC, E)), ("up", (DC, UP)),
                      ("w1", (E, INTER)), ("w2", (E, LAT)), ("wg", (DC, D)), ("down", (UP // P, D)), ("fc2", (1, D))):
    PACK[_name] = (_at, _shape)
    _at += _shape[0] * _shape[1]
PACKED = _at
BZ, BH, BG = 0, DC, 2 * DC


def layer1_phase(nc, w, dram, consts, route, out):
    with ExitStack() as ctx:
        def sb(name, shape, dt=F32):
            return ctx.enter_context(nc.sbuf_tensor(name, shape, dt))

        def sig(name, per):
            return Signal(nc, ctx, name, per)

        identf, iota8 = consts["identf"], consts["iota8"]
        CHUNKS = 4
        w32 = sb("l1_w32", [P, PACKED])
        w_hi, w_lo = (sb(f"l1_w_{k}", [P, PACKED], F16) for k in ("hi", "lo"))

        def part(t, name, row, cols):
            at, (_, n) = PACK[name]
            return t[:, at + row * n + cols.start:at + row * n + cols.stop]

        bias = sb("l1_bias", [P, 3 * DC])
        neg_bz = sb("neg_bz", [P, DC])
        corr = sb("corr", [P, E])
        minus_half = sb("l1_minus_half", [P, TT])
        xin = sb("xin", [P, TT, D])
        ysh = sb("ysh", [P, TT, D])
        rows_k = sb("rows_k", [P, TT, 2, D])
        slot = sb("slot", [P, TT, 2], I32)
        wk = sb("wk", [P, TT, 2])
        x2 = sb("x2", [P, 2, TT, D])
        stats = sb("l1_stats", [P, TT, 6])
        mv = sb("l1_mv", [P, TT, 2])
        var_eps = sb("l1_var_eps", [P, TT])
        rstd = sb("l1_rstd", [P, TT])
        xn = sb("l1_xn", [P, TT, D])
        xT_hi, xT_lo = (sb(f"l1_xT_{k}", [P, DC, S], F16) for k in ("hi", "lo"))
        zs = sb("zs", [P, DC, S])
        keep = sb("keep", [P, DC, S])
        inject = sb("inject", [P, DC, S])
        hT = sb("hT", [P, DC, S])
        hT_hi, hT_lo = (sb(f"hT_{k}", [P, DC, S], F16) for k in ("hi", "lo"))
        gs = sb("gs", [P, DC, S])
        gh = sb("gh", [P, DC, S])
        lat_hi, lat_lo = (sb(f"lat_{k}", [P, S], F16) for k in ("hi", "lo"))
        sc = sb("l1_sc", [P, TT, E])
        sfc = sb("sfc", [P, TT, E])
        pairs = sb("pairs", [P, TT * 2, 6])
        gscore = sb("gscore", [P, TT, 2])
        gmask = sb("gmask", [P, TT, 2])
        top = sb("l1_top", [P, TT, 8])
        topi = sb("l1_topi", [P, TT, 8], U32)
        onehot = sb("l1_onehot", [P, 2, TT, E])
        chosen = sb("chosen", [P, TT, E])
        total = sb("total", [P, TT])
        weight = sb("weight", [P, TT, E])
        wT = sb("wT", [E, S])
        w_bc = sb("w_bc", [P, E, S])
        r = sb("r", [P, 3, S])
        rw = sb("rw", [P, 3, S])
        sq = sb("sq", [P, 3, S])
        up_hi, up_lo = (sb(f"up_{k}", [P, UP // P, S], F16) for k in ("hi", "lo"))
        he_hi, he_lo = (sb(f"he_{k}", [P, HE, S], F16) for k in ("hi", "lo"))
        comb_hi, comb_lo = (sb(f"comb_{k}", [P, S], F16) for k in ("hi", "lo"))
        y = sb("l1_y", [P, TT, D])
        bank = [ctx.enter_context(nc.psum_tensor(f"ybank{i}", [P, 512], F32)) for i in range(8)]
        OUT_BANK = (3, 4, 5, 7)
        NU = UP // P
        NR = NU + E

        loaded = sig("l1_loaded", 16 * 3)
        pack_loaded = [sig(f"pack_loaded{c}", 16) for c in range(CHUNKS)]
        pack_hi = sig("pack_hi", CHUNKS)
        pack_lo = sig("pack_lo", CHUNKS)
        half_filled = sig("half_filled", 1)
        neg_bz_s = sig("neg_bz_s", 1)
        xin_loaded = sig("xin_loaded", 32)
        slot_s = sig("slot_s", 2)
        gathered = sig("rows_gathered", 16 * TT * 2)
        x2_base = sig("x2_base", 1)
        x2_sum = sig("x2_sum", 2)
        dve_ln = sig("l1_dve_ln", 2)
        rstd_s = sig("l1_rstd_s", 2)
        xn_ready = sig("l1_xn_ready", 1)
        xT_psum = sig("l1_xT_psum", DC)
        xT_hi_s = sig("l1_xT_hi_s", DC)
        xT_lo_s = sig("l1_xT_lo_s", DC)
        zh_psum = sig("zh_psum", 2 * DC)
        lg_psum = sig("l1_lg_psum", 1)
        lat_psum = sig("lat_psum", 1)
        sc_s = sig("sc_s", 1)
        zs_s = sig("zs_s", DC)
        keep_s = sig("keep_s", DC)
        lat_hi_s = sig("lat_hi_s", 1)
        lat_lo_s = sig("lat_lo_s", 1)
        inject_s = sig("inject_s", DC)
        hT_s = sig("hT_s", DC)
        hT_hi_s = sig("hT_hi_s", DC)
        hT_lo_s = sig("hT_lo_s", DC)
        rt = sig("l1_rt", 15)
        wT_psum = sig("wT_psum", 1)
        wT_s = sig("wT_s", 1)
        wT_stored = sig("wT_stored", 16)
        w_bc_loaded = sig("w_bc_loaded", 16)
        u_psum = sig("u_psum", NR)
        r_s = sig("r_s", NR)
        rw_s = sig("rw_s", E)
        sq_s = sig("sq_s", NR)
        hid_hi = sig("hid_hi", NR)
        hid_lo = sig("hid_lo", NR)
        comb_psum = sig("comb_psum", E)
        comb_hi_s = sig("comb_hi_s", 1)
        comb_lo_s = sig("comb_lo_s", 1)
        g_psum = sig("g_psum", DC)
        gs_s = sig("gs_s", DC)
        gh_s = sig("gh_s", DC)
        out_psum = sig("out_psum", TT)
        y_ready = sig("l1_y_ready", TT)
        y_stored = sig("l1_y_stored", 16)

        def rows(t, b):
            return t[bass.ds(b * S, S), :].rearrange("(t p) d -> p t d", p=P)

        def pipeline(eng, front, step):
            front(0, 0)
            step(0, 0, True)
            with eng.Fori(0, NB // 2 - 1) as i:
                for u in (1, 0):
                    step(2 * i + 2 - u, u, True)
            step(NB - 1, 1, False)

        def hidden_bank(n):
            return bank[n % 3]

        block = ctx.enter_context(nc.Block())

        @block.sync
        def _(sp):
            for c in range(CHUNKS):
                cols = slice(PACKED * c // CHUNKS // 2 * 2, PACKED * (c + 1) // CHUNKS // 2 * 2)
                sp.dma_start(w32[:, cols], w["pack"][:, cols]).then_inc(pack_loaded[c].sem, 16)
            sp.dma_start(bias[:, :], w["bias"]).then_inc(loaded.sem, 16)
            sp.dma_start(corr[:, :], w["corr"].partition_broadcast(P)).then_inc(loaded.sem, 16)
            sp.dma_start(neg_bz[:, :], w["bias"][:, BZ:BZ + DC]).then_inc(loaded.sem, 16)

            def front(b, u):
                sp.wait_ge(x2_base.sem, x2_base.at(b, 0))
                sp.dma_start(xin[:, :, :], rows(dram["x1"], b)).then_inc(xin_loaded.sem, 16)
                sp.dma_start(ysh[:, :, :], rows(dram["y"], b)).then_inc(xin_loaded.sem, 16)

            def step(b, u, more):
                if more:
                    front(b + 1, 1 - u)
                sp.wait_ge(wT_s.sem, wT_s.at(b))
                sp.dma_start(dram["wT"], wT[:, :]).then_inc(wT_stored.sem, 16)
                sp.wait_ge(wT_stored.sem, wT_stored.at(b))
                sp.nop(nofuse=True)
                sp.wait_ge(rw_s.sem, rw_s.at(b, 0))
                sp.dma_start(w_bc[:, :, :], dram["wT"].partition_broadcast(P)).then_inc(w_bc_loaded.sem, 16)
                sp.wait_ge(y_ready.sem, y_ready.at(b))
                sp.dma_start(rows(out, b), y[:, :, :]).then_inc(y_stored.sem, 16)

            pipeline(sp, front, step)
            sp.wait_ge(y_stored.sem, y_stored.at(NB - 1))

        @block.gpsimd
        def _(pool):
            pool.memset(minus_half[:, :], -0.5).then_inc(half_filled.sem, 1)
            pool.wait_ge(half_filled.sem, 1)

            def front(b, u):
                pool.wait_ge(xin_loaded.sem, xin_loaded.at(b))
                pool.wait_ge(y_ready.sem, y_ready.at(b - 1, 0))
                pool.tensor_tensor(x2[:, u, :, :], xin[:, :, :], ysh[:, :, :], ALU.add).then_inc(x2_base.sem, 1)
                pool.wait_ge(x2_sum.sem, x2_sum.at(b, 0))
                pool.wait_ge(slot_s.sem, slot_s.at(b))
                pool.nop(nofuse=True)
                for t in range(TT):
                    for k in range(2):
                        pool.indirect_dma_start(rows_k[:, t, k, :], None, dram["y"],
                                                bass.IndirectOffsetOnAxis(slot[:, t, k:k + 1], 0)).then_inc(gathered.sem, 16)
                pool.wait_ge(dve_ln.sem, dve_ln.at(b))
                pool.tensor_tensor(var_eps[:, :], mv[:, :, 1], consts["eps_col"][:, 0:TT], ALU.add).then_inc(rstd_s.sem, 1)
                pool.wait_ge(rstd_s.sem, rstd_s.at(b, 1))
                pool.tensor_tensor(rstd[:, :], var_eps[:, :], minus_half[:, :], ALU.pow).then_inc(rstd_s.sem, 1)

            def step(b, u, more):
                if more:
                    front(b + 1, 1 - u)
                pool.wait_ge(w_bc_loaded.sem, w_bc_loaded.at(b))
                for e in range(E):
                    n = NU + e
                    pool.wait_ge(r_s.sem, r_s.at(b, n + 1))
                    pool.wait_ge(sq_s.sem, sq_s.at(b, n - 2))
                    pool.tensor_tensor(rw[:, n % 3, :], r[:, n % 3, :], w_bc[:, e, :], ALU.mult).then_inc(rw_s.sem, 1)

            pipeline(pool, front, step)

        @block.scalar
        def _(act):
            for c in range(CHUNKS):
                cols = slice(PACKED * c // CHUNKS // 2 * 2, PACKED * (c + 1) // CHUNKS // 2 * 2)
                act.wait_ge(pack_loaded[c].sem, 16)
                act.activation(w_hi[:, cols], w32[:, cols], ACT.Copy).then_inc(pack_hi.sem, 1)
            act.wait_ge(loaded.sem, loaded.at(0))
            act.wait_ge(neg_bz_s.sem, 1)

            def front(b, u):
                for c in range(DC):
                    act.wait_ge(xT_psum.sem, xT_psum.at(b, c + 1))
                    act.wait_ge(u_psum.sem, u_psum.at(b - 1, NU))
                    act.activation(xT_hi[:, c, :], bank[c][:, :], ACT.Copy).then_inc(xT_hi_s.sem, 1)

            def relu(b, n):
                act.wait_ge(u_psum.sem, u_psum.at(b, n + 1))
                if n >= 3:
                    act.wait_ge(sq_s.sem, sq_s.at(b, n - 2))
                act.activation(r[:, n % 3, :], hidden_bank(n)[:, :], ACT.Relu).then_inc(r_s.sem, 1)

            def hidden_hi(b, n):
                act.wait_ge(sq_s.sem, sq_s.at(b, n + 1))
                if n < NU:
                    act.wait_ge(out_psum.sem, out_psum.at(b, 0))
                    dst = up_hi[:, n, :]
                else:
                    if n - NU >= HE:
                        act.wait_ge(comb_psum.sem, comb_psum.at(b, n - NU - HE + 1))
                    dst = he_hi[:, (n - NU) % HE, :]
                act.activation(dst, sq[:, n % 3, :], ACT.Copy).then_inc(hid_hi.sem, 1)

            def step(b, u, more):
                for c in range(DC):
                    act.wait_ge(zh_psum.sem, zh_psum.at(b, c + 1))
                    act.activation(zs[:, c, :], bank[2 + c][:, :], ACT.Sigmoid, bias=bias[:, BZ + c:BZ + c + 1]).then_inc(zs_s.sem, 1)
                    act.activation(keep[:, c, :], bank[2 + c][:, :], ACT.Sigmoid, bias=neg_bz[:, c:c + 1],
                                   scale=-1.0).then_inc(keep_s.sem, 1)
                act.wait_ge(lg_psum.sem, lg_psum.at(b))
                act.activation(sc[:, :, :], bank[7][:, 0:TT * E].rearrange("p (t e) -> p t e", e=E),
                               ACT.Sigmoid).then_inc(sc_s.sem, 1)
                act.wait_ge(lat_psum.sem, lat_psum.at(b))
                act.activation(lat_hi[:, :], bank[6][:, :], ACT.Copy).then_inc(lat_hi_s.sem, 1)
                for n in range(NU + 2):
                    if n < NU:
                        relu(b, n)
                    if n >= 2:
                        hidden_hi(b, n - 2)
                for c in range(DC):
                    act.wait_ge(hT_s.sem, hT_s.at(b, c + 1))
                    act.activation(hT_hi[:, c, :], hT[:, c, :], ACT.Copy).then_inc(hT_hi_s.sem, 1)
                for c in range(DC):
                    act.wait_ge(g_psum.sem, g_psum.at(b, c + 1))
                    act.activation(gs[:, c, :], bank[c][:, :], ACT.Sigmoid, bias=bias[:, BG + c:BG + c + 1]).then_inc(gs_s.sem, 1)
                for n in range(NU, NR + 2):
                    if n < NR:
                        relu(b, n)
                    if n >= NU + 2:
                        hidden_hi(b, n - 2)
                act.wait_ge(comb_psum.sem, comb_psum.at(b))
                act.activation(comb_hi[:, :], bank[6][:, :], ACT.Copy).then_inc(comb_hi_s.sem, 1)
                if more:
                    front(b + 1, 1 - u)

            pipeline(act, front, step)

        @block.vector
        def _(dve):
            for c in range(CHUNKS):
                cols = slice(PACKED * c // CHUNKS // 2 * 2, PACKED * (c + 1) // CHUNKS // 2 * 2)
                dve.wait_ge(pack_hi.sem, c + 1)
                dve.tensor_tensor(w_lo[:, cols], w32[:, cols], w_hi[:, cols], ALU.subtract).then_inc(pack_lo.sem, 1)
            dve.wait_ge(loaded.sem, loaded.at(0))
            dve.tensor_scalar(neg_bz[:, :], neg_bz[:, :], -1.0, None, ALU.mult).then_inc(neg_bz_s.sem, 1)

            def slots(b):
                tiles = bass.ds(b * TT, TT)
                dve.wait_ge(gathered.sem, gathered.at(b, 0))
                dve.tensor_scalar(slot[:, :, :], route["pos"][:, tiles, :], float(SHARED_TILES * ETOK), None,
                                  ALU.add).then_inc(slot_s.sem, 1)
                dve.tensor_copy(wk[:, :, :], route["weights"][:, tiles, :]).then_inc(slot_s.sem, 1)

            def front(b, u):
                dve.wait_ge(slot_s.sem, slot_s.at(b))
                dve.wait_ge(x2_base.sem, x2_base.at(b))
                dve.wait_ge(gathered.sem, gathered.at(b))
                for k in range(2):
                    for t in range(TT):
                        ins = dve.scalar_tensor_tensor(x2[:, u, t, :], rows_k[:, t, k, :], wk[:, t, k:k + 1], x2[:, u, t, :],
                                                       ALU.mult, ALU.add)
                    ins.then_inc(x2_sum.sem, 1)
                    dve.wait_ge(x2_sum.sem, x2_sum.at(b, k + 1))
                for t in range(TT):
                    ins = dve.bn_stats(stats[:, t, :], x2[:, u, t, :])
                ins.then_inc(dve_ln.sem, 1)
                dve.wait_ge(dve_ln.sem, dve_ln.at(b, 1))
                dve.nop(nofuse=True)
                for t in range(TT):
                    ins = dve.bn_aggr(mv[:, t, :], stats[:, t, :])
                ins.then_inc(dve_ln.sem, 1)
                dve.wait_ge(dve_ln.sem, dve_ln.at(b))
                dve.wait_ge(rstd_s.sem, rstd_s.at(b))
                for t in range(TT):
                    ins = dve.tensor_scalar(xn[:, t, :], x2[:, u, t, :], mv[:, t, 0:1], rstd[:, t:t + 1],
                                            ALU.subtract, ALU.mult)
                ins.then_inc(xn_ready.sem, 1)

            def x_low(b):
                for c in range(DC):
                    dve.wait_ge(xT_hi_s.sem, xT_hi_s.at(b, c + 1))
                    dve.tensor_tensor(xT_lo[:, c, :], bank[c][:, :], xT_hi[:, c, :], ALU.subtract).then_inc(xT_lo_s.sem, 1)

            def done(b, n, ins):
                ins.then_inc(rt.sem, 1)
                dve.wait_ge(rt.sem, rt.at(b, n))

            def router_groups(b):
                dve.wait_ge(sc_s.sem, sc_s.at(b))
                done(b, 1, dve.tensor_tensor(sfc[:, :, :], sc[:, :, :], corr[:, :].unsqueeze(1).to_broadcast([P, TT, E]), ALU.add))
                g4 = sfc[:, :, :].rearrange("p t (g s) -> p (t g) s", s=E // 2)
                dve.tensor_tensor(pairs[:, :, 0:3], g4[:, :, 0:3], g4[:, :, 1:4], ALU.add)
                dve.tensor_tensor(pairs[:, :, 3:5], g4[:, :, 0:2], g4[:, :, 2:4], ALU.add)
                done(b, 2, dve.tensor_tensor(pairs[:, :, 5:6], g4[:, :, 0:1], g4[:, :, 3:4], ALU.add))
                done(b, 3, dve.tensor_reduce(gscore[:, :, :].rearrange("p t g -> p (t g)"), pairs[:, :, :], AX.X, ALU.max))
                done(b, 4, dve.tensor_tensor(gmask[:, :, 0:1], gscore[:, :, 0:1], gscore[:, :, 1:2], ALU.is_ge))
                done(b, 5, dve.tensor_scalar(gmask[:, :, 1:2], gmask[:, :, 0:1], -1.0, 1.0, ALU.mult, ALU.add))
                done(b, 6, dve.tensor_tensor(g4, g4, gmask[:, :, :].rearrange("p t g -> p (t g)").unsqueeze(2).to_broadcast([P, TT * 2, E // 2]),
                                       ALU.mult))

            def router_choice(b):
                dve.nop(nofuse=True)
                for t in range(TT):
                    ins = dve.max(top[:, t, :], sfc[:, t, :])
                done(b, 7, ins)
                dve.nop(nofuse=True)
                for t in range(TT):
                    ins = dve.max_index(topi[:, t, :], top[:, t, :], sfc[:, t, :])
                done(b, 8, ins)
                for k in range(2):
                    ins = dve.tensor_tensor(onehot[:, k, :, :], iota8[:, :].unsqueeze(1).to_broadcast([P, TT, E]),
                                            topi[:, :, k:k + 1].to_broadcast([P, TT, E]), ALU.is_equal)
                done(b, 9, ins)

            def router_weights(b):
                done(b, 10, dve.tensor_tensor(chosen[:, :, :], onehot[:, 0, :, :], onehot[:, 1, :, :], ALU.add))
                done(b, 11, dve.tensor_tensor(chosen[:, :, :], chosen[:, :, :], sc[:, :, :], ALU.mult))
                done(b, 12, dve.tensor_reduce(total[:, :], chosen[:, :, :], AX.X, ALU.add))
                done(b, 13, dve.tensor_scalar(total[:, :], total[:, :], 1e-20, None, ALU.add))
                done(b, 14, dve.reciprocal(total[:, :], total[:, :]))
                done(b, 15, dve.tensor_tensor(weight[:, :, :], chosen[:, :, :], total[:, :].unsqueeze(2).to_broadcast([P, TT, E]), ALU.mult))

            def square(b, n):
                if n < NU:
                    dve.wait_ge(r_s.sem, r_s.at(b, n + 1))
                    other = r
                else:
                    dve.wait_ge(rw_s.sem, rw_s.at(b, n - NU + 1))
                    other = rw
                if n >= 3:
                    dve.wait_ge(hid_lo.sem, hid_lo.at(b, n - 2))
                dve.tensor_tensor(sq[:, n % 3, :], r[:, n % 3, :], other[:, n % 3, :], ALU.mult).then_inc(sq_s.sem, 1)

            def hidden_low(b, n):
                dve.wait_ge(hid_hi.sem, hid_hi.at(b, n + 1))
                hi, lo = (up_hi[:, n, :], up_lo[:, n, :]) if n < NU else (he_hi[:, (n - NU) % HE, :], he_lo[:, (n - NU) % HE, :])
                dve.tensor_tensor(lo, sq[:, n % 3, :], hi, ALU.subtract).then_inc(hid_lo.sem, 1)

            def step(b, u, more):
                if more:
                    slots(b + 1)
                for c in range(DC):
                    dve.wait_ge(zh_psum.sem, zh_psum.at(b, DC + c + 1))
                    dve.wait_ge(zs_s.sem, zs_s.at(b, c + 1))
                    dve.scalar_tensor_tensor(inject[:, c, :], bank[4 + c][:, :], bias[:, BH + c:BH + c + 1], zs[:, c, :],
                                             ALU.add, ALU.mult).then_inc(inject_s.sem, 1)
                dve.wait_ge(lat_hi_s.sem, lat_hi_s.at(b))
                dve.tensor_tensor(lat_lo[:, :], bank[6][:, :], lat_hi[:, :], ALU.subtract).then_inc(lat_lo_s.sem, 1)
                for n in range(NU + 2):
                    if n == NU + 1:
                        dve.wait_ge(wT_psum.sem, wT_psum.at(b))
                        dve.tensor_copy(wT[:, :], bank[7][0:E, :]).then_inc(wT_s.sem, 1)
                    if n < NU:
                        square(b, n)
                    if n >= 2:
                        hidden_low(b, n - 2)
                    if n == 0:
                        router_groups(b)
                    elif n == 1:
                        router_choice(b)
                    elif n == 2:
                        router_weights(b)
                for c in range(DC):
                    dve.wait_ge(inject_s.sem, inject_s.at(b, c + 1))
                    dve.wait_ge(keep_s.sem, keep_s.at(b, c + 1))
                    dve.tensor_tensor_scan(hT[:, c, :], keep[:, c, :], inject[:, c, :], 0.0, ALU.mult, ALU.add).then_inc(hT_s.sem, 1)
                for c in range(DC):
                    dve.wait_ge(hT_hi_s.sem, hT_hi_s.at(b, c + 1))
                    dve.tensor_tensor(hT_lo[:, c, :], hT[:, c, :], hT_hi[:, c, :], ALU.subtract).then_inc(hT_lo_s.sem, 1)
                if more:
                    front(b + 1, 1 - u)
                for n in range(NU, NR + 2):
                    if n < NR:
                        square(b, n)
                    if n >= NU + 2:
                        hidden_low(b, n - 2)
                    if n in (NU + 2, NU + 3):
                        c = n - NU - 2
                        dve.wait_ge(gs_s.sem, gs_s.at(b, c + 1))
                        dve.tensor_tensor(gh[:, c, :], gs[:, c, :], hT[:, c, :], ALU.mult).then_inc(gh_s.sem, 1)
                dve.wait_ge(comb_hi_s.sem, comb_hi_s.at(b))
                dve.tensor_tensor(comb_lo[:, :], bank[6][:, :], comb_hi[:, :], ALU.subtract).then_inc(comb_lo_s.sem, 1)
                if more:
                    x_low(b + 1)
                dve.wait_ge(y_stored.sem, y_stored.at(b, 0))
                for t in range(TT):
                    dve.wait_ge(out_psum.sem, out_psum.at(b, t + 1))
                    dve.tensor_tensor(y[:, t, :], bank[OUT_BANK[t]][:, 0:D], x2[:, u, t, :], ALU.add).then_inc(y_ready.sem, 1)

            def first(b, u):
                slots(b)
                front(b, u)
                x_low(b)

            pipeline(dve, first, step)

        @block.tensor
        def _(pe):
            whole = slice(0, S)

            def transposes(b):
                pe.wait_ge(xn_ready.sem, xn_ready.at(b))
                for c in range(DC):
                    for t in range(TT):
                        mm = pe.transpose(bank[c][:, t * P:(t + 1) * P], xn[:, t, c * P:(c + 1) * P], identf[:, :])
                    mm.then_inc(xT_psum.sem, 1)

            def from_x(out, name, cols):
                return three_products(pe, out, lambda c: part(w_hi, name, c, cols), lambda c: part(w_lo, name, c, cols),
                                      lambda c: xT_hi[:, c, :], lambda c: xT_lo[:, c, :], range(DC))

            def hidden(b, n):
                if n >= 3:
                    pe.wait_ge(r_s.sem, r_s.at(b, n - 2))
                if n < NU:
                    mm = from_x(hidden_bank(n)[:, :], "up", slice(n * P, (n + 1) * P))
                else:
                    mm = three_products(pe, hidden_bank(n)[:, :], lambda e: part(w_hi, "w1", e, slice(0, INTER)),
                                        lambda e: part(w_lo, "w1", e, slice(0, INTER)),
                                        lambda e: lat_hi[:, :], lambda e: lat_lo[:, :], (n - NU,))
                mm.then_inc(u_psum.sem, 1)

            def combine(b, e):
                pe.wait_ge(hid_lo.sem, hid_lo.at(b, NU + e + 1))
                three_products(pe, bank[6][:, :], lambda e: part(w_hi, "w2", e, slice(0, LAT)),
                               lambda e: part(w_lo, "w2", e, slice(0, LAT)),
                               lambda e: he_hi[:, e % HE, :], lambda e: he_lo[:, e % HE, :], (e,),
                               first=e == 0, last=e == E - 1).then_inc(comb_psum.sem, 1)

            def step(b, u, more):
                pe.wait_ge(xT_lo_s.sem, xT_lo_s.at(b))
                pe.wait_ge(y_ready.sem, y_ready.at(b - 1, 1))
                for c in range(DC):
                    from_x(bank[2 + c][:, :], "wz", slice(c * P, (c + 1) * P)).then_inc(zh_psum.sem, 1)
                pe.wait_ge(y_ready.sem, y_ready.at(b - 1))
                for c in range(DC):
                    from_x(bank[4 + c][:, :], "wh", slice(c * P, (c + 1) * P)).then_inc(zh_psum.sem, 1)
                for t in range(TT):
                    tok = slice(t * P, (t + 1) * P)
                    mm = three_products(pe, bank[7][:, t * E:(t + 1) * E], lambda c: xT_hi[:, c, tok], lambda c: xT_lo[:, c, tok],
                                        lambda c: part(w_hi, "gate", c, slice(0, E)), lambda c: part(w_lo, "gate", c, slice(0, E)),
                                        range(DC))
                mm.then_inc(lg_psum.sem, 1)
                from_x(bank[6][:, :], "fc1", slice(0, LAT)).then_inc(lat_psum.sem, 1)
                pe.wait_ge(keep_s.sem, keep_s.at(b))
                for n in range(NU):
                    hidden(b, n)
                    if n == NU - 1:
                        pe.wait_ge(rt.sem, rt.at(b))
                        for t in range(TT):
                            mm = pe.transpose(bank[7][0:E, t * P:(t + 1) * P], weight[:, t, :], identf[:, :])
                        mm.then_inc(wT_psum.sem, 1)
                pe.wait_ge(hid_lo.sem, hid_lo.at(b, NU))
                pe.wait_ge(wT_s.sem, wT_s.at(b))
                pe.wait_ge(inject_s.sem, inject_s.at(b))
                for t in range(TT):
                    tok = slice(t * P, (t + 1) * P)
                    three_products(pe, bank[OUT_BANK[t]][:, 0:D], lambda n: up_hi[:, n, tok], lambda n: up_lo[:, n, tok],
                                   lambda n: part(w_hi, "down", n, slice(0, D)), lambda n: part(w_lo, "down", n, slice(0, D)),
                                   range(NU), last=False)
                pe.wait_ge(hT_lo_s.sem, hT_lo_s.at(b))
                pe.wait_ge(r_s.sem, r_s.at(b, NU))
                for c in range(DC):
                    three_products(pe, bank[c][:, :], lambda k: part(w_hi, "wg", k, slice(c * P, (c + 1) * P)),
                                   lambda k: part(w_lo, "wg", k, slice(c * P, (c + 1) * P)),
                                   lambda k: hT_hi[:, k, :], lambda k: hT_lo[:, k, :], range(DC)).then_inc(g_psum.sem, 1)
                pe.wait_ge(lat_lo_s.sem, lat_lo_s.at(b))
                for e in range(E + COMBINE_LAG):
                    if e == 1:
                        pe.wait_ge(gs_s.sem, gs_s.at(b))
                    if e < E:
                        hidden(b, NU + e)
                    if e >= COMBINE_LAG:
                        combine(b, e - COMBINE_LAG)
                    if e == E and more:
                        pe.wait_ge(r_s.sem, r_s.at(b))
                        transposes(b + 1)
                pe.wait_ge(gh_s.sem, gh_s.at(b))
                for t in range(TT):
                    for c in range(DC):
                        pe.matmul(bank[OUT_BANK[t]][:, c * P:(c + 1) * P], gh[:, c, t * P:(t + 1) * P], identf[:, :],
                                  start=False, stop=False)
                pe.wait_ge(comb_lo_s.sem, comb_lo_s.at(b))
                for t in range(TT):
                    tok = slice(t * P, (t + 1) * P)
                    three_products(pe, bank[OUT_BANK[t]][:, 0:D], lambda n: comb_hi[:, tok], lambda n: comb_lo[:, tok],
                                   lambda n: part(w_hi, "fc2", 0, slice(0, D)), lambda n: part(w_lo, "fc2", 0, slice(0, D)),
                                   (0,), first=False).then_inc(out_psum.sem, 1)

            pe.wait_ge(pack_lo.sem, CHUNKS)
            pipeline(pe, lambda b, u: transposes(b), step)


_INS = ["x", "wqkv", "gate0", "wout", "bqk", "bv", "bout", "gate_b", "w13", "w2", "b13", "b2", "pack", "bias", "corr"]


def build(nc, ins, out):
    with ExitStack() as ctx:
        def sb(name, shape, dt=F32):
            return ctx.enter_context(nc.sbuf_tensor(name, shape, dt))

        consts = constants(nc, ctx)
        dram = {"x1": nc.dram_tensor("x1_dram", (T, D), F32).ap(),
                "xn": nc.dram_tensor("xn_dram", (T, D), F32).ap(),
                "qk_hi": nc.dram_tensor("qk_hi_dram", (2 * D, S), F16).ap(),
                "qk_lo": nc.dram_tensor("qk_lo_dram", (2 * D, S), F16).ap(),
                "y": nc.dram_tensor("y_dram", (MAX_TILES * ETOK, D), F32).ap(),
                "wT": nc.dram_tensor("wT_dram", (E, S), F32).ap()}
        route = {"weights": sb("route_weights", [P, T // P, 2]), "rank": sb("route_rank", [P, T // P, 2]),
                 "onehot": sb("route_onehot", [P, T // P, 2, E]), "run": sb("route_run", [P, TT + 1, E]),
                 "bounds": sb("bounds", [P, E + 1], I32), "pos": sb("pos", [P, T // P, 2], I32),
                 "tokens": sb("tokens", [P, SLOTS // P], I32), "ids": sb("ids", [P, T // P], I32),
                 "table": nc.dram_tensor("table_dram", (ROUTED_SLOTS, 1), I32).ap()}
        mix_phase(nc, ins["x"], ins, dram, consts, route)
        slots_phase(nc, route)
        experts_phase(nc, ins, dram, consts, route)
        layer1_phase(nc, ins, dram, consts, route, out)


def _layout(i):
    import numpy as np

    def rows(a):
        a = np.asarray(a)
        return a.reshape(-1, P, a.shape[-1]).transpose(1, 0, 2).reshape(P, -1)

    wqkv = np.asarray(i["L0_attn_Wqkv"]).reshape(NH, D, 3, HD).transpose(1, 2, 0, 3).reshape(D, 3 * D)
    bqkv = np.asarray(i["L0_attn_bqkv"]).reshape(NH, 3, HD).transpose(1, 0, 2).reshape(3 * D)
    f = {k: np.asarray(i["L0_ffn_" + k]) for k in ("w1", "w3", "w2", "b1", "b3", "b2", "sw1", "sw3", "sw2", "sb1", "sb3", "sb2")}

    def experts(shared, routed):
        return np.concatenate([shared[None], routed, routed[-1:]])

    b13 = np.zeros((NX + 1, P, 2 * len(HT)), f["b1"].dtype)
    for side, b in enumerate((experts(f["sb1"], f["b1"]), experts(f["sb3"], f["b3"]))):
        for m, (h0, n) in enumerate(HT):
            b13[:, :n, side * len(HT) + m] = b[:, h0:h0 + n]
    a = {k: np.asarray(i["L1_attn_" + k]) for k in ("Wz", "bz", "Wh", "bh", "Wg", "bg")}
    g = {k: np.asarray(i["L1_ffn_" + k]) for k in ("gate", "corr_bias", "w1", "w2", "fc1_w", "fc2_w", "up_w", "down_w")}
    pack = {"wz": rows(a["Wz"].transpose(1, 0, 2).reshape(D, D)), "wh": rows(a["Wh"].transpose(1, 0, 2).reshape(D, D)),
            "fc1": rows(g["fc1_w"].T), "gate": rows(g["gate"].T), "up": rows(g["up_w"].T),
            "w1": g["w1"].transpose(2, 0, 1).reshape(LAT, -1), "w2": g["w2"].transpose(2, 0, 1).reshape(INTER, -1),
            "wg": rows(a["Wg"]), "down": rows(g["down_w"].T), "fc2": rows(g["fc2_w"].T)}
    return {
        "x": np.asarray(i["L0_attn_x"]).reshape(T, D), "wqkv": wqkv, "gate0": np.asarray(i["L0_ffn_gate_w"]).T,
        "wout": np.asarray(i["L0_attn_Wout"]), "bqk": bqkv[:2 * D].reshape(4, P).T, "bv": bqkv[2 * D:],
        "bout": np.asarray(i["L0_attn_bout"]), "gate_b": np.asarray(i["L0_ffn_gate_b"]),
        "w13": np.concatenate([experts(f["sw1"], f["w1"]), experts(f["sw3"], f["w3"])], 2),
        "w2": experts(f["sw2"], f["w2"]), "b13": b13, "b2": experts(f["sb2"], f["b2"])[:, None, :],
        "pack": np.concatenate([pack[n] for n in PACK], 1),
        "bias": np.concatenate([a["bz"].reshape(DC, P).T, a["bh"].reshape(DC, P).T, a["bg"].reshape(DC, P).T], 1),
        "corr": g["corr_bias"],
    }


def kernel(**inputs):
    import numpy as np
    import concourse.bacc as bacc
    from concourse.bass_utils import run_bass_kernel_spmd

    laid = _layout(inputs)
    nc = bacc.Bacc("TRN2", target_bir_lowering=False, num_devices=1)
    arrays, ins = {}, {}
    for name in _INS:
        a = np.ascontiguousarray(laid[name])
        arrays[f"in_{name}"] = a
        ins[name] = nc.dram_tensor(f"in_{name}", a.shape, mybir.dt.from_np(a.dtype), kind="ExternalInput").ap()
    out = nc.dram_tensor("out_0", (T, D), F32, kind="ExternalOutput").ap()
    build(nc, ins, out)
    r = run_bass_kernel_spmd(nc, [arrays], core_ids=[0])
    return r.results[0]["out_0"].reshape(NB, S, D)
```

```python
from contextlib import ExitStack

import concourse.bass as bass
from concourse import mybir

F32 = mybir.dt.float32
F16 = mybir.dt.float16
BF16 = mybir.dt.bfloat16
I32 = mybir.dt.int32
U32 = mybir.dt.uint32
ALU = mybir.AluOpType
ACT = mybir.ActivationFunctionType
AX = mybir.AxisListType

P = 128
NB, S, D = 8, 512, 256
T = NB * S
DC = D // P
TT = S // P
NH, HD = 16, 16
E = 8
EPS = 1e-5
H0 = 352
HT = [(0, 128), (128, 128), (256, 96)]
ETOK = 256
NX = E + 1
SHARED_TILES = T // ETOK
MIN_TILES = 2
USED_TILES = SHARED_TILES + 2 * T // ETOK
MAX_TILES = USED_TILES + MIN_TILES * E
MOST_TILES = T // ETOK
ROUTED_TILES = MAX_TILES - SHARED_TILES
AHEAD = 2
SLOTS = (MAX_TILES + AHEAD) * ETOK
ROUTED_SLOTS = SLOTS - SHARED_TILES * ETOK
LAT, INTER, UP = 128, 128, 1024
COMBINE_LAG = 5
HE = 5

STK = 96
PCOLS = P * (TT * (TT + 1) // 2)
QOFF = [P * j * (j + 1) // 2 for j in range(TT)]
KOFF = [P * sum(TT - i for i in range(k)) for k in range(TT)]
Q_UNITS = ((0, 1), (2,), (3,))
K_UNITS = ((0,), (1,), (2, 3))
U = len(Q_UNITS)
MASKED = -1e30
AT_OUT_T, AT_PROJ = (3, 6), (9, 12)
AT_X_T, AT_Q, AT_K, AT_V, AT_LOGITS = (18, 21), (24, 27), (30, 33), (36, 39), 42
AT_DIVIDE, AT_STATS, AT_NORM = 2, 10, 13
AT_SCORES, AT_CHOICE, AT_WEIGHTS, AT_RANK_SUMS, AT_RANKS = (3, 4), (6, 7), 9, 15, (17, 18, 19, 21, 22, 24)
LAG = 1


def is_int(i, n):
    return isinstance(i, int) and i == n


class Signal:

    def __init__(self, nc, ctx, name, per_step):
        self.sem = ctx.enter_context(nc.semaphore(name))
        self.per = per_step

    def at(self, step, n=None):
        v = step * self.per + (self.per if n is None else n)
        return max(v, 0) if isinstance(v, int) else v


def three_products(pe, out, hi_a, lo_a, hi_b, lo_b, chunks, first=True, last=True):
    n = len(chunks)
    for x, c in enumerate(chunks):
        pe.matmul(out, hi_a(c), hi_b(c), start=first and x == 0, stop=False)
        pe.matmul(out, hi_a(c), lo_b(c), start=False, stop=False)
        mm = pe.matmul(out, lo_a(c), hi_b(c), start=False, stop=last and x == n - 1)
    return mm


def mix_phase(nc, x, w, dram, consts, route):
    with ExitStack() as ctx:
        def sb(name, shape, dt=F32):
            return ctx.enter_context(nc.sbuf_tensor(name, shape, dt))

        def ps(name, shape, dt=F32):
            return ctx.enter_context(nc.psum_tensor(name, shape, dt))

        def sig(name, per):
            return Signal(nc, ctx, name, per)

        identf, identb, ones_b, tri, maskadd, iota8 = (consts[k] for k in ("identf", "identb", "ones_b", "tri", "maskadd", "iota8"))
        wqkv32 = sb("wqkv32", [P, DC, 3 * D])
        wout32 = sb("wout32", [P, DC, D])
        gate32 = sb("gate32", [P, DC, E])
        wqkv_hi, wqkv_lo = (sb(f"wqkv_{k}", [P, DC, 3 * D], F16) for k in ("hi", "lo"))
        wout_hi, wout_lo = (sb(f"wout_{k}", [P, DC, D], F16) for k in ("hi", "lo"))
        gate_hi, gate_lo = (sb(f"gate_{k}", [P, DC, E], F16) for k in ("hi", "lo"))
        bqk = sb("bqk", [P, 4])
        bq = sb("bq", [P, 2])
        bv_row = sb("bv_row", [P, D])
        bout_row = sb("bout_row", [P, D])
        gateb_row = sb("gateb_row", [P, E])
        zeros16 = sb("zeros16", [P, S], F16)
        zeros_f = sb("zeros_f", [P, D])
        xr = sb("xr", [P, TT, D])
        stats = sb("stats", [P, TT, 6])
        mv = sb("mv", [P, TT, 2])
        var_eps = sb("var_eps", [P, TT])
        rstd = sb("rstd", [P, TT])
        minus_half = sb("minus_half", [P, TT])
        xb = sb("xb", [P, 2, TT, D])
        xn = sb("xn", [P, TT, D])
        xT_hi, xT_lo = (sb(f"xT_{k}", [P, DC, S], F16) for k in ("hi", "lo"))
        qk_hi, qk_lo = (sb(f"qk_{k}", [P, 4, S], F16) for k in ("hi", "lo"))
        q32 = sb("q32", [P, 2, S])
        q_stack = sb("q_stack", [STK, 2, NH, S], F16)
        k_stack = sb("k_stack", [STK, 2, NH, S], F16)
        v32 = sb("v32", [P, TT, D])
        v_hi, v_lo = (sb(f"v_{k}", [P, 2, TT, NH, HD], F16) for k in ("hi", "lo"))
        neg_max = sb("neg_max", [P, 2, TT])
        p32 = sb("p32", [P, 2, PCOLS])
        p_hi, p_lo = (sb(f"p_{k}", [P, 2, PCOLS], F16) for k in ("hi", "lo"))
        row_sum = sb("row_sum", [P, 2, TT, NH])
        o_rows = sb("o_rows", [P, TT, D])
        oT_hi, oT_lo = (sb(f"oT_{k}", [P, DC, S], F16) for k in ("hi", "lo"))
        x1 = sb("x1", [P, TT, D])
        lg = sb("lg", [P, TT, E])
        lmax = sb("lmax", [P, TT])
        ex = sb("ex", [P, TT, E])
        exs = sb("exs", [P, TT])
        scores = sb("scores", [P, TT, E])
        biased = sb("biased", [P, TT, E])
        top = sb("top", [P, TT, 8])
        topi = sb("topi", [P, TT, 8], U32)
        onehot = sb("onehot", [P, TT, 2, E])
        picked = sb("picked", [P, TT, 2, E])
        member = sb("member", [P, TT, E], BF16)
        ranks = sb("ranks", [P, TT, E])
        tot = sb("tot", [P, 2, TT, E])
        run = route["run"]

        bank = [ps(f"bank{i}", [P, 512]) for i in range(8)]

        w_loaded = sig("w_loaded", 16 * 7)
        w_hi = sig("w_hi", 3)
        w_lo = sig("w_lo", 3)
        bq_scaled = sig("bq_scaled", 1)
        filled = sig("filled", 3)
        stacks_filled = sig("stacks_filled", 16 * 4)
        tail_filled = sig("tail_filled", 16)
        run_cleared = sig("run_cleared", 1)
        x_loaded = sig("x_loaded", 16)
        dve_ln = sig("dve_ln", 2)
        rstd_s = sig("rstd_s", 2)
        xn_ready = sig("xn_ready", 1)
        xb_ready = sig("xb_ready", 1)
        xn_stored = sig("xn_stored", 16)
        xT_psum = sig("xT_psum", DC)
        xT_hi_s = sig("xT_hi_s", DC)
        xT_lo_s = sig("xT_lo_s", DC)
        qk_psum = sig("qk_psum", 4)
        q32_s = sig("q32_s", 2)
        qk_hi_s = sig("qk_hi_s", 4)
        q_lo_s = sig("q_lo_s", 2)
        k_lo_s = sig("k_lo_s", 2)
        qk_stored = sig("qk_stored", 32)
        stacks_loaded = sig("stacks_loaded", 96)
        v_psum = sig("v_psum", 2)
        v32_s = sig("v32_s", 2)
        v_hi_s = sig("v_hi_s", 1)
        v_lo_s = sig("v_lo_s", 1)
        lg_psum = sig("lg_psum", 1)
        lg_shifted = sig("lg_shifted", 2)
        ex_s = sig("ex_s", 1)
        rt = sig("rt", 20)
        rank_psum = sig("rank_psum", 1)
        s_psum = sig("s_psum", U * NH)
        s_max = sig("s_max", U * NH)
        p_exp = sig("p_exp", U * NH)
        pt_psum = sig("pt_psum", U * NH)
        p_hi_s = sig("p_hi_s", U * NH)
        p_lo_s = sig("p_lo_s", U * NH)
        pv_done = sig("pv_done", NH)
        o_sum = sig("o_sum", 1)
        o_ready = sig("o_ready", 2)
        oT_psum = sig("oT_psum", DC)
        oT_hi_s = sig("oT_hi_s", DC)
        oT_lo_s = sig("oT_lo_s", DC)
        proj_psum = sig("proj_psum", 2)
        x1_ready = sig("x1_ready", 2)
        x1_stored = sig("x1_stored", 16)

        def rows(t, b):
            return t[bass.ds(b * S, S), :].rearrange("(t p) d -> p t d", p=P)

        def pipeline(eng, prologue, step, epilogue):
            prologue()
            step(0, 0, False, True)
            with eng.Fori(0, NB // 2 - 1) as i:
                for u in (1, 0):
                    step(2 * i + 2 - u, u, True, True)
            step(NB - 1, 1, True, False)
            epilogue()

        def score_bank(h, n):
            return bank[(U * h + n) % 2]

        def prob_bank(h, n):
            return bank[2 + n]

        out_bank = (bank[5], bank[6])
        turn = bank[7]

        block = ctx.enter_context(nc.Block())

        @block.sync
        def _(sp):
            sp.dma_start(xr[:, :, :], rows(x, 0)).then_inc(x_loaded.sem, 16)
            sp.dma_start(wqkv32[:, :, :], w["wqkv"].rearrange("(c p) n -> p c n", p=P)).then_inc(w_loaded.sem, 16)
            sp.dma_start(gate32[:, :, :], w["gate0"].rearrange("(c p) n -> p c n", p=P)).then_inc(w_loaded.sem, 16)
            sp.dma_start(wout32[:, :, :], w["wout"].rearrange("(c p) n -> p c n", p=P)).then_inc(w_loaded.sem, 16)
            sp.dma_start(bqk[:, :], w["bqk"]).then_inc(w_loaded.sem, 16)
            sp.dma_start(bv_row[:, :], w["bv"].partition_broadcast(P)).then_inc(w_loaded.sem, 16)
            sp.dma_start(bout_row[:, :], w["bout"].partition_broadcast(P)).then_inc(w_loaded.sem, 16)
            sp.dma_start(gateb_row[:, :], w["gate_b"].partition_broadcast(P)).then_inc(w_loaded.sem, 16)

            def store_xn(b):
                sp.wait_ge(xn_ready.sem, xn_ready.at(b))
                sp.dma_start(rows(dram["xn"], b), xn[:, :, :]).then_inc(xn_stored.sem, 16)

            def store_x1(b):
                sp.wait_ge(x1_ready.sem, x1_ready.at(b))
                sp.dma_start(rows(dram["x1"], b), x1[:, :, :]).then_inc(x1_stored.sem, 16)

            def load_stacks(b, u):
                sp.wait_ge(qk_hi_s.sem, qk_hi_s.at(b))
                sp.dma_start(dram["qk_hi"].rearrange("(m p) s -> p m s", p=P), qk_hi[:, :, :]).then_inc(qk_stored.sem, 16)
                sp.wait_ge(q_lo_s.sem, q_lo_s.at(b))
                sp.wait_ge(k_lo_s.sem, k_lo_s.at(b))
                sp.dma_start(dram["qk_lo"].rearrange("(m p) s -> p m s", p=P), qk_lo[:, :, :]).then_inc(qk_stored.sem, 16)
                sp.wait_ge(qk_stored.sem, qk_stored.at(b))
                sp.wait_ge(s_psum.sem, s_psum.at(b - 2))
                hi = dram["qk_hi"].rearrange("(m h d) s -> m d h s", m=2, d=HD)
                lo = dram["qk_lo"].rearrange("(m h d) s -> m d h s", m=2, d=HD)
                for r, (q, k) in enumerate(((hi, hi), (hi, lo), (lo, hi))):
                    sp.dma_start(q_stack[HD * r:HD * r + HD, u, :, :], q[0]).then_inc(stacks_loaded.sem, 16)
                    sp.dma_start(k_stack[HD * r:HD * r + HD, u, :, :], k[1]).then_inc(stacks_loaded.sem, 16)

            def prologue():
                sp.wait_ge(filled.sem, 3)
                for u in range(2):
                    for stack in (q_stack, k_stack):
                        sp.dma_start(stack[3 * HD:STK, u, :, :],
                                     zeros16[3 * HD:STK, :].unsqueeze(1).to_broadcast([STK - 3 * HD, NH, S])).then_inc(stacks_filled.sem, 16)
                store_xn(0)
                load_stacks(0, 0)

            def step(b, u, before, more):
                if more:
                    sp.wait_ge(xb_ready.sem, xb_ready.at(b))
                    sp.dma_start(xr[:, :, :], rows(x, b + 1)).then_inc(x_loaded.sem, 16)
                if before:
                    store_x1(b - 1)
                if more:
                    store_xn(b + 1)
                    load_stacks(b + 1, 1 - u)
                if is_int(b, 0):
                    tail = dram["y"][USED_TILES * ETOK:MAX_TILES * ETOK, :].rearrange("(p c) d -> p c d", p=P)
                    sp.dma_start(tail, zeros_f[:, :].unsqueeze(1).to_broadcast([P, (MAX_TILES - USED_TILES) * ETOK // P, D])).then_inc(tail_filled.sem, 16)

            def epilogue():
                store_x1(NB - 1)
                sp.wait_ge(tail_filled.sem, tail_filled.at(0))
                sp.wait_ge(x1_stored.sem, x1_stored.at(NB - 1))
                sp.wait_ge(xn_stored.sem, xn_stored.at(NB - 1))

            pipeline(sp, prologue, step, epilogue)

        @block.gpsimd
        def _(pool):
            pool.memset(minus_half[:, :], -0.5).then_inc(filled.sem, 1)
            pool.memset(zeros16[:, :], 0.0).then_inc(filled.sem, 1)
            pool.memset(zeros_f[:, :], 0.0).then_inc(filled.sem, 1)
            pool.wait_ge(filled.sem, 3)

            def project(b, u):
                pool.wait_ge(dve_ln.sem, dve_ln.at(b))
                pool.tensor_tensor(var_eps[:, :], mv[:, :, 1], consts["eps_col"][:, 0:TT], ALU.add).then_inc(rstd_s.sem, 1)
                pool.wait_ge(rstd_s.sem, rstd_s.at(b, 1))
                pool.tensor_tensor(rstd[:, :], var_eps[:, :], minus_half[:, :], ALU.pow).then_inc(rstd_s.sem, 1)
                pool.wait_ge(x1_ready.sem, x1_ready.at(b - 2))
                pool.wait_ge(xn_ready.sem, xn_ready.at(b))
                if isinstance(b, int):
                    pool.wait_ge(w_loaded.sem, w_loaded.at(0))
                pool.tensor_tensor(xb[:, u, :, :], xr[:, :, :], bout_row[:, :].unsqueeze(1).to_broadcast([P, TT, D]),
                                   ALU.add).then_inc(xb_ready.sem, 1)
                for m in range(2):
                    pool.wait_ge(qk_hi_s.sem, qk_hi_s.at(b, m + 1))
                    pool.tensor_tensor(qk_lo[:, m, :], q32[:, m, :], qk_hi[:, m, :], ALU.subtract).then_inc(q_lo_s.sem, 1)
                pool.wait_ge(v_hi_s.sem, v_hi_s.at(b))
                pool.tensor_tensor(v_lo[:, u, :, :, :], v32[:, :, :].rearrange("p t (h d) -> p t h d", h=NH),
                                   v_hi[:, u, :, :, :], ALU.subtract).then_inc(v_lo_s.sem, 1)

            def step(b, u, before, more):
                if more:
                    project(b + 1, 1 - u)

            pipeline(pool, lambda: project(0, 0), step, lambda: None)

        @block.scalar
        def _(act):
            act.wait_ge(w_loaded.sem, w_loaded.at(0))
            act.activation(wqkv_hi[:, :, :], wqkv32[:, :, :], ACT.Copy).then_inc(w_hi.sem, 1)
            act.activation(gate_hi[:, :, :], gate32[:, :, :], ACT.Copy).then_inc(w_hi.sem, 1)
            act.activation(wout_hi[:, :, :], wout32[:, :, :], ACT.Copy).then_inc(w_hi.sem, 1)
            act.wait_ge(bq_scaled.sem, 1)

            def x_high(b, c):
                act.wait_ge(xT_psum.sem, xT_psum.at(b, c + 1))
                act.wait_ge(lg_psum.sem, lg_psum.at(b - 1))
                act.activation(xT_hi[:, c, :], turn[:, :], ACT.Copy).then_inc(xT_hi_s.sem, 1)

            def q_scaled(b, m):
                act.wait_ge(qk_psum.sem, qk_psum.at(b, m + 1))
                act.wait_ge(q_lo_s.sem, q_lo_s.at(b - 1))
                act.activation(q32[:, m, :], turn[:, :], ACT.Identity, bias=bq[:, m:m + 1],
                               scale=HD ** -0.5).then_inc(q32_s.sem, 1)

            def q_high(b, m):
                act.wait_ge(q32_s.sem, q32_s.at(b, m + 1))
                act.wait_ge(qk_stored.sem, qk_stored.at(b - 1))
                act.activation(qk_hi[:, m, :], q32[:, m, :], ACT.Copy).then_inc(qk_hi_s.sem, 1)

            def k_high(b, m):
                act.wait_ge(qk_psum.sem, qk_psum.at(b, m + 3))
                act.activation(qk_hi[:, 2 + m, :], turn[:, :], ACT.Identity, bias=bqk[:, 2 + m:3 + m]).then_inc(qk_hi_s.sem, 1)

            def v_high(b, u):
                act.wait_ge(v32_s.sem, v32_s.at(b))
                act.wait_ge(pv_done.sem, pv_done.at(b - 2))
                act.activation(v_hi[:, u, :, :, :], v32[:, :, :].rearrange("p t (h d) -> p t h d", h=NH),
                               ACT.Copy).then_inc(v_hi_s.sem, 1)

            def router_exp(b):
                act.wait_ge(lg_shifted.sem, lg_shifted.at(b))
                act.activation(ex[:, :, :], lg[:, :, :], ACT.Exp).then_inc(ex_s.sem, 1)

            def out_high(b, c):
                act.wait_ge(oT_psum.sem, oT_psum.at(b, c + 1))
                act.wait_ge(proj_psum.sem, proj_psum.at(b - 1))
                act.activation(oT_hi[:, c, :], turn[:, :], ACT.Copy).then_inc(oT_hi_s.sem, 1)

            def exps(b, u, h, n):
                act.wait_ge(s_max.sem, s_max.at(b, U * h + n + 1))
                if h == 0 and n == 0:
                    act.wait_ge(o_ready.sem, o_ready.at(b - 2))
                for j in Q_UNITS[n]:
                    at = QOFF[j] - QOFF[Q_UNITS[n][0]]
                    ins = act.activation(p32[:, h % 2, QOFF[j]:QOFF[j] + (j + 1) * P], score_bank(h, n)[:, at:at + (j + 1) * P],
                                         ACT.Exp, bias=neg_max[:, h % 2, j:j + 1], accum_out=row_sum[:, u, j, h:h + 1])
                ins.then_inc(p_exp.sem, 1)

            def prob_high(b, h, n):
                act.wait_ge(pt_psum.sem, pt_psum.at(b, U * h + n + 1))
                if n == 0:
                    act.wait_ge(pv_done.sem, pv_done.at(b, h - 1))
                first, last = K_UNITS[n][0], K_UNITS[n][-1]
                cols = slice(KOFF[first], KOFF[last] + (TT - last) * P)
                act.activation(p_hi[:, h % 2, cols], prob_bank(h, n)[:, 0:cols.stop - cols.start], ACT.Copy).then_inc(p_hi_s.sem, 1)

            def prologue():
                for c in range(DC):
                    x_high(0, c)
                for m in range(2):
                    q_scaled(0, m)
                for m in range(2):
                    q_high(0, m)
                for m in range(2):
                    k_high(0, m)
                v_high(0, 0)
                router_exp(0)
                for n in range(U):
                    exps(0, 0, 0, n)

            def pieces(b, u, at, before, more):
                if before and at - 1 in AT_OUT_T:
                    out_high(b - 1, AT_OUT_T.index(at - 1))
                if more:
                    if at - 1 in AT_X_T:
                        x_high(b + 1, AT_X_T.index(at - 1))
                    if at - 1 in AT_Q:
                        q_scaled(b + 1, AT_Q.index(at - 1))
                    if at - 2 in AT_Q:
                        q_high(b + 1, AT_Q.index(at - 2))
                    if at - 1 in AT_K:
                        k_high(b + 1, AT_K.index(at - 1))
                    if at - 3 == AT_V[1]:
                        v_high(b + 1, 1 - u)
                    if at - 3 == AT_LOGITS:
                        router_exp(b + 1)

            def step(b, u, before, more):
                for h in range(NH):
                    for n in range(U):
                        if h + 1 < NH:
                            exps(b, u, h + 1, n)
                        elif more:
                            exps(b + 1, 1 - u, 0, n)
                        prob_high(b, h, n)
                        pieces(b, u, U * h + n, before, more)

            def epilogue():
                for c in range(DC):
                    out_high(NB - 1, c)

            pipeline(act, prologue, step, epilogue)

        @block.vector
        def _(dve):
            dve.memset(run[:, 0, :], 0.0).then_inc(run_cleared.sem, 1)
            dve.wait_ge(run_cleared.sem, run_cleared.at(0))

            def norm_stats(b):
                dve.wait_ge(x_loaded.sem, x_loaded.at(b))
                for t in range(TT):
                    st = dve.bn_stats(stats[:, t, :], xr[:, t, :])
                st.then_inc(dve_ln.sem, 1)
                dve.wait_ge(rstd_s.sem, rstd_s.at(b - 1))
                dve.wait_ge(dve_ln.sem, dve_ln.at(b, 1))
                dve.nop(nofuse=True)
                for t in range(TT):
                    st = dve.bn_aggr(mv[:, t, :], stats[:, t, :])
                st.then_inc(dve_ln.sem, 1)

            def normalise(b):
                dve.wait_ge(dve_ln.sem, dve_ln.at(b))
                dve.wait_ge(rstd_s.sem, rstd_s.at(b))
                dve.wait_ge(xT_psum.sem, xT_psum.at(b - 1))
                dve.wait_ge(xn_stored.sem, xn_stored.at(b - 1))
                for t in range(TT):
                    st = dve.tensor_scalar(xn[:, t, :], xr[:, t, :], mv[:, t, 0:1], rstd[:, t:t + 1],
                                           ALU.subtract, ALU.mult)
                st.then_inc(xn_ready.sem, 1)

            def x_low(b, c):
                dve.wait_ge(xT_hi_s.sem, xT_hi_s.at(b, c + 1))
                dve.tensor_tensor(xT_lo[:, c, :], turn[:, :], xT_hi[:, c, :], ALU.subtract).then_inc(xT_lo_s.sem, 1)

            def k_low(b, m):
                dve.wait_ge(qk_hi_s.sem, qk_hi_s.at(b, m + 3))
                dve.scalar_tensor_tensor(qk_lo[:, 2 + m, :], turn[:, :], bqk[:, 2 + m:3 + m], qk_hi[:, 2 + m, :],
                                         ALU.add, ALU.subtract).then_inc(k_lo_s.sem, 1)

            def v_bias(b, g):
                dve.wait_ge(v_lo_s.sem, v_lo_s.at(b - 1))
                dve.wait_ge(v_psum.sem, v_psum.at(b, g + 1))
                dve.tensor_tensor(v32[:, 2 * g:2 * g + 2, :], turn[:, :].rearrange("p (t n) -> p t n", t=2),
                                  bv_row[:, :].unsqueeze(1).to_broadcast([P, 2, D]), ALU.add).then_inc(v32_s.sem, 1)

            def done(b, n, ins):
                ins.then_inc(rt.sem, 1)
                dve.wait_ge(rt.sem, rt.at(b, n))

            def router_shift(b):
                dve.wait_ge(lg_psum.sem, lg_psum.at(b))
                lgp = turn[:, 0:TT * E].rearrange("p (t e) -> p t e", e=E)
                dve.tensor_reduce(lmax[:, :], lgp, AX.X, ALU.max).then_inc(lg_shifted.sem, 1)
                dve.wait_ge(lg_shifted.sem, lg_shifted.at(b, 1))
                dve.tensor_tensor(lg[:, :, :], lgp, lmax[:, :].unsqueeze(2).to_broadcast([P, TT, E]),
                                  ALU.subtract).then_inc(lg_shifted.sem, 1)

            def router_scores(b, part):
                if part == 0:
                    dve.wait_ge(ex_s.sem, ex_s.at(b))
                    done(b, 1, dve.tensor_reduce(exs[:, :], ex[:, :, :], AX.X, ALU.add))
                    done(b, 2, dve.reciprocal(exs[:, :], exs[:, :]))
                else:
                    done(b, 3, dve.tensor_tensor(scores[:, :, :], ex[:, :, :],
                                                 exs[:, :].unsqueeze(2).to_broadcast([P, TT, E]), ALU.mult))
                    done(b, 4, dve.tensor_tensor(biased[:, :, :], scores[:, :, :],
                                                 gateb_row[:, :].unsqueeze(1).to_broadcast([P, TT, E]), ALU.add))

            def router_choice(b, part):
                if part == 0:
                    for t in range(TT):
                        mx = dve.max(top[:, t, :], biased[:, t, :])
                    done(b, 5, mx)
                    dve.nop(nofuse=True)
                    for t in range(TT):
                        mx = dve.max_index(topi[:, t, :], top[:, t, :], biased[:, t, :])
                    done(b, 6, mx)
                else:
                    for k in range(2):
                        oh = dve.tensor_tensor(onehot[:, :, k, :], iota8[:, :].unsqueeze(1).to_broadcast([P, TT, E]),
                                               topi[:, :, k:k + 1].to_broadcast([P, TT, E]), ALU.is_equal)
                    done(b, 7, oh)
                    done(b, 8, dve.tensor_tensor(member[:, :, :], onehot[:, :, 0, :], onehot[:, :, 1, :], ALU.add))

            def router_weights(b):
                for k in range(2):
                    oh = dve.tensor_tensor(picked[:, :, k, :], onehot[:, :, k, :], scores[:, :, :], ALU.mult)
                done(b, 9, oh)
                done(b, 10, dve.tensor_reduce(route["weights"][:, bass.ds(b * TT, TT), :], picked[:, :, :, :], AX.X, ALU.add))

            def router_ranks(b, part):
                if part == 0:
                    dve.wait_ge(rank_psum.sem, rank_psum.at(b))
                    done(b, 11, dve.tensor_copy(tot[:, :, :, :], turn[:, 0:2 * TT * E].rearrange("p (k t e) -> p k t e", k=2, e=E)))
                elif part <= 2:
                    for t in (2 * part - 2, 2 * part - 1):
                        done(b, 12 + t, dve.tensor_tensor(run[:, t + 1, :], run[:, t, :], tot[:, 1, t, :], ALU.add))
                elif part == 3:
                    done(b, 16, dve.tensor_tensor(ranks[:, :, :], tot[:, 0, :, :], run[:, 0:TT, :], ALU.add))
                    for k in range(2):
                        oh = dve.tensor_tensor(picked[:, :, k, :], onehot[:, :, k, :], ranks[:, :, :], ALU.mult)
                    done(b, 17, oh)
                elif part == 4:
                    done(b, 18, dve.tensor_reduce(route["rank"][:, bass.ds(b * TT, TT), :], picked[:, :, :, :], AX.X, ALU.add))
                else:
                    done(b, 19, dve.tensor_copy(route["onehot"][:, bass.ds(b * TT, TT), :, :], onehot[:, :, :, :]))
                    done(b, 20, dve.tensor_copy(run[:, 0, :], run[:, TT, :]))

            def divide(b, u):
                dve.wait_ge(pv_done.sem, pv_done.at(b))
                dve.wait_ge(oT_psum.sem, oT_psum.at(b - 1))
                dve.reciprocal(row_sum[:, u, :, :], row_sum[:, u, :, :]).then_inc(o_sum.sem, 1)
                dve.wait_ge(o_sum.sem, o_sum.at(b))
                for g in range(2):
                    dve.tensor_tensor(o_rows[:, 2 * g:2 * g + 2, :].rearrange("p t (h d) -> p (t h) d", h=NH),
                                      out_bank[g][:, :].rearrange("p (t d) -> p t d", d=HD),
                                      row_sum[:, u, 2 * g:2 * g + 2, :].rearrange("p t h -> p (t h)").unsqueeze(2).to_broadcast([P, 2 * NH, HD]),
                                      ALU.mult).then_inc(o_ready.sem, 1)

            def out_low(b, c):
                dve.wait_ge(oT_hi_s.sem, oT_hi_s.at(b, c + 1))
                dve.tensor_tensor(oT_lo[:, c, :], turn[:, :], oT_hi[:, c, :], ALU.subtract).then_inc(oT_lo_s.sem, 1)

            def residual(b, u, g):
                dve.wait_ge(x1_stored.sem, x1_stored.at(b - 1))
                dve.wait_ge(proj_psum.sem, proj_psum.at(b, g + 1))
                dve.tensor_tensor(x1[:, 2 * g:2 * g + 2, :], turn[:, :].rearrange("p (t n) -> p t n", t=2),
                                  xb[:, u, 2 * g:2 * g + 2, :], ALU.add).then_inc(x1_ready.sem, 1)

            def maxima(b, h, n):
                dve.wait_ge(s_psum.sem, s_psum.at(b, U * h + n + 1))
                for j in Q_UNITS[n]:
                    at = QOFF[j] - QOFF[Q_UNITS[n][0]]
                    ins = dve.tensor_reduce(neg_max[:, h % 2, j:j + 1], score_bank(h, n)[:, at:at + (j + 1) * P], AX.X,
                                            ALU.max, negate=True)
                ins.then_inc(s_max.sem, 1)

            def prob_low(b, h, n):
                dve.wait_ge(p_hi_s.sem, p_hi_s.at(b, U * h + n + 1))
                first, last = K_UNITS[n][0], K_UNITS[n][-1]
                cols = slice(KOFF[first], KOFF[last] + (TT - last) * P)
                dve.tensor_tensor(p_lo[:, h % 2, cols], prob_bank(h, n)[:, 0:cols.stop - cols.start], p_hi[:, h % 2, cols],
                                  ALU.subtract).then_inc(p_lo_s.sem, 1)

            def prologue():
                norm_stats(0)
                normalise(0)
                dve.wait_ge(w_loaded.sem, w_loaded.at(0))
                dve.tensor_scalar(bq[:, :], bqk[:, 0:2], HD ** -0.5, None, ALU.mult).then_inc(bq_scaled.sem, 1)
                dve.wait_ge(w_hi.sem, 1)
                dve.tensor_tensor(wqkv_lo[:, :, :], wqkv32[:, :, :], wqkv_hi[:, :, :], ALU.subtract).then_inc(w_lo.sem, 1)
                dve.wait_ge(w_hi.sem, 2)
                dve.tensor_tensor(gate_lo[:, :, :], gate32[:, :, :], gate_hi[:, :, :], ALU.subtract).then_inc(w_lo.sem, 1)
                dve.wait_ge(w_hi.sem, 3)
                dve.tensor_tensor(wout_lo[:, :, :], wout32[:, :, :], wout_hi[:, :, :], ALU.subtract).then_inc(w_lo.sem, 1)
                for c in range(DC):
                    x_low(0, c)
                for m in range(2):
                    k_low(0, m)
                for g in range(2):
                    v_bias(0, g)
                router_shift(0)
                for n in range(U):
                    maxima(0, 0, n)

            def pieces(b, u, at, before, more):
                for when, part in ((AT_SCORES, router_scores), (AT_CHOICE, router_choice), (AT_RANKS, router_ranks)):
                    if at in when:
                        part(b, when.index(at))
                if at == AT_WEIGHTS:
                    router_weights(b)
                if before:
                    if at == AT_DIVIDE:
                        divide(b - 1, 1 - u)
                    if at - 2 in AT_OUT_T:
                        out_low(b - 1, AT_OUT_T.index(at - 2))
                    if at - 2 in AT_PROJ:
                        residual(b - 1, 1 - u, AT_PROJ.index(at - 2))
                if more:
                    if at == AT_STATS:
                        norm_stats(b + 1)
                    if at == AT_NORM:
                        normalise(b + 1)
                    if at - 2 in AT_X_T:
                        x_low(b + 1, AT_X_T.index(at - 2))
                    if at - 2 in AT_K:
                        k_low(b + 1, AT_K.index(at - 2))
                    if at - 2 in AT_V:
                        v_bias(b + 1, AT_V.index(at - 2))
                    if at - 2 == AT_LOGITS:
                        router_shift(b + 1)

            def step(b, u, before, more):
                for h in range(NH):
                    for n in range(U):
                        if h + 1 < NH or more:
                            maxima(b, h + 1, n)
                        if n >= LAG:
                            prob_low(b, h, n - LAG)
                        elif h >= 1 or before:
                            prob_low(b, h - 1, n - LAG + U)
                        pieces(b, u, U * h + n, before, more)

            def epilogue():
                for n in range(U - LAG, U):
                    prob_low(NB - 1, NH - 1, n)
                divide(NB - 1, 1)
                for c in range(DC):
                    out_low(NB - 1, c)
                for g in range(2):
                    residual(NB - 1, 1, g)

            pipeline(dve, prologue, step, epilogue)

        @block.tensor
        def _(pe):
            def x_transposes(b, c):
                if c == 0:
                    pe.wait_ge(xn_ready.sem, xn_ready.at(b))
                    pe.wait_ge(rt.sem, rt.at(b - 1, 11))
                else:
                    pe.wait_ge(xT_lo_s.sem, xT_lo_s.at(b, 1))
                for t in range(TT):
                    mm = pe.transpose(turn[:, t * P:(t + 1) * P], xn[:, t, c * P:(c + 1) * P], identf[:, :])
                mm.then_inc(xT_psum.sem, 1)

            def qk_products(b, m):
                if m == 0:
                    pe.wait_ge(xT_lo_s.sem, xT_lo_s.at(b))
                elif m <= 2:
                    pe.wait_ge(q32_s.sem, q32_s.at(b, m))
                else:
                    pe.wait_ge(k_lo_s.sem, k_lo_s.at(b, 1))
                cols = slice(m * P, (m + 1) * P)
                three_products(pe, turn[:, :], lambda c: wqkv_hi[:, c, cols], lambda c: wqkv_lo[:, c, cols],
                               lambda c: xT_hi[:, c, :], lambda c: xT_lo[:, c, :], range(DC)).then_inc(qk_psum.sem, 1)

            def v_products(b, g):
                if g == 0:
                    pe.wait_ge(k_lo_s.sem, k_lo_s.at(b))
                else:
                    pe.wait_ge(v32_s.sem, v32_s.at(b, 1))
                for t in (2 * g, 2 * g + 1):
                    tok = slice(t * P, (t + 1) * P)
                    mm = three_products(pe, turn[:, (t % 2) * D:(t % 2 + 1) * D],
                                        lambda c: xT_hi[:, c, tok], lambda c: xT_lo[:, c, tok],
                                        lambda c: wqkv_hi[:, c, 2 * D:3 * D], lambda c: wqkv_lo[:, c, 2 * D:3 * D], range(DC))
                mm.then_inc(v_psum.sem, 1)

            def logits(b):
                pe.wait_ge(v32_s.sem, v32_s.at(b))
                for t in range(TT):
                    tok = slice(t * P, (t + 1) * P)
                    mm = three_products(pe, turn[:, t * E:(t + 1) * E], lambda c: xT_hi[:, c, tok], lambda c: xT_lo[:, c, tok],
                                        lambda c: gate_hi[:, c, :], lambda c: gate_lo[:, c, :], range(DC))
                mm.then_inc(lg_psum.sem, 1)

            def rank_sums(b, before):
                if before:
                    pe.wait_ge(x1_ready.sem, x1_ready.at(b - 1))
                pe.wait_ge(rt.sem, rt.at(b, 8))
                m = member[:, :, :].rearrange("p t e -> p (t e)")
                pe.matmul(turn[:, 0:TT * E], tri[:, :], m, start=True, stop=True)
                pe.matmul(turn[:, TT * E:2 * TT * E], ones_b[:, :], m, start=True, stop=True).then_inc(rank_psum.sem, 1)

            def scores_of(b, u, h, n):
                if h == 0 and n == 0:
                    pe.wait_ge(stacks_loaded.sem, stacks_loaded.at(b))
                if not (h == 0 and n < 2 and isinstance(b, int) and b == 0):
                    pe.wait_ge(p_exp.sem, p_exp.at(b, U * h + n - 1))
                for j in Q_UNITS[n]:
                    at = QOFF[j] - QOFF[Q_UNITS[n][0]]
                    pe.matmul(score_bank(h, n)[:, at:at + (j + 1) * P], q_stack[0:STK, u, h, j * P:(j + 1) * P],
                              k_stack[0:STK, u, h, 0:(j + 1) * P], start=True, stop=False)
                    mm = pe.matmul(score_bank(h, n)[:, at + j * P:at + (j + 1) * P], identb[:, :], maskadd[:, :],
                                   start=False, stop=True)
                mm.then_inc(s_psum.sem, 1)

            def prob_transposes(b, h, n):
                if n == 0:
                    pe.wait_ge(p_exp.sem, p_exp.at(b, U * h + U))
                if not (h == 0 and isinstance(b, int) and b == 0):
                    pe.wait_ge(p_lo_s.sem, p_lo_s.at(b, U * h + n - 2))
                for k in K_UNITS[n]:
                    for j in range(k, TT):
                        at = KOFF[k] - KOFF[K_UNITS[n][0]] + (j - k) * P
                        mm = pe.transpose(prob_bank(h, n)[:, at:at + P], p32[:, h % 2, QOFF[j] + k * P:QOFF[j] + (k + 1) * P],
                                          identf[:, :])
                mm.then_inc(pt_psum.sem, 1)

            def values(b, u, h, before):
                if h == 0:
                    pe.wait_ge(v_lo_s.sem, v_lo_s.at(b))
                    if before:
                        pe.wait_ge(o_ready.sem, o_ready.at(b - 1))
                pe.wait_ge(p_lo_s.sem, p_lo_s.at(b, U * h + U))
                for j in range(TT):
                    out = out_bank[j // 2][:, (j % 2) * D + h * HD:(j % 2) * D + (h + 1) * HD]
                    for k in range(j + 1):
                        cols = slice(KOFF[k] + (j - k) * P, KOFF[k] + (j - k + 1) * P)
                        pe.matmul(out, p_hi[:, h % 2, cols], v_hi[:, u, k, h, :], start=k == 0, stop=False)
                        pe.matmul(out, p_hi[:, h % 2, cols], v_lo[:, u, k, h, :], start=False, stop=False)
                        mm = pe.matmul(out, p_lo[:, h % 2, cols], v_hi[:, u, k, h, :], start=False, stop=k == j)
                mm.then_inc(pv_done.sem, 1)

            def out_transposes(b, c):
                if c == 0:
                    pe.wait_ge(o_ready.sem, o_ready.at(b))
                    pe.wait_ge(lg_shifted.sem, lg_shifted.at(NB - 1 if is_int(b, NB - 1) else b + 1))
                else:
                    pe.wait_ge(oT_lo_s.sem, oT_lo_s.at(b, 1))
                for t in range(TT):
                    mm = pe.transpose(turn[:, t * P:(t + 1) * P], o_rows[:, t, c * P:(c + 1) * P], identf[:, :])
                mm.then_inc(oT_psum.sem, 1)

            def out_products(b, g):
                if g == 0:
                    pe.wait_ge(oT_lo_s.sem, oT_lo_s.at(b))
                else:
                    pe.wait_ge(x1_ready.sem, x1_ready.at(b, 1))
                for t in (2 * g, 2 * g + 1):
                    tok = slice(t * P, (t + 1) * P)
                    mm = three_products(pe, turn[:, (t % 2) * D:(t % 2 + 1) * D],
                                        lambda c: oT_hi[:, c, tok], lambda c: oT_lo[:, c, tok],
                                        lambda c: wout_hi[:, c, :], lambda c: wout_lo[:, c, :], range(DC))
                mm.then_inc(proj_psum.sem, 1)

            def prologue():
                for c in range(DC):
                    x_transposes(0, c)
                pe.wait_ge(w_lo.sem, 3)
                for m in range(4):
                    qk_products(0, m)
                for g in range(2):
                    v_products(0, g)
                logits(0)
                pe.wait_ge(stacks_filled.sem, stacks_filled.at(0))
                for n in range(U):
                    scores_of(0, 0, 0, n)

            def pieces(b, u, at, before, more):
                if at == AT_RANK_SUMS:
                    rank_sums(b, before)
                if before:
                    if at in AT_OUT_T:
                        out_transposes(b - 1, AT_OUT_T.index(at))
                    if at in AT_PROJ:
                        out_products(b - 1, AT_PROJ.index(at))
                if more:
                    if at in AT_X_T:
                        x_transposes(b + 1, AT_X_T.index(at))
                    if at in AT_Q + AT_K:
                        qk_products(b + 1, (AT_Q + AT_K).index(at))
                    if at in AT_V:
                        v_products(b + 1, AT_V.index(at))
                    if at == AT_LOGITS:
                        logits(b + 1)

            def step(b, u, before, more):
                for h in range(NH):
                    for n in range(U):
                        if h + 1 < NH:
                            scores_of(b, u, h + 1, n)
                        elif more:
                            scores_of(b + 1, 1 - u, 0, n)
                        prob_transposes(b, h, n)
                        if n == 1 and h >= 1:
                            values(b, u, h - 1, before)
                        elif n == 1 and before:
                            values(b - 1, 1 - u, NH - 1, True)
                        pieces(b, u, U * h + n, before, more)

            def epilogue():
                values(NB - 1, 1, NH - 1, True)
                for c in range(DC):
                    out_transposes(NB - 1, c)
                for g in range(2):
                    out_products(NB - 1, g)

            pipeline(pe, prologue, step, epilogue)


def constants(nc, ctx):
    def sb(name, shape, dt=F32):
        return ctx.enter_context(nc.sbuf_tensor(name, shape, dt))

    c = {"identf": sb("identf", [P, P]), "identb": sb("identb", [P, P], BF16), "ones_b": sb("ones_b", [P, P], BF16),
         "tri": sb("tri", [P, P], BF16), "maskadd": sb("maskadd", [P, P], BF16), "iota8": sb("iota8", [P, E]),
         "eps_col": sb("eps_col", [P, TT]), "zero_i": sb("zero_i", [P, 2], I32)}
    with ExitStack() as own:
        start = own.enter_context(nc.semaphore("const_start"))
        made = own.enter_context(nc.semaphore("const_made"))
        zeros = own.enter_context(nc.sbuf_tensor("zeros", [P, P], F32))
        onesf = own.enter_context(nc.sbuf_tensor("onesf", [P, P], F32))
        block = own.enter_context(nc.Block())

        @block.gpsimd
        def _(pool):
            pool.memset(zeros[:, :], 0.0).then_inc(start, 1)
            pool.memset(onesf[:, :], 1.0).then_inc(start, 1)
            pool.memset(c["ones_b"][:, :], 1.0).then_inc(made, 1)
            pool.memset(c["eps_col"][:, :], EPS).then_inc(made, 1)
            pool.memset(c["zero_i"][:, :], 0).then_inc(made, 1)
            pool.iota(c["iota8"][:, :], [[1, E]], base=0, channel_multiplier=0,
                      allow_small_or_imprecise_dtypes=True).then_inc(made, 1)
            pool.wait_ge(start, 2)
            for name in ("identf", "identb"):
                pool.affine_select(out=c[name][:, :], in_=zeros[:, :], pattern=[[-1, P]], compare_op=ALU.not_equal,
                                   fill=1.0, base=0, channel_multiplier=1).then_inc(made, 1)
            pool.affine_select(out=c["tri"][:, :], in_=onesf[:, :], pattern=[[1, P]], compare_op=ALU.is_gt,
                               fill=0.0, base=0, channel_multiplier=-1).then_inc(made, 1)
            pool.affine_select(out=c["maskadd"][:, :], in_=zeros[:, :], pattern=[[-1, P]], compare_op=ALU.is_ge,
                               fill=MASKED, base=0, channel_multiplier=1).then_inc(made, 1)
            pool.wait_ge(made, 8)
    return c


def experts_phase(nc, w, dram, consts, route, packed):
    identf, bounds, pos, tokens = consts["identf"], route["bounds"], route["pos"], route["tokens"]
    pack32, pack_hi, pack_lo = packed
    HM = len(HT)
    HALF = ETOK // P
    with ExitStack() as ctx:
        def sb(name, shape, dt=F32):
            return ctx.enter_context(nc.sbuf_tensor(name, shape, dt))

        def sig(name, per):
            return Signal(nc, ctx, name, per)

        w13_32 = sb("w13_32", [P, DC, 2 * H0])
        w2_32 = sb("w2_32", [P, HM, D])
        w13_hi, w13_lo = (sb(f"w13_{k}", [P, 2, DC, 2 * H0], F16) for k in ("hi", "lo"))
        w2_hi, w2_lo = (sb(f"w2_{k}", [P, 2, HM, D], F16) for k in ("hi", "lo"))
        b13 = sb("b13", [P, 2, 2 * HM])
        b2 = sb("b2", [P, 2, D])
        token_now = sb("token_now", [P, HALF], I32)
        xg = sb("xg", [P, HALF, D])
        xT_hi, xT_lo = (sb(f"gT_{k}", [P, DC, ETOK], F16) for k in ("hi", "lo"))
        a1 = sb("a1", [P, HM, ETOK])
        prod = sb("prod", [P, HM, ETOK])
        h32 = sb("h32", [P, HM, ETOK])
        h_hi, h_lo = (sb(f"h_{k}", [P, HM, ETOK], F16) for k in ("hi", "lo"))
        y = sb("y", [P, HALF, D])
        table_rows = sb("table_rows", [ROUTED_SLOTS // P, P], I32)
        table_f = sb("table_f", [ROUTED_SLOTS // P, P])
        steps_i = sb("steps_i", [P, MOST_TILES], I32)
        steps = sb("steps", [P, MOST_TILES])
        above = sb("above", [P, E, MOST_TILES])
        tiles = sb("tiles", [P, E])
        ones8 = sb("ones8", [P, E])
        ends = sb("ends", [P, E])
        starts = sb("starts", [P, E])
        base = sb("base", [P, T // P, 2, E])
        posf = sb("posf", [P, T // P, 2])
        zeros_i = sb("zeros_i", [P, ROUTED_SLOTS // P], I32)
        bank = [ctx.enter_context(nc.psum_tensor(f"xbank{i}", [P, 512], F32)) for i in range(6)]

        e_loaded = sig("e_loaded", 16 * 5)
        e_hi = sig("e_hi", 3)
        e_lo = sig("e_lo", 3)
        token_now_s = sig("token_now_s", 1)
        gathered = sig("gathered", 16 * HALF)
        x_loaded = sig("tile_loaded", 16 * HALF)
        gT_psum = sig("gT_psum", 1)
        gT_hi_s = sig("gT_hi_s", 1)
        gT_lo_s = sig("gT_lo_s", 1)
        gu_psum = sig("gu_psum", HM)
        a1_s = sig("a1_s", HM)
        prod_s = sig("prod_s", HM)
        h32_s = sig("h32_s", HM)
        h_hi_s = sig("h_hi_s", HM)
        h_lo_s = sig("h_lo_s", HM)
        y_psum = sig("y_psum", 1)
        y_ready = sig("y_ready", 1)
        y_stored = sig("y_stored", 16)
        scattered = sig("scattered", 16 * 2 * T // P)
        table_loaded = sig("table_loaded", 16)
        table_f_s = sig("table_f_s", 1)
        table_psum = sig("table_psum", 1)
        tokens_s = sig("tokens_s", 1)
        made = sig("slot_made", 4)
        slots = sig("slots", 11)
        zeroed = sig("table_zeroed", 16)
        pack_loaded = sig("pack_loaded", 16)
        pack_hi_s = sig("pack_hi_s", 1)
        pack_lo_s = sig("pack_lo_s", 1)

        def over_experts(eng, prologue, new_expert, tile, after_first, table):
            prologue()
            new_expert(0, 0, 0)
            tile(0, 0, True)
            after_first(0, 0, 0)
            with eng.Fori(1, SHARED_TILES - AHEAD) as i:
                tile(i, 0, True)
            table()
            for i in range(SHARED_TILES - AHEAD, SHARED_TILES):
                tile(i, 0, False)
            eng.wait_ge(slots.sem, slots.at(0))
            with eng.Fori(0, E // 2) as half:
                for k in range(2):
                    first = eng.value_load(bounds[0:1, bass.ds(2 * half + k, 1)], min_val=0, max_val=ROUTED_TILES - MIN_TILES)
                    end = eng.value_load(bounds[0:1, bass.ds(2 * half + k + 1, 1)], min_val=MIN_TILES, max_val=ROUTED_TILES)
                    new_expert(2 * half + k + 1, 1 - k, first + SHARED_TILES)
                    tile(first + SHARED_TILES, 1 - k, False)
                    after_first(2 * half + k + 1, 1 - k, first + SHARED_TILES)
                    with eng.Fori(first + 1, end) as r:
                        tile(r + SHARED_TILES, 1 - k, False)

        block = ctx.enter_context(nc.Block())

        @block.sync
        def _(sp):
            def load_expert(e, u, first):
                sp.wait_ge(e_hi.sem, e_hi.at(e, 0))
                sp.wait_ge(e_lo.sem, e_lo.at(e, 0))
                sp.nop(nofuse=True)
                sp.wait_ge(y_ready.sem, y_ready.at(first, 0))
                d = e if isinstance(e, int) else bass.ds(e, 1)
                row = (lambda t: t[e]) if isinstance(e, int) else (lambda t: t[bass.ds(e, 1)].rearrange("a m n -> (a m) n"))
                sp.dma_start(w13_32[:, :, :], row(w["w13"]).rearrange("(c p) n -> p c n", p=P)).then_inc(e_loaded.sem, 16)
                sp.dma_start(w2_32[:, 0:2, :], row(w["w2"])[0:2 * P, :].rearrange("(m p) n -> p m n", p=P)).then_inc(e_loaded.sem, 16)
                sp.dma_start(w2_32[0:HT[2][1], 2, :], row(w["w2"])[2 * P:H0, :]).then_inc(e_loaded.sem, 16)
                sp.dma_start(b13[:, u, :], row(w["b13"])).then_inc(e_loaded.sem, 16)
                sp.dma_start(b2[:, u, :], row(w["b2"])[0].partition_broadcast(P)).then_inc(e_loaded.sem, 16)

            def new_expert(e, u, first):
                load_expert(e + 1, 1 - u, first)

            def load_x(i):
                sp.wait_ge(gT_psum.sem, gT_psum.at(i, 0))
                for half in range(HALF):
                    sp.dma_start(xg[:, half, :], dram["xn"][bass.ds(i * ETOK + half * P, P), :]).then_inc(x_loaded.sem, 16)

            def tile(i, u, ahead):
                if ahead:
                    load_x(i + AHEAD)
                    if not is_int(i, 0):
                        sp.wait_ge(pack_loaded.sem, pack_loaded.at(i - 1))
                    cols = bass.ds(i * PACK_PART, PACK_PART)
                    sp.dma_start(pack32[:, cols], w["pack"][:, cols]).then_inc(pack_loaded.sem, 16)
                sp.wait_ge(y_ready.sem, y_ready.at(i))
                sp.dma_start(dram["y"][bass.ds(i * ETOK, ETOK), :].rearrange("(t p) d -> p t d", p=P),
                             y[:, :, :]).then_inc(y_stored.sem, 16)

            def table():
                sp.wait_ge(scattered.sem, scattered.at(0))
                sp.dma_start(table_rows[:, :], route["table"].rearrange("(c p) o -> c (p o)", p=P)).then_inc(table_loaded.sem, 16)

            def prologue():
                load_expert(0, 0, 0)
                load_x(0)
                sp.wait_ge(made.sem, made.at(0))
                sp.dma_start(route["table"].rearrange("(p c) o -> p (c o)", p=P), zeros_i[:, :]).then_inc(zeroed.sem, 16)
                load_x(1)

            over_experts(sp, prologue, new_expert, tile, lambda e, u, first: None, table)
            last = sp.value_load(bounds[0:1, E:E + 1], min_val=MIN_TILES, max_val=ROUTED_TILES)
            sp.wait_ge(y_stored.sem, y_stored.at(last + SHARED_TILES, 0))
            sp.nop(nofuse=True)

        @block.gpsimd
        def _(pool):
            def gather(i):
                pool.wait_ge(gT_psum.sem, gT_psum.at(i, 0))
                pool.wait_ge(token_now_s.sem, token_now_s.at(i - SHARED_TILES))
                pool.nop(nofuse=True)
                for half in range(HALF):
                    pool.indirect_dma_start(xg[:, half, :], None, dram["xn"],
                                            bass.IndirectOffsetOnAxis(token_now[:, half:half + 1], 0)).then_inc(gathered.sem, 16)

            pool.iota(route["ids"][:, :], [[P, T // P]], base=0, channel_multiplier=1).then_inc(made.sem, 1)
            pool.iota(steps_i[:, :], [[ETOK, MOST_TILES]], base=0, channel_multiplier=0).then_inc(made.sem, 1)
            pool.memset(zeros_i[:, :], 0).then_inc(made.sem, 1)
            pool.memset(ones8[:, :], 1.0).then_inc(made.sem, 1)
            pool.wait_ge(made.sem, made.at(0))
            pool.wait_ge(zeroed.sem, zeroed.at(0))
            pool.wait_ge(slots.sem, slots.at(0))
            for t in range(T // P):
                for k in range(2):
                    pool.indirect_dma_start(route["table"], bass.IndirectOffsetOnAxis(pos[:, t, k:k + 1], 0),
                                            route["ids"][:, t:t + 1], None).then_inc(scattered.sem, 16)
            gather(SHARED_TILES)
            end = pool.value_load(bounds[0:1, E:E + 1], min_val=MIN_TILES, max_val=ROUTED_TILES)
            with pool.Fori(0, end) as r:
                gather(r + (SHARED_TILES + 1))

        @block.scalar
        def _(act):
            def split(e, u, first):
                act.wait_ge(e_loaded.sem, e_loaded.at(e))
                act.wait_ge(y_psum.sem, y_psum.at(first, 0))
                act.activation(w13_hi[:, u, :, :], w13_32[:, :, :], ACT.Copy).then_inc(e_hi.sem, 1)
                act.activation(w2_hi[:, u, 0:2, :], w2_32[:, 0:2, :], ACT.Copy).then_inc(e_hi.sem, 1)
                act.activation(w2_hi[0:HT[2][1], u, 2, :], w2_32[0:HT[2][1], 2, :], ACT.Copy).then_inc(e_hi.sem, 1)

            def x_part(i):
                act.wait_ge(gT_psum.sem, gT_psum.at(i))
                act.wait_ge(gu_psum.sem, gu_psum.at(i, 0))
                act.activation(xT_hi[:, :, :], bank[3][:, :].rearrange("p (c t) -> p c t", c=DC), ACT.Copy).then_inc(gT_hi_s.sem, 1)

            def bias1(i, u, m):
                M = HT[m][1]
                act.wait_ge(gu_psum.sem, gu_psum.at(i, m + 1))
                act.activation(a1[0:M, m, :], bank[m][0:M, 0:ETOK], ACT.Identity, bias=b13[0:M, u, m:m + 1]).then_inc(a1_s.sem, 1)

            def hidden(i, m):
                M = HT[m][1]
                act.wait_ge(prod_s.sem, prod_s.at(i, m + 1))
                act.wait_ge(y_psum.sem, y_psum.at(i, 0))
                act.activation(h32[0:M, m, :], prod[0:M, m, :], ACT.Silu).then_inc(h32_s.sem, 1)
                act.activation(h_hi[0:M, m, :], prod[0:M, m, :], ACT.Silu).then_inc(h_hi_s.sem, 1)

            def pack_part(i):
                cols = bass.ds((i - 1) * PACK_PART, PACK_PART)
                act.wait_ge(pack_loaded.sem, pack_loaded.at(i - 1))
                act.activation(pack_hi[:, cols], pack32[:, cols], ACT.Copy).then_inc(pack_hi_s.sem, 1)

            def tile(i, u, ahead):
                bias1(i, u, 0)
                bias1(i, u, 1)
                hidden(i, 0)
                bias1(i, u, 2)
                hidden(i, 1)
                hidden(i, 2)
                x_part(i + 1)
                if ahead and not is_int(i, 0) or is_int(i, PACK_PARTS):
                    pack_part(i)

            def prologue():
                x_part(0)
                split(0, 0, 0)

            over_experts(act, prologue, lambda e, u, first: None, tile,
                         lambda e, u, first: split(e + 1, 1 - u, first), lambda: None)

        @block.vector
        def _(dve):
            def split(e, u, first):
                dve.wait_ge(y_psum.sem, y_psum.at(first, 0))
                for n, (lo, a32, hi) in enumerate((
                        (w13_lo[:, u, :, :], w13_32[:, :, :], w13_hi[:, u, :, :]),
                        (w2_lo[:, u, 0:2, :], w2_32[:, 0:2, :], w2_hi[:, u, 0:2, :]),
                        (w2_lo[0:HT[2][1], u, 2, :], w2_32[0:HT[2][1], 2, :], w2_hi[0:HT[2][1], u, 2, :]))):
                    dve.wait_ge(e_hi.sem, e_hi.at(e, n + 1))
                    dve.tensor_tensor(lo, a32, hi, ALU.subtract).then_inc(e_lo.sem, 1)

            def name_tokens(i):
                dve.wait_ge(gathered.sem, gathered.at(i - SHARED_TILES, 0))
                dve.nop(nofuse=True)
                dve.tensor_copy(token_now[:, :],
                                tokens[:, bass.ds((i - SHARED_TILES) * HALF, HALF)]).then_inc(token_now_s.sem, 1)

            def x_part(i):
                dve.wait_ge(gT_hi_s.sem, gT_hi_s.at(i))
                dve.tensor_tensor(xT_lo[:, :, :], bank[3][:, :].rearrange("p (c t) -> p c t", c=DC), xT_hi[:, :, :],
                                  ALU.subtract).then_inc(gT_lo_s.sem, 1)

            def gated(i, u, m):
                M = HT[m][1]
                dve.wait_ge(a1_s.sem, a1_s.at(i, m + 1))
                dve.wait_ge(h_hi_s.sem, h_hi_s.at(i, 0))
                dve.scalar_tensor_tensor(prod[0:M, m, :], bank[m][0:M, ETOK:2 * ETOK], b13[0:M, u, HM + m:HM + m + 1],
                                         a1[0:M, m, :], ALU.add, ALU.mult).then_inc(prod_s.sem, 1)

            def hidden_lo(i, m):
                M = HT[m][1]
                dve.wait_ge(h_hi_s.sem, h_hi_s.at(i, m + 1))
                dve.tensor_tensor(h_lo[0:M, m, :], h32[0:M, m, :], h_hi[0:M, m, :], ALU.subtract).then_inc(h_lo_s.sem, 1)

            def tile(i, u, ahead):
                gated(i, u, 0)
                gated(i, u, 1)
                hidden_lo(i, 0)
                if not ahead:
                    name_tokens(i + AHEAD)
                gated(i, u, 2)
                hidden_lo(i, 1)
                hidden_lo(i, 2)
                x_part(i + 1)
                dve.wait_ge(y_psum.sem, y_psum.at(i))
                dve.wait_ge(y_stored.sem, y_stored.at(i, 0))
                for half in range(HALF):
                    ins = dve.tensor_tensor(y[:, half, :], bank[4 + half][:, 0:D], b2[:, u, :], ALU.add)
                ins.then_inc(y_ready.sem, 1)
                if ahead and not is_int(i, 0) or is_int(i, PACK_PARTS):
                    pack_part(i)

            def pack_part(i):
                cols = bass.ds((i - 1) * PACK_PART, PACK_PART)
                dve.wait_ge(pack_hi_s.sem, pack_hi_s.at(i - 1))
                dve.tensor_tensor(pack_lo[:, cols], pack32[:, cols], pack_hi[:, cols], ALU.subtract).then_inc(pack_lo_s.sem, 1)

            def done(n, ins):
                ins.then_inc(slots.sem, 1)
                dve.wait_ge(slots.sem, n)

            def find_slots():
                dve.wait_ge(made.sem, made.at(0))
                done(1, dve.tensor_copy(steps[:, :], steps_i[:, :]))
                done(2, dve.tensor_tensor(above[:, :, :], route["run"][:, 0, :].unsqueeze(2).to_broadcast([P, E, MOST_TILES]),
                                          steps[:, :].unsqueeze(1).to_broadcast([P, E, MOST_TILES]), ALU.is_gt))
                done(3, dve.tensor_reduce(tiles[:, :], above[:, :, :], AX.X, ALU.add))
                done(4, dve.tensor_scalar(tiles[:, :], tiles[:, :], float(MIN_TILES), None, ALU.max))
                done(5, dve.tensor_tensor_scan(ends[:, :], ones8[:, :], tiles[:, :], 0.0, ALU.mult, ALU.add))
                done(6, dve.tensor_tensor(starts[:, :], ends[:, :], tiles[:, :], ALU.subtract))
                dve.tensor_copy(bounds[:, 0:E], starts[:, :])
                done(7, dve.tensor_copy(bounds[:, E:E + 1], ends[:, E - 1:E]))
                done(8, dve.tensor_scalar(starts[:, :], starts[:, :], float(ETOK), None, ALU.mult))
                done(9, dve.tensor_tensor(base[:, :, :, :].rearrange("p t k e -> p (t k) e"),
                                          route["onehot"][:, :, :, :].rearrange("p t k e -> p (t k) e"),
                                          starts[:, :].unsqueeze(1).to_broadcast([P, 2 * T // P, E]), ALU.mult))
                done(10, dve.tensor_reduce(posf[:, :, :], base[:, :, :, :], AX.X, ALU.add))
                done(11, dve.tensor_tensor(pos[:, :, :], posf[:, :, :], route["rank"][:, :, :], ALU.add))

            def prologue():
                find_slots()
                x_part(0)
                split(0, 0, 0)

            def table():
                n = ROUTED_SLOTS // P
                dve.wait_ge(table_loaded.sem, 16)
                dve.tensor_copy(table_f[:, :], table_rows[:, :]).then_inc(table_f_s.sem, 1)
                dve.wait_ge(table_psum.sem, 1)
                dve.tensor_copy(tokens[:, :], bank[0][:, 0:n]).then_inc(tokens_s.sem, 1)
                dve.wait_ge(tokens_s.sem, 1)

            over_experts(dve, prologue, lambda e, u, first: None, tile,
                         lambda e, u, first: split(e + 1, 1 - u, first), table)

        @block.tensor
        def _(pe):
            def x_transposes(i, shared):
                if shared:
                    pe.wait_ge(x_loaded.sem, x_loaded.at(i))
                else:
                    pe.wait_ge(gathered.sem, gathered.at(i - SHARED_TILES))
                for c in range(DC):
                    for half in range(HALF):
                        mm = pe.transpose(bank[3][:, c * ETOK + half * P:c * ETOK + half * P + P],
                                          xg[:, half, c * P:(c + 1) * P], identf[:, :])
                mm.then_inc(gT_psum.sem, 1)

            def tile(i, u, ahead):
                pe.wait_ge(gT_lo_s.sem, gT_lo_s.at(i))
                for m, (h0, M) in enumerate(HT):
                    pe.wait_ge(prod_s.sem, prod_s.at(i, 0))
                    for side in range(2):
                        cols = slice(side * H0 + h0, side * H0 + h0 + M)
                        mm = three_products(pe, bank[m][0:M, side * ETOK:(side + 1) * ETOK],
                                            lambda c: w13_hi[:, u, c, cols], lambda c: w13_lo[:, u, c, cols],
                                            lambda c: xT_hi[:, c, :], lambda c: xT_lo[:, c, :], range(DC))
                    mm.then_inc(gu_psum.sem, 1)
                x_transposes(i + 1, ahead or is_int(i, SHARED_TILES - AHEAD))
                pe.wait_ge(y_ready.sem, y_ready.at(i, 0))
                for m, (_, M) in enumerate(HT):
                    pe.wait_ge(h_lo_s.sem, h_lo_s.at(i, m + 1))
                    for half in range(HALF):
                        tok = slice(half * P, (half + 1) * P)
                        mm = three_products(pe, bank[4 + half][:, 0:D], lambda m: h_hi[0:M, m, tok], lambda m: h_lo[0:M, m, tok],
                                            lambda m: w2_hi[0:M, u, m, :], lambda m: w2_lo[0:M, u, m, :], (m,),
                                            first=m == 0, last=m == HM - 1)
                mm.then_inc(y_psum.sem, 1)

            def new_expert(e, u, first):
                pe.wait_ge(e_lo.sem, e_lo.at(e))
                pe.nop(nofuse=True)

            def table():
                n = ROUTED_SLOTS // P
                pe.wait_ge(table_f_s.sem, 1)
                pe.wait_ge(prod_s.sem, prod_s.at(SHARED_TILES - AHEAD - 1))
                pe.transpose(bank[0][:, 0:n], table_f[:, :], identf[0:n, 0:n]).then_inc(table_psum.sem, 1)
                pe.wait_ge(tokens_s.sem, 1)

            over_experts(pe, lambda: x_transposes(0, True), new_expert, tile, lambda e, u, first: None, table)


PACK = {}
_at = 0
for _name, _shape in (("wz", (DC, D)), ("wh", (DC, D)), ("fc1", (DC, LAT)), ("gate", (DC, E)), ("up", (DC, UP)),
                      ("w1", (E, INTER)), ("w2", (E, LAT)), ("wg", (DC, D)), ("down", (UP // P, D)), ("fc2", (1, D))):
    PACK[_name] = (_at, _shape)
    _at += _shape[0] * _shape[1]
PACK_PARTS = SHARED_TILES - AHEAD
PACK_PART = -(-_at // PACK_PARTS)
PACKED = PACK_PARTS * PACK_PART
BZ, BH, BG = 0, DC, 2 * DC


def layer1_phase(nc, w, dram, consts, route, packed, out):
    w_hi, w_lo = packed[1:]
    with ExitStack() as ctx:
        def sb(name, shape, dt=F32):
            return ctx.enter_context(nc.sbuf_tensor(name, shape, dt))

        def sig(name, per):
            return Signal(nc, ctx, name, per)

        identf, iota8 = consts["identf"], consts["iota8"]

        def part(t, name, row, cols):
            at, (_, n) = PACK[name]
            return t[:, at + row * n + cols.start:at + row * n + cols.stop]

        bias = sb("l1_bias", [P, 3 * DC])
        neg_bz = sb("neg_bz", [P, DC])
        corr = sb("corr", [P, E])
        minus_half = sb("l1_minus_half", [P, TT])
        xin = sb("xin", [P, TT, D])
        ysh = sb("ysh", [P, TT, D])
        rows_k = sb("rows_k", [P, TT, 2, D])
        slot = sb("slot", [P, TT, 2], I32)
        wk = sb("wk", [P, TT, 2])
        x2 = sb("x2", [P, 2, TT, D])
        stats = sb("l1_stats", [P, TT, 6])
        mv = sb("l1_mv", [P, TT, 2])
        var_eps = sb("l1_var_eps", [P, TT])
        rstd = sb("l1_rstd", [P, TT])
        xn = sb("l1_xn", [P, TT, D])
        xT_hi, xT_lo = (sb(f"l1_xT_{k}", [P, DC, S], F16) for k in ("hi", "lo"))
        zs = sb("zs", [P, DC, S])
        keep = sb("keep", [P, DC, S])
        inject = sb("inject", [P, DC, S])
        hT = sb("hT", [P, DC, S])
        hT_hi, hT_lo = (sb(f"hT_{k}", [P, DC, S], F16) for k in ("hi", "lo"))
        gs = sb("gs", [P, DC, S])
        gh = sb("gh", [P, DC, S])
        lat_hi, lat_lo = (sb(f"lat_{k}", [P, S], F16) for k in ("hi", "lo"))
        sc = sb("l1_sc", [P, TT, E])
        sfc = sb("sfc", [P, TT, E])
        pairs = sb("pairs", [P, TT * 2, 6])
        gscore = sb("gscore", [P, TT, 2])
        gmask = sb("gmask", [P, TT, 2])
        top = sb("l1_top", [P, TT, 8])
        topi = sb("l1_topi", [P, TT, 8], U32)
        onehot = sb("l1_onehot", [P, 2, TT, E])
        chosen = sb("chosen", [P, TT, E])
        total = sb("total", [P, TT])
        weight = sb("weight", [P, TT, E])
        wT = sb("wT", [E, S])
        w_bc = sb("w_bc", [P, E, S])
        r = sb("r", [P, 3, S])
        rw = sb("rw", [P, 3, S])
        sq = sb("sq", [P, 3, S])
        up_hi, up_lo = (sb(f"up_{k}", [P, UP // P, S], F16) for k in ("hi", "lo"))
        he_hi, he_lo = (sb(f"he_{k}", [P, HE, S], F16) for k in ("hi", "lo"))
        comb_hi, comb_lo = (sb(f"comb_{k}", [P, S], F16) for k in ("hi", "lo"))
        y = sb("l1_y", [P, TT, D])
        bank = [ctx.enter_context(nc.psum_tensor(f"ybank{i}", [P, 512], F32)) for i in range(8)]
        OUT_BANK = (3, 4, 5, 7)
        NU = UP // P
        NR = NU + E

        loaded = sig("l1_loaded", 16 * 3)
        half_filled = sig("half_filled", 1)
        neg_bz_s = sig("neg_bz_s", 1)
        xin_loaded = sig("xin_loaded", 32)
        slot_s = sig("slot_s", 2)
        gathered = sig("rows_gathered", 16 * TT * 2)
        x2_base = sig("x2_base", 1)
        x2_sum = sig("x2_sum", 2)
        dve_ln = sig("l1_dve_ln", 2)
        rstd_s = sig("l1_rstd_s", 2)
        xn_ready = sig("l1_xn_ready", 1)
        xT_psum = sig("l1_xT_psum", DC)
        xT_hi_s = sig("l1_xT_hi_s", DC)
        xT_lo_s = sig("l1_xT_lo_s", DC)
        zh_psum = sig("zh_psum", 2 * DC)
        lg_psum = sig("l1_lg_psum", 1)
        lat_psum = sig("lat_psum", 1)
        sc_s = sig("sc_s", 1)
        zs_s = sig("zs_s", DC)
        keep_s = sig("keep_s", DC)
        lat_hi_s = sig("lat_hi_s", 1)
        lat_lo_s = sig("lat_lo_s", 1)
        inject_s = sig("inject_s", DC)
        hT_s = sig("hT_s", DC)
        hT_hi_s = sig("hT_hi_s", DC)
        hT_lo_s = sig("hT_lo_s", DC)
        rt = sig("l1_rt", 15)
        wT_psum = sig("wT_psum", 1)
        wT_s = sig("wT_s", 1)
        wT_stored = sig("wT_stored", 16)
        w_bc_loaded = sig("w_bc_loaded", 16)
        u_psum = sig("u_psum", NR)
        r_s = sig("r_s", NR)
        rw_s = sig("rw_s", E)
        sq_s = sig("sq_s", NR)
        hid_hi = sig("hid_hi", NR)
        hid_lo = sig("hid_lo", NR)
        comb_psum = sig("comb_psum", E)
        comb_hi_s = sig("comb_hi_s", 1)
        comb_lo_s = sig("comb_lo_s", 1)
        g_psum = sig("g_psum", DC)
        gs_s = sig("gs_s", DC)
        gh_s = sig("gh_s", DC)
        out_psum = sig("out_psum", TT)
        y_ready = sig("l1_y_ready", TT)
        y_stored = sig("l1_y_stored", 16)

        def rows(t, b):
            return t[bass.ds(b * S, S), :].rearrange("(t p) d -> p t d", p=P)

        def pipeline(eng, front, step):
            front(0, 0)
            step(0, 0, True)
            with eng.Fori(0, NB // 2 - 1) as i:
                for u in (1, 0):
                    step(2 * i + 2 - u, u, True)
            step(NB - 1, 1, False)

        def hidden_bank(n):
            return bank[n % 3]

        block = ctx.enter_context(nc.Block())

        @block.sync
        def _(sp):
            sp.dma_start(bias[:, :], w["bias"]).then_inc(loaded.sem, 16)
            sp.dma_start(corr[:, :], w["corr"].partition_broadcast(P)).then_inc(loaded.sem, 16)
            sp.dma_start(neg_bz[:, :], w["bias"][:, BZ:BZ + DC]).then_inc(loaded.sem, 16)

            def front(b, u):
                sp.wait_ge(x2_base.sem, x2_base.at(b, 0))
                sp.dma_start(xin[:, :, :], rows(dram["x1"], b)).then_inc(xin_loaded.sem, 16)
                sp.dma_start(ysh[:, :, :], rows(dram["y"], b)).then_inc(xin_loaded.sem, 16)

            def step(b, u, more):
                if more:
                    front(b + 1, 1 - u)
                sp.wait_ge(wT_s.sem, wT_s.at(b))
                sp.dma_start(dram["wT"], wT[:, :]).then_inc(wT_stored.sem, 16)
                sp.wait_ge(wT_stored.sem, wT_stored.at(b))
                sp.nop(nofuse=True)
                sp.wait_ge(rw_s.sem, rw_s.at(b, 0))
                sp.dma_start(w_bc[:, :, :], dram["wT"].partition_broadcast(P)).then_inc(w_bc_loaded.sem, 16)
                sp.wait_ge(y_ready.sem, y_ready.at(b))
                sp.dma_start(rows(out, b), y[:, :, :]).then_inc(y_stored.sem, 16)

            pipeline(sp, front, step)
            sp.wait_ge(y_stored.sem, y_stored.at(NB - 1))

        @block.gpsimd
        def _(pool):
            pool.memset(minus_half[:, :], -0.5).then_inc(half_filled.sem, 1)
            pool.wait_ge(half_filled.sem, 1)

            def front(b, u):
                pool.wait_ge(x2_sum.sem, x2_sum.at(b, 0))
                pool.wait_ge(slot_s.sem, slot_s.at(b))
                pool.nop(nofuse=True)
                for t in range(TT):
                    for k in range(2):
                        pool.indirect_dma_start(rows_k[:, t, k, :], None, dram["y"],
                                                bass.IndirectOffsetOnAxis(slot[:, t, k:k + 1], 0)).then_inc(gathered.sem, 16)
                pool.wait_ge(xin_loaded.sem, xin_loaded.at(b))
                pool.wait_ge(y_ready.sem, y_ready.at(b - 1, 0))
                pool.tensor_tensor(x2[:, u, :, :], xin[:, :, :], ysh[:, :, :], ALU.add).then_inc(x2_base.sem, 1)
                pool.wait_ge(dve_ln.sem, dve_ln.at(b))
                pool.tensor_tensor(var_eps[:, :], mv[:, :, 1], consts["eps_col"][:, 0:TT], ALU.add).then_inc(rstd_s.sem, 1)
                pool.wait_ge(rstd_s.sem, rstd_s.at(b, 1))
                pool.tensor_tensor(rstd[:, :], var_eps[:, :], minus_half[:, :], ALU.pow).then_inc(rstd_s.sem, 1)

            def step(b, u, more):
                if more:
                    front(b + 1, 1 - u)
                pool.wait_ge(w_bc_loaded.sem, w_bc_loaded.at(b))
                for e in range(E):
                    n = NU + e
                    pool.wait_ge(r_s.sem, r_s.at(b, n + 1))
                    pool.wait_ge(sq_s.sem, sq_s.at(b, n - 2))
                    pool.tensor_tensor(rw[:, n % 3, :], r[:, n % 3, :], w_bc[:, e, :], ALU.mult).then_inc(rw_s.sem, 1)

            pipeline(pool, front, step)

        @block.scalar
        def _(act):
            act.wait_ge(loaded.sem, loaded.at(0))
            act.wait_ge(neg_bz_s.sem, 1)

            def front(b, u):
                for c in range(DC):
                    act.wait_ge(xT_psum.sem, xT_psum.at(b, c + 1))
                    act.wait_ge(u_psum.sem, u_psum.at(b - 1, NU))
                    act.activation(xT_hi[:, c, :], bank[c][:, :], ACT.Copy).then_inc(xT_hi_s.sem, 1)

            def relu(b, n):
                act.wait_ge(u_psum.sem, u_psum.at(b, n + 1))
                if n >= 3:
                    act.wait_ge(sq_s.sem, sq_s.at(b, n - 2))
                act.activation(r[:, n % 3, :], hidden_bank(n)[:, :], ACT.Relu).then_inc(r_s.sem, 1)

            def hidden_hi(b, n):
                act.wait_ge(sq_s.sem, sq_s.at(b, n + 1))
                if n < NU:
                    act.wait_ge(out_psum.sem, out_psum.at(b, 0))
                    dst = up_hi[:, n, :]
                else:
                    if n - NU >= HE:
                        act.wait_ge(comb_psum.sem, comb_psum.at(b, n - NU - HE + 1))
                    dst = he_hi[:, (n - NU) % HE, :]
                act.activation(dst, sq[:, n % 3, :], ACT.Copy).then_inc(hid_hi.sem, 1)

            def step(b, u, more):
                for c in range(DC):
                    act.wait_ge(zh_psum.sem, zh_psum.at(b, c + 1))
                    act.activation(zs[:, c, :], bank[2 + c][:, :], ACT.Sigmoid, bias=bias[:, BZ + c:BZ + c + 1]).then_inc(zs_s.sem, 1)
                    act.activation(keep[:, c, :], bank[2 + c][:, :], ACT.Sigmoid, bias=neg_bz[:, c:c + 1],
                                   scale=-1.0).then_inc(keep_s.sem, 1)
                act.wait_ge(lg_psum.sem, lg_psum.at(b))
                act.activation(sc[:, :, :], bank[7][:, 0:TT * E].rearrange("p (t e) -> p t e", e=E),
                               ACT.Sigmoid).then_inc(sc_s.sem, 1)
                act.wait_ge(lat_psum.sem, lat_psum.at(b))
                act.activation(lat_hi[:, :], bank[6][:, :], ACT.Copy).then_inc(lat_hi_s.sem, 1)
                for n in range(NU + 2):
                    if n < NU:
                        relu(b, n)
                    if n >= 2:
                        hidden_hi(b, n - 2)
                for c in range(DC):
                    act.wait_ge(hT_s.sem, hT_s.at(b, c + 1))
                    act.activation(hT_hi[:, c, :], hT[:, c, :], ACT.Copy).then_inc(hT_hi_s.sem, 1)
                for c in range(DC):
                    act.wait_ge(g_psum.sem, g_psum.at(b, c + 1))
                    act.activation(gs[:, c, :], bank[c][:, :], ACT.Sigmoid, bias=bias[:, BG + c:BG + c + 1]).then_inc(gs_s.sem, 1)
                for n in range(NU, NR + 2):
                    if n < NR:
                        relu(b, n)
                    if n >= NU + 2:
                        hidden_hi(b, n - 2)
                act.wait_ge(comb_psum.sem, comb_psum.at(b))
                act.activation(comb_hi[:, :], bank[6][:, :], ACT.Copy).then_inc(comb_hi_s.sem, 1)
                if more:
                    front(b + 1, 1 - u)

            pipeline(act, front, step)

        @block.vector
        def _(dve):
            dve.wait_ge(loaded.sem, loaded.at(0))
            dve.tensor_scalar(neg_bz[:, :], neg_bz[:, :], -1.0, None, ALU.mult).then_inc(neg_bz_s.sem, 1)

            def slots(b):
                tiles = bass.ds(b * TT, TT)
                dve.wait_ge(gathered.sem, gathered.at(b, 0))
                dve.tensor_scalar(slot[:, :, :], route["pos"][:, tiles, :], float(SHARED_TILES * ETOK), None,
                                  ALU.add).then_inc(slot_s.sem, 1)
                dve.tensor_copy(wk[:, :, :], route["weights"][:, tiles, :]).then_inc(slot_s.sem, 1)

            def front(b, u):
                dve.wait_ge(slot_s.sem, slot_s.at(b))
                dve.wait_ge(x2_base.sem, x2_base.at(b))
                dve.wait_ge(gathered.sem, gathered.at(b))
                for k in range(2):
                    for t in range(TT):
                        ins = dve.scalar_tensor_tensor(x2[:, u, t, :], rows_k[:, t, k, :], wk[:, t, k:k + 1], x2[:, u, t, :],
                                                       ALU.mult, ALU.add)
                    ins.then_inc(x2_sum.sem, 1)
                    dve.wait_ge(x2_sum.sem, x2_sum.at(b, k + 1))
                for t in range(TT):
                    ins = dve.bn_stats(stats[:, t, :], x2[:, u, t, :])
                ins.then_inc(dve_ln.sem, 1)
                dve.wait_ge(dve_ln.sem, dve_ln.at(b, 1))
                dve.nop(nofuse=True)
                for t in range(TT):
                    ins = dve.bn_aggr(mv[:, t, :], stats[:, t, :])
                ins.then_inc(dve_ln.sem, 1)
                dve.wait_ge(dve_ln.sem, dve_ln.at(b))
                dve.wait_ge(rstd_s.sem, rstd_s.at(b))
                for t in range(TT):
                    ins = dve.tensor_scalar(xn[:, t, :], x2[:, u, t, :], mv[:, t, 0:1], rstd[:, t:t + 1],
                                            ALU.subtract, ALU.mult)
                ins.then_inc(xn_ready.sem, 1)

            def x_low(b):
                for c in range(DC):
                    dve.wait_ge(xT_hi_s.sem, xT_hi_s.at(b, c + 1))
                    dve.tensor_tensor(xT_lo[:, c, :], bank[c][:, :], xT_hi[:, c, :], ALU.subtract).then_inc(xT_lo_s.sem, 1)

            def done(b, n, ins):
                ins.then_inc(rt.sem, 1)
                dve.wait_ge(rt.sem, rt.at(b, n))

            def router_groups(b):
                dve.wait_ge(sc_s.sem, sc_s.at(b))
                done(b, 1, dve.tensor_tensor(sfc[:, :, :], sc[:, :, :], corr[:, :].unsqueeze(1).to_broadcast([P, TT, E]), ALU.add))
                g4 = sfc[:, :, :].rearrange("p t (g s) -> p (t g) s", s=E // 2)
                dve.tensor_tensor(pairs[:, :, 0:3], g4[:, :, 0:3], g4[:, :, 1:4], ALU.add)
                dve.tensor_tensor(pairs[:, :, 3:5], g4[:, :, 0:2], g4[:, :, 2:4], ALU.add)
                done(b, 2, dve.tensor_tensor(pairs[:, :, 5:6], g4[:, :, 0:1], g4[:, :, 3:4], ALU.add))
                done(b, 3, dve.tensor_reduce(gscore[:, :, :].rearrange("p t g -> p (t g)"), pairs[:, :, :], AX.X, ALU.max))
                done(b, 4, dve.tensor_tensor(gmask[:, :, 0:1], gscore[:, :, 0:1], gscore[:, :, 1:2], ALU.is_ge))
                done(b, 5, dve.tensor_scalar(gmask[:, :, 1:2], gmask[:, :, 0:1], -1.0, 1.0, ALU.mult, ALU.add))
                done(b, 6, dve.tensor_tensor(g4, g4, gmask[:, :, :].rearrange("p t g -> p (t g)").unsqueeze(2).to_broadcast([P, TT * 2, E // 2]),
                                       ALU.mult))

            def router_choice(b):
                dve.nop(nofuse=True)
                for t in range(TT):
                    ins = dve.max(top[:, t, :], sfc[:, t, :])
                done(b, 7, ins)
                dve.nop(nofuse=True)
                for t in range(TT):
                    ins = dve.max_index(topi[:, t, :], top[:, t, :], sfc[:, t, :])
                done(b, 8, ins)
                for k in range(2):
                    ins = dve.tensor_tensor(onehot[:, k, :, :], iota8[:, :].unsqueeze(1).to_broadcast([P, TT, E]),
                                            topi[:, :, k:k + 1].to_broadcast([P, TT, E]), ALU.is_equal)
                done(b, 9, ins)

            def router_weights(b):
                done(b, 10, dve.tensor_tensor(chosen[:, :, :], onehot[:, 0, :, :], onehot[:, 1, :, :], ALU.add))
                done(b, 11, dve.tensor_tensor(chosen[:, :, :], chosen[:, :, :], sc[:, :, :], ALU.mult))
                done(b, 12, dve.tensor_reduce(total[:, :], chosen[:, :, :], AX.X, ALU.add))
                done(b, 13, dve.tensor_scalar(total[:, :], total[:, :], 1e-20, None, ALU.add))
                done(b, 14, dve.reciprocal(total[:, :], total[:, :]))
                done(b, 15, dve.tensor_tensor(weight[:, :, :], chosen[:, :, :], total[:, :].unsqueeze(2).to_broadcast([P, TT, E]), ALU.mult))

            def square(b, n):
                if n < NU:
                    dve.wait_ge(r_s.sem, r_s.at(b, n + 1))
                    other = r
                else:
                    dve.wait_ge(rw_s.sem, rw_s.at(b, n - NU + 1))
                    other = rw
                if n >= 3:
                    dve.wait_ge(hid_lo.sem, hid_lo.at(b, n - 2))
                dve.tensor_tensor(sq[:, n % 3, :], r[:, n % 3, :], other[:, n % 3, :], ALU.mult).then_inc(sq_s.sem, 1)

            def hidden_low(b, n):
                dve.wait_ge(hid_hi.sem, hid_hi.at(b, n + 1))
                hi, lo = (up_hi[:, n, :], up_lo[:, n, :]) if n < NU else (he_hi[:, (n - NU) % HE, :], he_lo[:, (n - NU) % HE, :])
                dve.tensor_tensor(lo, sq[:, n % 3, :], hi, ALU.subtract).then_inc(hid_lo.sem, 1)

            def step(b, u, more):
                if more:
                    slots(b + 1)
                for c in range(DC):
                    dve.wait_ge(zh_psum.sem, zh_psum.at(b, DC + c + 1))
                    dve.wait_ge(zs_s.sem, zs_s.at(b, c + 1))
                    dve.scalar_tensor_tensor(inject[:, c, :], bank[4 + c][:, :], bias[:, BH + c:BH + c + 1], zs[:, c, :],
                                             ALU.add, ALU.mult).then_inc(inject_s.sem, 1)
                dve.wait_ge(lat_hi_s.sem, lat_hi_s.at(b))
                dve.tensor_tensor(lat_lo[:, :], bank[6][:, :], lat_hi[:, :], ALU.subtract).then_inc(lat_lo_s.sem, 1)
                for n in range(NU + 2):
                    if n == NU + 1:
                        dve.wait_ge(wT_psum.sem, wT_psum.at(b))
                        dve.tensor_copy(wT[:, :], bank[7][0:E, :]).then_inc(wT_s.sem, 1)
                    if n < NU:
                        square(b, n)
                    if n >= 2:
                        hidden_low(b, n - 2)
                    if n == 0:
                        router_groups(b)
                    elif n == 1:
                        router_choice(b)
                    elif n == 2:
                        router_weights(b)
                for c in range(DC):
                    dve.wait_ge(inject_s.sem, inject_s.at(b, c + 1))
                    dve.wait_ge(keep_s.sem, keep_s.at(b, c + 1))
                    dve.tensor_tensor_scan(hT[:, c, :], keep[:, c, :], inject[:, c, :], 0.0, ALU.mult, ALU.add).then_inc(hT_s.sem, 1)
                for c in range(DC):
                    dve.wait_ge(hT_hi_s.sem, hT_hi_s.at(b, c + 1))
                    dve.tensor_tensor(hT_lo[:, c, :], hT[:, c, :], hT_hi[:, c, :], ALU.subtract).then_inc(hT_lo_s.sem, 1)
                if more:
                    front(b + 1, 1 - u)
                for n in range(NU, NR + 2):
                    if n < NR:
                        square(b, n)
                    if n >= NU + 2:
                        hidden_low(b, n - 2)
                    if n in (NU + 2, NU + 3):
                        c = n - NU - 2
                        dve.wait_ge(gs_s.sem, gs_s.at(b, c + 1))
                        dve.tensor_tensor(gh[:, c, :], gs[:, c, :], hT[:, c, :], ALU.mult).then_inc(gh_s.sem, 1)
                dve.wait_ge(comb_hi_s.sem, comb_hi_s.at(b))
                dve.tensor_tensor(comb_lo[:, :], bank[6][:, :], comb_hi[:, :], ALU.subtract).then_inc(comb_lo_s.sem, 1)
                if more:
                    x_low(b + 1)
                dve.wait_ge(y_stored.sem, y_stored.at(b, 0))
                for t in range(TT):
                    dve.wait_ge(out_psum.sem, out_psum.at(b, t + 1))
                    dve.tensor_tensor(y[:, t, :], bank[OUT_BANK[t]][:, 0:D], x2[:, u, t, :], ALU.add).then_inc(y_ready.sem, 1)

            def first(b, u):
                slots(b)
                front(b, u)
                x_low(b)

            pipeline(dve, first, step)

        @block.tensor
        def _(pe):
            whole = slice(0, S)

            def transposes(b):
                pe.wait_ge(xn_ready.sem, xn_ready.at(b))
                for c in range(DC):
                    for t in range(TT):
                        mm = pe.transpose(bank[c][:, t * P:(t + 1) * P], xn[:, t, c * P:(c + 1) * P], identf[:, :])
                    mm.then_inc(xT_psum.sem, 1)

            def from_x(out, name, cols):
                return three_products(pe, out, lambda c: part(w_hi, name, c, cols), lambda c: part(w_lo, name, c, cols),
                                      lambda c: xT_hi[:, c, :], lambda c: xT_lo[:, c, :], range(DC))

            def hidden(b, n):
                if n >= 3:
                    pe.wait_ge(r_s.sem, r_s.at(b, n - 2))
                if n < NU:
                    mm = from_x(hidden_bank(n)[:, :], "up", slice(n * P, (n + 1) * P))
                else:
                    mm = three_products(pe, hidden_bank(n)[:, :], lambda e: part(w_hi, "w1", e, slice(0, INTER)),
                                        lambda e: part(w_lo, "w1", e, slice(0, INTER)),
                                        lambda e: lat_hi[:, :], lambda e: lat_lo[:, :], (n - NU,))
                mm.then_inc(u_psum.sem, 1)

            def combine(b, e):
                pe.wait_ge(hid_lo.sem, hid_lo.at(b, NU + e + 1))
                three_products(pe, bank[6][:, :], lambda e: part(w_hi, "w2", e, slice(0, LAT)),
                               lambda e: part(w_lo, "w2", e, slice(0, LAT)),
                               lambda e: he_hi[:, e % HE, :], lambda e: he_lo[:, e % HE, :], (e,),
                               first=e == 0, last=e == E - 1).then_inc(comb_psum.sem, 1)

            def step(b, u, more):
                pe.wait_ge(xT_lo_s.sem, xT_lo_s.at(b))
                pe.wait_ge(y_ready.sem, y_ready.at(b - 1, 1))
                for c in range(DC):
                    from_x(bank[2 + c][:, :], "wz", slice(c * P, (c + 1) * P)).then_inc(zh_psum.sem, 1)
                pe.wait_ge(y_ready.sem, y_ready.at(b - 1))
                for c in range(DC):
                    from_x(bank[4 + c][:, :], "wh", slice(c * P, (c + 1) * P)).then_inc(zh_psum.sem, 1)
                for t in range(TT):
                    tok = slice(t * P, (t + 1) * P)
                    mm = three_products(pe, bank[7][:, t * E:(t + 1) * E], lambda c: xT_hi[:, c, tok], lambda c: xT_lo[:, c, tok],
                                        lambda c: part(w_hi, "gate", c, slice(0, E)), lambda c: part(w_lo, "gate", c, slice(0, E)),
                                        range(DC))
                mm.then_inc(lg_psum.sem, 1)
                from_x(bank[6][:, :], "fc1", slice(0, LAT)).then_inc(lat_psum.sem, 1)
                pe.wait_ge(keep_s.sem, keep_s.at(b))
                for n in range(NU):
                    hidden(b, n)
                    if n == NU - 1:
                        pe.wait_ge(rt.sem, rt.at(b))
                        for t in range(TT):
                            mm = pe.transpose(bank[7][0:E, t * P:(t + 1) * P], weight[:, t, :], identf[:, :])
                        mm.then_inc(wT_psum.sem, 1)
                pe.wait_ge(hid_lo.sem, hid_lo.at(b, NU))
                pe.wait_ge(wT_s.sem, wT_s.at(b))
                pe.wait_ge(inject_s.sem, inject_s.at(b))
                for t in range(TT):
                    tok = slice(t * P, (t + 1) * P)
                    three_products(pe, bank[OUT_BANK[t]][:, 0:D], lambda n: up_hi[:, n, tok], lambda n: up_lo[:, n, tok],
                                   lambda n: part(w_hi, "down", n, slice(0, D)), lambda n: part(w_lo, "down", n, slice(0, D)),
                                   range(NU), last=False)
                pe.wait_ge(hT_lo_s.sem, hT_lo_s.at(b))
                pe.wait_ge(r_s.sem, r_s.at(b, NU))
                for c in range(DC):
                    three_products(pe, bank[c][:, :], lambda k: part(w_hi, "wg", k, slice(c * P, (c + 1) * P)),
                                   lambda k: part(w_lo, "wg", k, slice(c * P, (c + 1) * P)),
                                   lambda k: hT_hi[:, k, :], lambda k: hT_lo[:, k, :], range(DC)).then_inc(g_psum.sem, 1)
                pe.wait_ge(lat_lo_s.sem, lat_lo_s.at(b))
                for e in range(E + COMBINE_LAG):
                    if e == 1:
                        pe.wait_ge(gs_s.sem, gs_s.at(b))
                    if e < E:
                        hidden(b, NU + e)
                    if e >= COMBINE_LAG:
                        combine(b, e - COMBINE_LAG)
                    if e == E and more:
                        pe.wait_ge(r_s.sem, r_s.at(b))
                        transposes(b + 1)
                pe.wait_ge(gh_s.sem, gh_s.at(b))
                for t in range(TT):
                    for c in range(DC):
                        pe.matmul(bank[OUT_BANK[t]][:, c * P:(c + 1) * P], gh[:, c, t * P:(t + 1) * P], identf[:, :],
                                  start=False, stop=False)
                pe.wait_ge(comb_lo_s.sem, comb_lo_s.at(b))
                for t in range(TT):
                    tok = slice(t * P, (t + 1) * P)
                    three_products(pe, bank[OUT_BANK[t]][:, 0:D], lambda n: comb_hi[:, tok], lambda n: comb_lo[:, tok],
                                   lambda n: part(w_hi, "fc2", 0, slice(0, D)), lambda n: part(w_lo, "fc2", 0, slice(0, D)),
                                   (0,), first=False).then_inc(out_psum.sem, 1)

            pipeline(pe, lambda b, u: transposes(b), step)


_INS = ["x", "wqkv", "gate0", "wout", "bqk", "bv", "bout", "gate_b", "w13", "w2", "b13", "b2", "pack", "bias", "corr"]


def build(nc, ins, out):
    with ExitStack() as ctx:
        def sb(name, shape, dt=F32):
            return ctx.enter_context(nc.sbuf_tensor(name, shape, dt))

        consts = constants(nc, ctx)
        dram = {"x1": nc.dram_tensor("x1_dram", (T, D), F32).ap(),
                "xn": nc.dram_tensor("xn_dram", (T, D), F32).ap(),
                "qk_hi": nc.dram_tensor("qk_hi_dram", (2 * D, S), F16).ap(),
                "qk_lo": nc.dram_tensor("qk_lo_dram", (2 * D, S), F16).ap(),
                "y": nc.dram_tensor("y_dram", (MAX_TILES * ETOK, D), F32).ap(),
                "wT": nc.dram_tensor("wT_dram", (E, S), F32).ap()}
        route = {"weights": sb("route_weights", [P, T // P, 2]), "rank": sb("route_rank", [P, T // P, 2]),
                 "onehot": sb("route_onehot", [P, T // P, 2, E]), "run": sb("route_run", [P, TT + 1, E]),
                 "bounds": sb("bounds", [P, E + 1], I32), "pos": sb("pos", [P, T // P, 2], I32),
                 "tokens": sb("tokens", [P, ROUTED_SLOTS // P], I32), "ids": sb("ids", [P, T // P], I32),
                 "table": nc.dram_tensor("table_dram", (ROUTED_SLOTS, 1), I32).ap()}
        mix_phase(nc, ins["x"], ins, dram, consts, route)
        packed = [sb("pack32", [P, PACKED])] + [sb(f"pack_{k}", [P, PACKED], F16) for k in ("hi", "lo")]
        experts_phase(nc, ins, dram, consts, route, packed)
        layer1_phase(nc, ins, dram, consts, route, packed, out)


def _layout(i):
    import numpy as np

    def rows(a):
        a = np.asarray(a)
        return a.reshape(-1, P, a.shape[-1]).transpose(1, 0, 2).reshape(P, -1)

    wqkv = np.asarray(i["L0_attn_Wqkv"]).reshape(NH, D, 3, HD).transpose(1, 2, 0, 3).reshape(D, 3 * D)
    bqkv = np.asarray(i["L0_attn_bqkv"]).reshape(NH, 3, HD).transpose(1, 0, 2).reshape(3 * D)
    f = {k: np.asarray(i["L0_ffn_" + k]) for k in ("w1", "w3", "w2", "b1", "b3", "b2", "sw1", "sw3", "sw2", "sb1", "sb3", "sb2")}

    def experts(shared, routed):
        return np.concatenate([shared[None], routed, routed[-1:]])

    b13 = np.zeros((NX + 1, P, 2 * len(HT)), f["b1"].dtype)
    for side, b in enumerate((experts(f["sb1"], f["b1"]), experts(f["sb3"], f["b3"]))):
        for m, (h0, n) in enumerate(HT):
            b13[:, :n, side * len(HT) + m] = b[:, h0:h0 + n]
    a = {k: np.asarray(i["L1_attn_" + k]) for k in ("Wz", "bz", "Wh", "bh", "Wg", "bg")}
    g = {k: np.asarray(i["L1_ffn_" + k]) for k in ("gate", "corr_bias", "w1", "w2", "fc1_w", "fc2_w", "up_w", "down_w")}
    pack = {"wz": rows(a["Wz"].transpose(1, 0, 2).reshape(D, D)), "wh": rows(a["Wh"].transpose(1, 0, 2).reshape(D, D)),
            "fc1": rows(g["fc1_w"].T), "gate": rows(g["gate"].T), "up": rows(g["up_w"].T),
            "w1": g["w1"].transpose(2, 0, 1).reshape(LAT, -1), "w2": g["w2"].transpose(2, 0, 1).reshape(INTER, -1),
            "wg": rows(a["Wg"]), "down": rows(g["down_w"].T), "fc2": rows(g["fc2_w"].T)}
    return {
        "x": np.asarray(i["L0_attn_x"]).reshape(T, D), "wqkv": wqkv, "gate0": np.asarray(i["L0_ffn_gate_w"]).T,
        "wout": np.asarray(i["L0_attn_Wout"]), "bqk": bqkv[:2 * D].reshape(4, P).T, "bv": bqkv[2 * D:],
        "bout": np.asarray(i["L0_attn_bout"]), "gate_b": np.asarray(i["L0_ffn_gate_b"]),
        "w13": np.concatenate([experts(f["sw1"], f["w1"]), experts(f["sw3"], f["w3"])], 2),
        "w2": experts(f["sw2"], f["w2"]), "b13": b13, "b2": experts(f["sb2"], f["b2"])[:, None, :],
        "pack": np.concatenate([pack[n] for n in PACK] + [np.zeros((P, PACKED - sum(pack[n].shape[1] for n in PACK)), np.float32)], 1),
        "bias": np.concatenate([a["bz"].reshape(DC, P).T, a["bh"].reshape(DC, P).T, a["bg"].reshape(DC, P).T], 1),
        "corr": g["corr_bias"],
    }


def kernel(**inputs):
    import numpy as np
    import concourse.bacc as bacc
    from concourse.bass_utils import run_bass_kernel_spmd

    laid = _layout(inputs)
    nc = bacc.Bacc("TRN2", target_bir_lowering=False, num_devices=1)
    arrays, ins = {}, {}
    for name in _INS:
        a = np.ascontiguousarray(laid[name])
        arrays[f"in_{name}"] = a
        ins[name] = nc.dram_tensor(f"in_{name}", a.shape, mybir.dt.from_np(a.dtype), kind="ExternalInput").ap()
    out = nc.dram_tensor("out_0", (T, D), F32, kind="ExternalOutput").ap()
    build(nc, ins, out)
    r = run_bass_kernel_spmd(nc, [arrays], core_ids=[0])
    return r.results[0]["out_0"].reshape(NB, S, D)
```
